# Optimizing a Trainium2 kernel written in Bass

```python
import numpy as np
import jax
import jax.numpy as jnp

def _softmax(x, axis=-1):
    return jax.nn.softmax(x, axis=axis)

def _gelu(x):
    return jax.nn.gelu(x, approximate=True)

def _silu(x):
    return jax.nn.silu(x)

def _sigmoid(x):
    return jax.nn.sigmoid(x)

def _layernorm(x, axis=-1, eps=1e-05):
    m = jnp.mean(x, axis=axis, keepdims=True)
    v = jnp.var(x, axis=axis, keepdims=True)
    return (x - m) / jnp.sqrt(v + eps)

def _scatter_add(tgt, idx, src, axis=0):
    return tgt.at[idx].add(src)

def _segment_sum(src, seg, n):
    return jax.ops.segment_sum(src, seg, n)
kernel_name = 'mk_prb_d2_jaxref_r8_b333e6'

def setup_inputs(seed: int=0):
    np.random.seed(seed)
    _w = jnp.asarray

    def _L0_attn_setup():
        import jax, jax.numpy as jnp
        import numpy as np
        BATCH, SEQ, D_MODEL, N_HEADS, D_HEAD = (2, 256, 256, 16, 128)
        ATTN_SCALE = np.sqrt(D_HEAD).astype(np.float32)
        IGNORE = jnp.float32(-100000.0)
        key = jax.random.key(seed)
        ks = jax.random.split(key, 5)
        init = 1.0 / np.sqrt(D_MODEL)
        return {'x': jax.random.normal(ks[0], (BATCH, SEQ, D_MODEL), jnp.float32), 'W_Q': jax.random.normal(ks[1], (N_HEADS, D_MODEL, D_HEAD), jnp.float32) * init, 'W_K': jax.random.normal(ks[2], (N_HEADS, D_MODEL, D_HEAD), jnp.float32) * init, 'W_V': jax.random.normal(ks[3], (N_HEADS, D_MODEL, D_HEAD), jnp.float32) * init, 'W_O': jax.random.normal(ks[4], (N_HEADS, D_HEAD, D_MODEL), jnp.float32) * init, 'b_Q': jnp.zeros((N_HEADS, D_HEAD), jnp.float32), 'b_K': jnp.zeros((N_HEADS, D_HEAD), jnp.float32), 'b_V': jnp.zeros((N_HEADS, D_HEAD), jnp.float32), 'b_O': jnp.zeros((D_MODEL,), jnp.float32)}
    _L0_attn_in = _L0_attn_setup()

    def _L0_ffn_setup():
        import jax, jax.numpy as jnp
        import numpy as np
        B, S, EMB = (4, 256, 256)
        LAT, HID = (64, 128)
        E, K = (16, 8)
        SCALE = 2.5

        def _w(key, shape, fan_in):
            return jax.random.normal(key, shape, jnp.float32) * fan_in ** (-0.5)

        def _sqrelu(x):
            return jnp.square(jax.nn.relu(x))
        key = jax.random.key(seed)
        ks = jax.random.split(key, 11)
        return {'x': jax.random.normal(ks[0], (B, S, EMB), jnp.float32), 'sw1': _w(ks[1], (HID, EMB), EMB), 'swg': _w(ks[2], (HID, EMB), EMB), 'sw2': _w(ks[3], (EMB, HID), HID), 'rw1': _w(ks[4], (E, HID, LAT), LAT), 'rwg': _w(ks[5], (E, HID, LAT), LAT), 'rw2': _w(ks[6], (E, LAT, HID), HID), 'Wg': _w(ks[7], (E, EMB), EMB), 'Wdown': _w(ks[8], (LAT, EMB), EMB), 'Wup': _w(ks[9], (EMB, LAT), LAT), 'biases': jnp.zeros((E,), jnp.float32)}
    _L0_ffn_in = _L0_ffn_setup()

    def _L1_attn_setup():
        import jax, jax.numpy as jnp
        import numpy as np
        HIDDEN = 256
        N_HEADS = 16
        HEAD_DIM = HIDDEN // N_HEADS

        def rotate_half(x):
            x1, x2 = jnp.split(x, 2, axis=-1)
            return jnp.concatenate([-x2, x1], axis=-1)
        key = jax.random.key(seed)
        k0, k1, k2, k3, k4 = jax.random.split(key, 5)
        B, S = (1, 256)
        scale = 1.0 / np.sqrt(HIDDEN)
        return {'hidden_states': jax.random.normal(k0, (B, S, HIDDEN), dtype=jnp.float32), 'Wq': jax.random.normal(k1, (HIDDEN, HIDDEN), dtype=jnp.float32) * scale, 'Wk': jax.random.normal(k2, (HIDDEN, HIDDEN), dtype=jnp.float32) * scale, 'Wv': jax.random.normal(k3, (HIDDEN, HIDDEN), dtype=jnp.float32) * scale, 'Wo': jax.random.normal(k4, (HIDDEN, HIDDEN), dtype=jnp.float32) * scale, 'gate': jnp.zeros((1, N_HEADS, 1, 1), dtype=jnp.float32)}
    _L1_attn_in = _L1_attn_setup()

    def _L1_ffn_setup():
        import jax, jax.numpy as jnp
        import numpy as np
        B, T, D = (1, 128, 256)
        F_DIM = 176
        E = 8
        TOPK = 2
        key = jax.random.key(seed)
        ks = jax.random.split(key, 5)
        x = jax.random.normal(ks[0], (B, T, D), dtype=jnp.float32)
        gate_w = jax.random.normal(ks[1], (E, D), dtype=jnp.float32) * 0.02
        gate_proj = jax.random.normal(ks[2], (E, F_DIM, D), dtype=jnp.float32) * 0.02
        up_proj = jax.random.normal(ks[3], (E, F_DIM, D), dtype=jnp.float32) * 0.02
        down_proj = jax.random.normal(ks[4], (E, D, F_DIM), dtype=jnp.float32) * 0.02
        return {'x': x, 'gate_w': gate_w, 'gate_proj': gate_proj, 'up_proj': up_proj, 'down_proj': down_proj}
    _L1_ffn_in = _L1_ffn_setup()
    _d = {'L0_attn_x': _L0_attn_in['x'], 'L0_attn_W_Q': _L0_attn_in['W_Q'], 'L0_attn_W_K': _L0_attn_in['W_K'], 'L0_attn_W_V': _L0_attn_in['W_V'], 'L0_attn_W_O': _L0_attn_in['W_O'], 'L0_attn_b_Q': _L0_attn_in['b_Q'], 'L0_attn_b_K': _L0_attn_in['b_K'], 'L0_attn_b_V': _L0_attn_in['b_V'], 'L0_attn_b_O': _L0_attn_in['b_O'], 'L0_ffn_sw1': _L0_ffn_in['sw1'], 'L0_ffn_swg': _L0_ffn_in['swg'], 'L0_ffn_sw2': _L0_ffn_in['sw2'], 'L0_ffn_rw1': _L0_ffn_in['rw1'], 'L0_ffn_rwg': _L0_ffn_in['rwg'], 'L0_ffn_rw2': _L0_ffn_in['rw2'], 'L0_ffn_Wg': _L0_ffn_in['Wg'], 'L0_ffn_Wdown': _L0_ffn_in['Wdown'], 'L0_ffn_Wup': _L0_ffn_in['Wup'], 'L0_ffn_biases': _L0_ffn_in['biases'], 'L1_attn_Wq': _L1_attn_in['Wq'], 'L1_attn_Wk': _L1_attn_in['Wk'], 'L1_attn_Wv': _L1_attn_in['Wv'], 'L1_attn_Wo': _L1_attn_in['Wo'], 'L1_attn_gate': _L1_attn_in['gate'], 'L1_ffn_gate_w': _L1_ffn_in['gate_w'], 'L1_ffn_gate_proj': _L1_ffn_in['gate_proj'], 'L1_ffn_up_proj': _L1_ffn_in['up_proj'], 'L1_ffn_down_proj': _L1_ffn_in['down_proj']}
    _x0 = _d['L0_attn_x']
    _d['L0_attn_x'] = jax.random.normal(jax.random.fold_in(jax.random.key(seed), 1), (2, 512, 256), dtype=_x0.dtype)
    del _x0
    return _d

def reference(L0_attn_x, L0_attn_W_Q, L0_attn_W_K, L0_attn_W_V, L0_attn_W_O, L0_attn_b_Q, L0_attn_b_K, L0_attn_b_V, L0_attn_b_O, L0_ffn_sw1, L0_ffn_swg, L0_ffn_sw2, L0_ffn_rw1, L0_ffn_rwg, L0_ffn_rw2, L0_ffn_Wg, L0_ffn_Wdown, L0_ffn_Wup, L0_ffn_biases, L1_attn_Wq, L1_attn_Wk, L1_attn_Wv, L1_attn_Wo, L1_attn_gate, L1_ffn_gate_w, L1_ffn_gate_proj, L1_ffn_up_proj, L1_ffn_down_proj):

    def _L0_attn_ref(x, W_Q, W_K, W_V, W_O, b_Q, b_K, b_V, b_O):
        import jax, jax.numpy as jnp
        import numpy as np
        BATCH, SEQ, D_MODEL, N_HEADS, D_HEAD = (2, 256, 256, 16, 128)
        ATTN_SCALE = np.sqrt(D_HEAD).astype(np.float32)
        IGNORE = jnp.float32(-100000.0)
        q = jnp.einsum('bpd,hde->bphe', x, W_Q) + b_Q
        k = jnp.einsum('bpd,hde->bphe', x, W_K) + b_K
        v = jnp.einsum('bpd,hde->bphe', x, W_V) + b_V
        scores = jnp.einsum('bqhe,bkhe->bhqk', q, k) / ATTN_SCALE
        S = x.shape[1]
        causal = jnp.tril(jnp.ones((S, S), bool))
        scores = jnp.where(causal, scores, IGNORE)
        attn = jax.nn.softmax(scores, axis=-1)
        z = jnp.einsum('bkhe,bhqk->bqhe', v, attn)
        out = jnp.einsum('bqhe,hed->bqd', z, W_O) + b_O
        return out

    def _L0_ffn_ref(x, sw1, swg, sw2, rw1, rwg, rw2, Wg, Wdown, Wup, biases):
        import jax, jax.numpy as jnp
        import numpy as np
        B, S, EMB = (4, 256, 256)
        LAT, HID = (64, 128)
        E, K = (16, 8)
        SCALE = 2.5

        def _w(key, shape, fan_in):
            return jax.random.normal(key, shape, jnp.float32) * fan_in ** (-0.5)

        def _sqrelu(x):
            return jnp.square(jax.nn.relu(x))
        b, s, d = x.shape
        x2 = x.reshape(-1, d)
        shared = x2 @ sw1.T * _sqrelu(x2 @ swg.T) @ sw2.T
        xl = x2 @ Wdown.T
        probas = jax.nn.sigmoid(x2 @ Wg.T)
        _, idx = jax.lax.top_k(probas + biases, K)
        p = jnp.take_along_axis(probas, idx, axis=-1)
        p = p / p.sum(-1, keepdims=True) * SCALE
        T = x2.shape[0]
        w_dense = jnp.zeros((T, E), x2.dtype).at[jnp.arange(T)[:, None], idx].add(p)
        acc = jnp.zeros_like(xl)
        for e in range(E):
            ye = xl @ rw1[e].T * _sqrelu(xl @ rwg[e].T) @ rw2[e].T
            acc = acc + w_dense[:, e:e + 1] * ye
        out = shared + acc @ Wup.T
        return out.reshape(b, s, d)

    def _L1_attn_ref(hidden_states, Wq, Wk, Wv, Wo, gate):
        import jax, jax.numpy as jnp
        import numpy as np
        HIDDEN = 256
        N_HEADS = 16
        HEAD_DIM = HIDDEN // N_HEADS

        def rotate_half(x):
            x1, x2 = jnp.split(x, 2, axis=-1)
            return jnp.concatenate([-x2, x1], axis=-1)
        B, S, H = hidden_states.shape
        q = hidden_states @ Wq.T
        k = hidden_states @ Wk.T
        v = hidden_states @ Wv.T
        inv_freq = 1.0 / 10000.0 ** (jnp.arange(0, H, 2, dtype=jnp.float32) / H)
        t = jnp.arange(S, dtype=jnp.float32)
        freqs = t[:, None] * inv_freq[None, :]
        emb = jnp.concatenate([freqs, freqs], axis=-1)[None]
        cos, sin = (jnp.cos(emb), jnp.sin(emb))
        q = q * cos + rotate_half(q) * sin
        k = k * cos + rotate_half(k) * sin

        def split_heads(x):
            return x.reshape(B, S, N_HEADS, HEAD_DIM).transpose(0, 2, 1, 3)
        q, k, v = (split_heads(q), split_heads(k), split_heads(v))
        k_feat = jax.nn.elu(k) + 1.0
        memory = jnp.einsum('bhsd,bhse->bhde', k_feat, v)
        norm_term = k_feat.sum(axis=2)
        q_feat = jax.nn.elu(q) + 1.0
        mem_out = jnp.einsum('bhsd,bhde->bhse', q_feat, memory)
        denom = jnp.einsum('bhsd,bhd->bhs', q_feat, norm_term)[..., None]
        mem_out = mem_out / denom
        scale = 1.0 / jnp.sqrt(jnp.float32(HEAD_DIM))
        scores = jnp.einsum('bhqd,bhkd->bhqk', q, k) * scale
        attn = jnp.einsum('bhqk,bhkd->bhqd', jax.nn.softmax(scores, axis=-1), v)
        g = jax.nn.sigmoid(gate)
        combined = g * mem_out + (1.0 - g) * attn
        combined = combined.transpose(0, 2, 1, 3).reshape(B, S, H)
        return combined @ Wo.T

    def _L1_ffn_ref(x, gate_w, gate_proj, up_proj, down_proj):
        import jax, jax.numpy as jnp
        import numpy as np
        B, T, D = (1, 128, 256)
        F_DIM = 176
        E = 8
        TOPK = 2
        b, t, d = x.shape
        x_flat = x.reshape(-1, d)
        n = x_flat.shape[0]
        router_logits = x_flat @ gate_w.T
        top_w, sel = jax.lax.top_k(router_logits, TOPK)
        top_w = jax.nn.softmax(top_w, axis=-1)
        tok_ids = jnp.arange(n)[:, None]
        tw = jnp.zeros((n, E), dtype=x.dtype).at[tok_ids, sel].add(top_w)
        g = jnp.einsum('nd,efd->enf', x_flat, gate_proj)
        u = jnp.einsum('nd,efd->enf', x_flat, up_proj)
        h = jax.nn.silu(g) * u
        eo = jnp.einsum('enf,edf->end', h, down_proj)
        out = jnp.einsum('end,ne->nd', eo, tw)
        return out.reshape(b, t, d)
    x = L0_attn_x
    xn = _layernorm(x, axis=-1)
    x = x + _L0_attn_ref(xn, L0_attn_W_Q, L0_attn_W_K, L0_attn_W_V, L0_attn_W_O, L0_attn_b_Q, L0_attn_b_K, L0_attn_b_V, L0_attn_b_O) + _L0_ffn_ref(xn, L0_ffn_sw1, L0_ffn_swg, L0_ffn_sw2, L0_ffn_rw1, L0_ffn_rwg, L0_ffn_rw2, L0_ffn_Wg, L0_ffn_Wdown, L0_ffn_Wup, L0_ffn_biases)
    xn = _layernorm(x, axis=-1)
    x = x + _L1_attn_ref(xn, L1_attn_Wq, L1_attn_Wk, L1_attn_Wv, L1_attn_Wo, L1_attn_gate) + _L1_ffn_ref(xn, L1_ffn_gate_w, L1_ffn_gate_proj, L1_ffn_up_proj, L1_ffn_down_proj)
    return x

_drawn_inputs = setup_inputs


def setup_inputs(seed=0):
    import zlib

    import numpy as np

    out = dict(_drawn_inputs(seed))
    spreads = {'L0_attn_b_Q': (0.0, 0.385),
     'L0_attn_b_K': (0.0, 0.8),
     'L0_attn_b_V': (0.0, 0.1),
     'L0_attn_b_O': (0.0, 0.1),
     'L0_ffn_biases': (0.0, 0.1),
     'L1_attn_gate': (0.0, 0.8)}
    factors = {'L1_attn_Wq': 2.796,
     'L1_ffn_gate_w': 8.0,
     'L1_ffn_gate_proj': 8.0,
     'L1_ffn_up_proj': 8.0,
     'L1_ffn_down_proj': 8.0}
    for name, (base, spread) in spreads.items():
        noise = np.random.default_rng([zlib.crc32(name.encode()), seed]).standard_normal(out[name].shape)
        drawn = base * np.exp(spread * noise) if base else spread * noise
        out[name] = jnp.asarray(drawn.astype(out[name].dtype))
    for name, factor in factors.items():
        out[name] = (out[name] * factor).astype(out[name].dtype)
    return out
```

```python
from contextlib import ExitStack

import concourse.bass as bass
from concourse import mybir


F32 = mybir.dt.float32
F32R = mybir.dt.float32r
BF16 = mybir.dt.bfloat16
ALU = mybir.AluOpType
ACT = mybir.ActivationFunctionType
X_AXIS = mybir.AxisListType.X

P = 128
D = 256
KC = D // P
BATCH, SEQ = 2, 512
TOKENS = BATCH * SEQ
NT = TOKENS // P
QT = SEQ // P
EPS = 1e-5

HEADS0, DH0 = 16, 128
GROUP = 4
GROUPS = HEADS0 // GROUP
UNITS = BATCH * GROUP
TRI = QT * (QT + 1) // 2 * P
MASKED = -1e5

E0, TOP0, LAT, HID = 16, 8, 64, 128
ROUTE_SCALE = 2.5

HEADS1, DH1 = 16, 16
HM = P // DH1
VW = 32

E1, F1 = 8, 176
FC = E1 * F1 // P


def program(nc, a):
    with ExitStack() as ctx:
        def sb(name, shape, dt):
            return ctx.enter_context(nc.sbuf_tensor(name, shape, dt))

        def sem(name):
            return ctx.enter_context(nc.semaphore(name))

        bank = [ctx.enter_context(nc.psum_tensor(f"bank{i}", [P, 512], F32)) for i in range(8)]

        X = sb("X", [P, NT, D], F32)
        xnT_hi = sb("xnT_hi", [P, KC, TOKENS], F32R)
        xnT_lo = sb("xnT_lo", [P, KC, TOKENS], F32R)
        ident = sb("ident", [P, P], F32)
        small = sb("small", [P, 512], F32)
        bo_row = sb("bo_row", [P, D], F32)

        FWORDS, RWORDS = 18944, 26624
        farena = sb("farena", [P, FWORDS], F32)
        rarena = sb("rarena", [P, RWORDS], F32R)

        def layout(arena, limit, **shapes):
            at, views = 0, {}
            for name, shape in shapes.items():
                n = 1
                for s in shape:
                    n *= s
                v = arena[:, at:at + n]
                if len(shape) == 2:
                    v = v.rearrange("p (a b) -> p a b", a=shape[0])
                elif len(shape) == 3:
                    v = v.rearrange("p (a b c) -> p a b c", a=shape[0], b=shape[1])
                elif len(shape) == 4:
                    v = v.rearrange("p (a b c d) -> p a b c d", a=shape[0], b=shape[1], c=shape[2])
                views[name] = v
                at += n
            assert at <= limit, (at, limit)
            return views

        def f(v):
            return v.bitcast(F32)

        stats = small[:, 0:48].rearrange("p (t s) -> p t s", t=NT)
        mean_var = small[:, 48:64].rearrange("p (t s) -> p t s", t=NT)
        std = small[:, 64:72]
        rstd = small[:, 72:80]
        s_x = [sem(f"s_x{i}") for i in range(2)]
        s_const = sem("s_const")
        s_stats, s_aggr, s_eps, s_std, s_rstd = (sem(n) for n in ("s_stats", "s_aggr", "s_eps", "s_std", "s_rstd"))
        s_xn, s_xnt, s_xnh, s_xnl = (sem(n) for n in ("s_xn", "s_xnt", "s_xnh", "s_xnl"))
        xn = layout(farena, FWORDS, skip=(FWORDS - NT * D,), xn=(NT, D))["xn"]

        def norm_vector(dve, n):
            for t in range(NT):
                if n == 0 and t % 4 == 0:
                    dve.wait_ge(s_x[t // 4], 16)
                nc.vector.bn_stats(stats[:, t, :], X[:, t, :]).then_inc(s_stats, 1)
            for t in range(NT):
                dve.wait_ge(s_stats, NT * n + t + 1)
                nc.vector.bn_aggr(mean_var[:, t, :], stats[:, t, :]).then_inc(s_aggr, 1)
            dve.wait_ge(s_aggr, NT * (n + 1))
            nc.vector.tensor_scalar(std, mean_var[:, :, 1], EPS, None, ALU.add).then_inc(s_eps, 1)
            dve.wait_ge(s_std, n + 1)
            nc.vector.reciprocal(rstd, std).then_inc(s_rstd, 1)
            dve.wait_ge(s_rstd, n + 1)
            for t in range(NT):
                nc.vector.tensor_scalar(xn[:, t, :], X[:, t, :], mean_var[:, t, 0:1], rstd[:, t:t + 1],
                                        ALU.subtract, ALU.mult).then_inc(s_xn, 1)
            for r in range(4):
                k = 4 * n + r
                dve.wait_ge(s_xnh, k + 1)
                nc.vector.tensor_tensor(xnT_lo[:, :, 2 * P * r:2 * P * (r + 1)],
                                        bank[r % 2][:, :].rearrange("p (c t) -> p c t", c=KC),
                                        f(xnT_hi[:, :, 2 * P * r:2 * P * (r + 1)]),
                                        ALU.subtract).then_inc(s_xnl, 1)

        def norm_scalar(act, n):
            act.wait_ge(s_eps, n + 1)
            nc.scalar.activation(std, std, ACT.Sqrt).then_inc(s_std, 1)
            for r in range(4):
                act.wait_ge(s_xnt, 4 * n + r + 1)
                nc.scalar.activation(xnT_hi[:, :, 2 * P * r:2 * P * (r + 1)],
                                     bank[r % 2][:, :].rearrange("p (c t) -> p c t", c=KC),
                                     ACT.Identity).then_inc(s_xnh, 1)

        def norm_tensor(pe, n):
            if n == 0:
                pe.wait_ge(s_const, 16 * N_CONST)
            for r in range(4):
                pe.wait_ge(s_xn, NT * n + 2 * r + 2)
                if r >= 2:
                    pe.wait_ge(s_xnl, 4 * n + r - 1)
                for c in range(KC):
                    for t in range(2):
                        mm = nc.tensor.transpose(bank[r % 2][:, (2 * c + t) * P:(2 * c + t + 1) * P],
                                                 xn[:, 2 * r + t, c * P:(c + 1) * P], ident[:, :])
                mm.then_inc(s_xnt, 1)

        A = layout(farena, FWORDS, wqk_raw=(GROUP, 2, KC, P), wv_raw=(KC, GROUP * P), wo_raw=(GROUP, D),
                   k_scaled=(KC * P,), prob=(4, TRI))
        wqk_raw, wv_raw, wo_raw = A["wqk_raw"], A["wv_raw"], A["wo_raw"]
        k_scaled, prob = A["k_scaled"], A["prob"]
        R = layout(rarena, RWORDS, wqk_hi=(GROUP, 2, KC, P), wqk_lo=(GROUP, 2, KC, P),
                   wv_hi=(KC, GROUP * P), wv_lo=(KC, GROUP * P), wo_hi=(GROUP, D), wo_lo=(GROUP, D),
                   qk_hi=(2, 2, SEQ), qk_lo=(2, 2, SEQ), v_hi=(BATCH, QT, GROUP * P), v_lo=(BATCH, QT, GROUP * P),
                   pT_hi=(2, SEQ), pT_lo=(2, SEQ), zT_hi=(GROUP, SEQ), zT_lo=(GROUP, SEQ))
        wqk_hi, wqk_lo, wv_hi, wv_lo, wo_hi, wo_lo = (R[n] for n in ("wqk_hi", "wqk_lo", "wv_hi", "wv_lo", "wo_hi", "wo_lo"))
        qk_hi, qk_lo, v_hi, v_lo = (R[n] for n in ("qk_hi", "qk_lo", "v_hi", "v_lo"))
        pT_hi, pT_lo, zT_hi, zT_lo = (R[n] for n in ("pT_hi", "pT_lo", "zT_hi", "zT_lo"))
        bias_qkv = sb("bias_qkv", [P, 3, HEADS0], F32)
        scale0 = sb("scale0", [P, 2], F32)
        mask_neg = sb("mask_neg", [P, P], BF16)
        ident_bf = sb("ident_bf", [P, P], BF16)
        neg_max = small[:, 80:84]
        bias_now = small[:, 120:144].rearrange("p (u w) -> p u w", u=UNITS)
        row_sum = small[:, 84:92].rearrange("p (a b) -> p a b", a=2)
        row_inv = small[:, 92:100].rearrange("p (a b) -> p a b", a=2)

        s_wqk_raw = [sem(f"s_wqk_raw{h}") for h in range(GROUP)]
        s_wv_raw, s_wo_raw = sem("s_wv_raw"), sem("s_wo_raw")
        s_wtmp, s_wqk, s_wv, s_wo, s_bk = (sem(n) for n in ("s_wtmp", "s_wqk", "s_wv", "s_wo", "s_bk"))
        s_proj, s_proj_hi, s_proj_lo = (sem(n) for n in ("s_proj", "s_proj_hi", "s_proj_lo"))
        s_score, s_max, s_exp, s_inv, s_prob = (sem(n) for n in ("s_score", "s_max", "s_exp", "s_inv", "s_prob"))
        s_pT, s_pT_hi, s_pT_lo = (sem(n) for n in ("s_pT", "s_pT_hi", "s_pT_lo"))
        s_pv, s_z_hi, s_z_lo, s_y, s_y_added = (sem(n) for n in ("s_pv", "s_z_hi", "s_z_lo", "s_y", "s_y_added"))
        s_bo = sem("s_bo")
        s_bias = sem("s_bias")
        score_bank, pT_bank, proj_bank, z_bank, y_bank = bank[0:2], bank[2:4], bank[4:6], bank[6], bank[7]

        SCORED, TURNED, FINISHED = 1, 3, 4
        DEPTH = FINISHED + 1

        def jobs(u):
            return {0: [("q", 0, 0), ("k", 0, 2), ("v", 0, 3)],
                    1: [("q", 0, 0), ("v", 1, 1), ("k", 0, 2), ("v", 2, 3)],
                    2: [("q", 0, 0), ("v", 3, 1), ("k", 0, 2)],
                    3: [("q", 0, 0), ("k", 0, 2)]}[u % GROUP]

        JOBS = [(u, *job) for u in range(UNITS) for job in jobs(u)]
        NJ = len(JOBS)

        def job_number(u, kind, i=0):
            return next(n for n, j in enumerate(JOBS) if (j[0], j[1], j[2]) == (u, kind, i))

        def last_value_job(b):
            return job_number(GROUP * b + 2, "v", QT - 1)

        def slot_jobs(u, step):
            return [(n, kind, i) for n, (uu, kind, i, s) in enumerate(JOBS) if uu == u and s == step]

        def back(g, u, k):
            return (g, u - k) if u >= k else (g - 1, u - k + UNITS)

        def tri(i):
            return P * i * (i + 1) // 2

        def attn_tensor_slot(pe, g, u, first=False, tail=False):
            has = [not tail or k > u for k in range(DEPTH)] if not first else [u >= k for k in range(DEPTH)]

            def unit(k):
                gg, uu = back(g, u, k)
                return gg, uu, UNITS * gg + uu

            def value_product(k, kt):
                gg, uu, v = unit(k)
                b, h = uu // GROUP, uu % GROUP
                pe.wait_ge(s_pT_lo, QT * v + kt + 1)
                if kt == 0:
                    pe.wait_ge(s_z_lo, v)
                    pe.wait_ge(s_proj_lo, NJ * gg + last_value_job(b) + 1)
                n = kt % 2
                w = SEQ - kt * P
                hs = slice(h * P, (h + 1) * P)
                out = z_bank[:, kt * P:SEQ]
                nc.tensor.matmul(out, v_hi[:, b, kt, hs], pT_hi[:, n, 0:w], start=(kt == 0), stop=False)
                nc.tensor.matmul(out, v_hi[:, b, kt, hs], pT_lo[:, n, 0:w], start=False, stop=False)
                nc.tensor.matmul(out, v_lo[:, b, kt, hs], pT_hi[:, n, 0:w], start=False,
                                 stop=(kt == QT - 1)).then_inc(s_pv, 1)

            def output_product(gg, b, pair):
                n = 2 * (BATCH * gg + b) + pair
                if pair == 0:
                    pe.wait_ge(s_wo, 2 * (gg + 1))
                pe.wait_ge(s_z_lo, UNITS * gg + GROUP * (b + 1))
                pe.wait_ge(s_y_added, n)
                for t in range(2):
                    i = 2 * pair + t
                    ts = slice(i * P, (i + 1) * P)
                    for h in range(GROUP):
                        out = y_bank[:, t * D:(t + 1) * D]
                        nc.tensor.matmul(out, zT_hi[:, h, ts], wo_hi[:, h, :], start=(h == 0), stop=False)
                        nc.tensor.matmul(out, zT_hi[:, h, ts], wo_lo[:, h, :], start=False, stop=False)
                        mm = nc.tensor.matmul(out, zT_lo[:, h, ts], wo_hi[:, h, :], start=False,
                                              stop=(h == GROUP - 1))
                mm.then_inc(s_y, 1)

            for i in range(QT):
                if has[TURNED]:
                    gg, uu, v = unit(TURNED)
                    pe.wait_ge(s_prob, QT * (v + 1))
                    if not (first and u == TURNED and i < 2):
                        pe.wait_ge(s_pT_lo, QT * v + i - 1)
                    for q in range(i, QT):
                        mm = nc.tensor.transpose(pT_bank[i % 2][:, (q - i) * P:(q - i + 1) * P],
                                                 prob[:, uu % 4, tri(q) + i * P:tri(q) + (i + 1) * P], ident[:, :])
                    mm.then_inc(s_pT, 1)
                if has[SCORED]:
                    gg, uu, v = unit(SCORED)
                    if i == 0:
                        pe.wait_ge(s_proj_lo, NJ * gg + job_number(uu, "k") + 1)
                    if not (first and u == SCORED and i < 2):
                        pe.wait_ge(s_exp, QT * v + i - 1)
                    w = (i + 1) * P
                    par = uu % 2
                    qs = slice(i * P, (i + 1) * P)
                    out = score_bank[i % 2]
                    nc.tensor.matmul(out[:, 0:w], qk_hi[:, par, 0, qs], qk_hi[:, par, 1, 0:w], start=True, stop=False)
                    nc.tensor.matmul(out[:, i * P:w], ident_bf[:, :], mask_neg[:, :], start=False, stop=False)
                    nc.tensor.matmul(out[:, 0:w], qk_hi[:, par, 0, qs], qk_lo[:, par, 1, 0:w], start=False, stop=False)
                    nc.tensor.matmul(out[:, 0:w], qk_lo[:, par, 0, qs], qk_hi[:, par, 1, 0:w], start=False,
                                     stop=True).then_inc(s_score, 1)
                if i == 0 and has[FINISHED]:
                    value_product(FINISHED, QT - 1)
                if has[0]:
                    for n, kind, j in slot_jobs(u, i):
                        if not (first and n < 2):
                            pe.wait_ge(s_proj_lo, NJ * g + n - 1)
                        out = proj_bank[n % 2][:, :]
                        b, h = u // GROUP, u % GROUP
                        if kind == "v":
                            pe.wait_ge(s_wv, 2 * (g + 1))
                            tok = slice((QT * b + j) * P, (QT * b + j + 1) * P)
                            terms = [(xh[:, c, tok], wh[:, c, :]) for xh, wh in
                                     ((xnT_hi, wv_hi), (xnT_hi, wv_lo), (xnT_lo, wv_hi)) for c in range(KC)]
                        else:
                            pe.wait_ge(s_wqk, GROUP * g + h + 1)
                            tok = slice(SEQ * b, SEQ * (b + 1))
                            w = 0 if kind == "q" else 1
                            terms = [(wh[:, h, w, c, :], xh[:, c, tok]) for wh, xh in
                                     ((wqk_hi, xnT_hi), (wqk_hi, xnT_lo), (wqk_lo, xnT_hi)) for c in range(KC)]
                        for m, (lhs, rhs) in enumerate(terms):
                            mm = nc.tensor.matmul(out, lhs, rhs, start=(m == 0), stop=(m == len(terms) - 1))
                        mm.then_inc(s_proj, 1)
                if i >= 1 and has[TURNED]:
                    value_product(TURNED, i - 1)
                if u % GROUP == GROUP - 1 and i >= 2 and has[FINISHED]:
                    gg, uu, _ = unit(FINISHED)
                    output_product(gg, uu // GROUP, i - 2)

        def attn_scalar_slot(act, g, u, first=False, tail=False):
            has = [not tail or k > u for k in range(DEPTH)] if not first else [u >= k for k in range(DEPTH)]

            def unit(k):
                gg, uu = back(g, u, k)
                return gg, uu, UNITS * gg + uu

            for i in range(QT):
                if has[TURNED]:
                    gg, uu, v = unit(TURNED)
                    act.wait_ge(s_pT, QT * v + i + 1)
                    if not (first and u == TURNED and i < 2):
                        act.wait_ge(s_pv, QT * v + i - 1)
                    w = SEQ - i * P
                    nc.scalar.activation(pT_hi[:, i % 2, 0:w], pT_bank[i % 2][:, 0:w], ACT.Identity).then_inc(s_pT_hi, 1)
                if has[SCORED]:
                    gg, uu, v = unit(SCORED)
                    act.wait_ge(s_max, QT * v + i + 1)
                    if not first or u >= 5:
                        act.wait_ge(s_pT, QT * (v - 3))
                    w = (i + 1) * P
                    nc.scalar.activation(prob[:, uu % 4, tri(i):tri(i) + w], score_bank[i % 2][:, 0:w], ACT.Exp,
                                         bias=neg_max[:, i:i + 1],
                                         accum_out=row_sum[:, uu % 2, i:i + 1]).then_inc(s_exp, 1)
                if i == 0 and has[FINISHED]:
                    gg, uu, v = unit(FINISHED)
                    act.wait_ge(s_pv, QT * (v + 1))
                    if not first or uu >= GROUP:
                        act.wait_ge(s_y, 2 * (BATCH * gg + uu // GROUP))
                    nc.scalar.activation(zT_hi[:, uu % GROUP, :], z_bank[:, :], ACT.Identity,
                                         bias=bias_now[:, uu, 2:3]).then_inc(s_z_hi, 1)
                if has[0]:
                    for n, kind, j in slot_jobs(u, i):
                        act.wait_ge(s_proj, NJ * g + n + 1)
                        b, h = u // GROUP, u % GROUP
                        out, bias = job_target(u, kind, j, qk_hi, v_hi), 0.0
                        if kind == "v":
                            if not first:
                                act.wait_ge(s_pv, QT * (UNITS * g - (GROUP if b == 0 else 0)))
                        else:
                            if not first or u >= 2:
                                act.wait_ge(s_score, QT * (UNITS * g + u - 1))
                            act.wait_ge(s_bias, UNITS * g + u + 1)
                            bias = bias_now[:, u, 0:1] if kind == "q" else bias_now[:, u, 1:2]
                        nc.scalar.activation(out, proj_bank[n % 2][:, :], ACT.Identity, bias=bias).then_inc(s_proj_hi, 1)

        def job_target(u, kind, j, qk, v):
            return v[:, u // GROUP, j, :] if kind == "v" else qk[:, u % 2, 0 if kind == "q" else 1, :]

        def attn_vector_slot(dve, g, u, first=False, tail=False):
            has = [not tail or k > u for k in range(DEPTH)] if not first else [u >= k for k in range(DEPTH)]

            def unit(k):
                gg, uu = back(g, u, k)
                return gg, uu, UNITS * gg + uu

            if has[0] and not (first and u == 0):
                nc.vector.tensor_copy(bias_now[:, u, :], bias_qkv[:, :, bass.ds(GROUP * g + u % GROUP, 1)]
                                      .rearrange("p w o -> p (w o)")).then_inc(s_bias, 1)
            for i in range(QT):
                if has[SCORED]:
                    gg, uu, v = unit(SCORED)
                    dve.wait_ge(s_score, QT * v + i + 1)
                    if not (first and u == SCORED):
                        dve.wait_ge(s_exp, QT * (v - 1) + i + 1)
                    nc.vector.tensor_reduce(neg_max[:, i:i + 1], score_bank[i % 2][:, 0:(i + 1) * P], X_AXIS,
                                            ALU.max, negate=True).then_inc(s_max, 1)
                if has[TURNED]:
                    gg, uu, v = unit(TURNED)
                    dve.wait_ge(s_pT_hi, QT * v + i + 1)
                    w = SEQ - i * P
                    nc.vector.tensor_tensor(pT_lo[:, i % 2, 0:w], pT_bank[i % 2][:, 0:w], f(pT_hi[:, i % 2, 0:w]),
                                            ALU.subtract).then_inc(s_pT_lo, 1)
                if i == 0 and has[FINISHED]:
                    gg, uu, v = unit(FINISHED)
                    dve.wait_ge(s_z_hi, v + 1)
                    nc.vector.scalar_tensor_tensor(
                        out=zT_lo[:, uu % GROUP, :], in0=z_bank[:, :],
                        scalar=bias_now[:, uu, 2:3],
                        in1=f(zT_hi[:, uu % GROUP, :]), op0=ALU.add, op1=ALU.subtract).then_inc(s_z_lo, 1)
                if has[SCORED]:
                    gg, uu, v = unit(SCORED)
                    dve.wait_ge(s_exp, QT * v + i + 1)
                    if not first or u >= 3:
                        dve.wait_ge(s_prob, QT * (v - 2) + i + 1)
                    nc.vector.reciprocal(row_inv[:, uu % 2, i:i + 1], row_sum[:, uu % 2, i:i + 1]).then_inc(s_inv, 1)
                if has[0]:
                    for n, kind, j in slot_jobs(u, i):
                        dve.wait_ge(s_proj_hi, NJ * g + n + 1)
                        h = u % GROUP
                        hi, lo = job_target(u, kind, j, qk_hi, v_hi), job_target(u, kind, j, qk_lo, v_lo)
                        if kind == "v":
                            nc.vector.tensor_tensor(lo, proj_bank[n % 2][:, :], f(hi), ALU.subtract).then_inc(s_proj_lo, 1)
                        else:
                            if kind == "q":
                                dve.wait_ge(s_bias, UNITS * g + u + 1)
                            nc.vector.scalar_tensor_tensor(
                                out=lo, in0=proj_bank[n % 2][:, :],
                                scalar=bias_now[:, u, 0:1] if kind == "q" else bias_now[:, u, 1:2],
                                in1=f(hi), op0=ALU.add, op1=ALU.subtract).then_inc(s_proj_lo, 1)
                if u % GROUP == GROUP - 1 and i >= 2 and has[FINISHED]:
                    gg, uu, _ = unit(FINISHED)
                    b, pair = uu // GROUP, i - 2
                    n = 2 * (BATCH * gg + b) + pair
                    dve.wait_ge(s_y, n + 1)
                    rows = X[:, QT * b + 2 * pair:QT * b + 2 * pair + 2, :]
                    if first and n == 0:
                        dve.wait_ge(s_bo, 1)
                    nc.vector.tensor_tensor(rows, y_bank[:, :].rearrange("p (t d) -> p t d", t=2), rows,
                                            ALU.add).then_inc(s_y_added, 1)

        def one(n):
            return scale0[:, 1:2].broadcast_to((P, n))

        def split_qk(pool, g, h, count):
            pool.wait_ge(s_wqk_raw[h], 16 * (g + 1))
            nc.gpsimd.tensor_tensor(wqk_hi[:, h, 0, :, :].rearrange("p c e -> p (c e)"),
                                    wqk_raw[:, h, 0, :, :].rearrange("p c e -> p (c e)"),
                                    one(KC * P), ALU.mult).then_inc(s_wtmp, 1)
            nc.gpsimd.tensor_tensor(k_scaled, wqk_raw[:, h, 1, :, :].rearrange("p c e -> p (c e)"),
                                    scale0[:, 0:1].broadcast_to((P, KC * P)), ALU.mult).then_inc(s_wtmp, 1)
            pool.wait_ge(s_wtmp, count + 2)
            nc.gpsimd.tensor_tensor(wqk_hi[:, h, 1, :, :].rearrange("p c e -> p (c e)"), k_scaled, one(KC * P),
                                    ALU.mult).then_inc(s_wtmp, 1)
            nc.gpsimd.tensor_tensor(wqk_lo[:, h, 0, :, :], wqk_raw[:, h, 0, :, :], f(wqk_hi[:, h, 0, :, :]),
                                    ALU.subtract).then_inc(s_wtmp, 1)
            pool.wait_ge(s_wtmp, count + 4)
            nc.gpsimd.tensor_tensor(wqk_lo[:, h, 1, :, :].rearrange("p c e -> p (c e)"), k_scaled,
                                    f(wqk_hi[:, h, 1, :, :]).rearrange("p c e -> p (c e)"),
                                    ALU.subtract).then_inc(s_wqk, 1)
            pool.wait_ge(s_wqk, GROUP * g + h + 1)

        def split_half(pool, s_raw, s_done, g, half, hi, lo, raw, count):
            pool.wait_ge(s_raw, 16 * (g + 1))
            nc.gpsimd.tensor_tensor(hi, raw, one(GROUP * P), ALU.mult).then_inc(s_wtmp, 1)
            pool.wait_ge(s_wtmp, count + 1)
            nc.gpsimd.tensor_tensor(lo, raw, f(hi), ALU.subtract).then_inc(s_done, 1)

        W_STEPS = GROUP * 4 + 4

        def split_v(pool, g, c, count):
            split_half(pool, s_wv_raw, s_wv, g, c, wv_hi[:, c, :], wv_lo[:, c, :], wv_raw[:, c, :], count)

        def split_o(pool, g, c, count):
            hs = slice(2 * c, 2 * c + 2)
            hi, lo, raw = (w[:, hs, :].rearrange("p h d -> p (h d)") for w in (wo_hi, wo_lo, wo_raw))
            split_half(pool, s_wo_raw, s_wo, g, c, hi, lo, raw, count)

        def normalise(pool, g, u, first=False):
            gg, uu = back(g, u, 1)
            v = UNITS * gg + uu
            for i in range(QT):
                pool.wait_ge(s_inv, QT * v + i + 1)
                p = prob[:, uu % 4, tri(i):tri(i) + (i + 1) * P]
                nc.gpsimd.tensor_tensor(p, p, row_inv[:, uu % 2, i:i + 1].broadcast_to((P, (i + 1) * P)),
                                        ALU.mult).then_inc(s_prob, 1)

        def attn_pool_early(pool, g, first=False):
            base = W_STEPS * g
            if first:
                split_qk(pool, g, 0, base)
                split_qk(pool, g, 1, base + 4)
                split_v(pool, g, 0, base + 8)
                split_v(pool, g, 1, base + 9)
                split_qk(pool, g, 2, base + 10)
                normalise(pool, g, 1, first)
                split_qk(pool, g, 3, base + 14)
                pool.wait_ge(s_xnt, 4)
                nc.gpsimd.tensor_tensor(X[:], X[:], bo_row[:, :].rearrange("p (o d) -> p o d", o=1)
                                        .broadcast_to((P, NT, D)), ALU.add).then_inc(s_bo, 1)
            else:
                normalise(pool, g, 0)
                pool.wait_ge(s_proj, NJ * (g - 1) + job_number(UNITS - 1, "k") + 1)
                split_qk(pool, g, 3, base + 14)
                normalise(pool, g, 1)
            normalise(pool, g, 2, first)
            normalise(pool, g, 3, first)
            normalise(pool, g, 4, first)
            if not first:
                pool.wait_ge(s_y, 4 * g)
            split_o(pool, g, 0, base + 18)
            split_o(pool, g, 1, base + 19)

        def attn_pool_late(pool, g, ahead=True):
            base = W_STEPS * (g + 1)
            for u in range(5, UNITS):
                normalise(pool, g, u)
                if ahead:
                    h = u - 5
                    pool.wait_ge(s_proj, NJ * g + job_number(GROUP + h, "k") + 1)
                    if u < 7:
                        split_qk(pool, g + 1, h, base + 4 * h)
                    else:
                        pool.wait_ge(s_proj, NJ * g + last_value_job(1) + 1)
                        split_v(pool, g + 1, 0, base + 8)
                        split_v(pool, g + 1, 1, base + 9)
                        split_qk(pool, g + 1, 2, base + 10)

        def attn_loads(sp, g, first=False):
            for h in range(GROUP):
                if not first:
                    sp.wait_ge(s_wqk, GROUP * (g - 1) + h + 1)
                sp.dma_start(wqk_raw[:, h, :, :, :].rearrange("p a c e -> p (a c e)"),
                             a["w_qk"][bass.ds(GROUP * g + h, 1), :, :].rearrange("o p n -> p (o n)")).then_inc(s_wqk_raw[h], 16)
                if h == 1:
                    if not first:
                        sp.wait_ge(s_wv, 2 * g)
                    sp.dma_start(wv_raw.rearrange("p c e -> p (c e)"),
                                 a["w_v"][bass.ds(g, 1), :, :].rearrange("o p n -> p (o n)")).then_inc(s_wv_raw, 16)
            if not first:
                sp.wait_ge(s_wo, 2 * g)
            sp.dma_start(wo_raw.rearrange("p c e -> p (c e)"),
                         a["w_o"][bass.ds(g, 1), :, :].rearrange("o p n -> p (o n)")).then_inc(s_wo_raw, 16)

        ATTN_F = 2048 + 1024 + 1024 + 256 + 4 * TRI
        ATTN_DONE = 4 * GROUPS

        B0 = layout(farena, FWORDS, skip=(ATTN_F,), router=(KC, E0), down=(KC, 2 * LAT), gate_up=(2, KC, HID),
                    shared_out=(D,), lat_up=(D,), pick=(E0, P), route_bias=(E0,),
                    expert=(2, 2 * HID), expert_out=(2, LAT), e=(NT, E0), p=(NT, E0), b=(NT, E0), left=(NT, E0),
                    chosen=(NT, E0), w=(NT, E0), top=(NT, 8), total=(NT,), gate=(2, SEQ), prod=(2, SEQ), hid=(2, SEQ))
        M0 = layout(rarena, RWORDS, router_hi=(KC, E0), router_lo=(KC, E0), down_hi=(KC, 2 * LAT), down_lo=(KC, 2 * LAT),
                    gate_up_hi=(2, KC, HID), gate_up_lo=(2, KC, HID), expert=(2, 2 * HID), pick=(2, P),
                    w_split=(NT, 2 * E0), end_of_weights=(1,), wT=(TOKENS,), lat_hi=(TOKENS,), lat_lo=(TOKENS,))
        N0 = layout(farena, FWORDS, shared_hid=(TOKENS,), acc=(TOKENS,))
        zeros_bf = sb("zeros_bf", [P, LAT + SEQ], BF16)
        s_m0_raw, s_m0_w, s_m0_tmp = sem("s_m0_raw"), sem("s_m0_w"), sem("s_m0_tmp")
        s_logit0, s_e0, s_route0, s_split0, s_wT_ps, s_wT = (sem(n) for n in (
            "s_logit0", "s_e0", "s_route0", "s_split0", "s_wT_ps", "s_wT"))
        s_lat, s_lat_hi, s_lat_lo = (sem(n) for n in ("s_lat", "s_lat_hi", "s_lat_lo"))
        s_ex_raw = [sem(f"s_ex_raw{i}") for i in range(2)]
        s_exo_raw = [sem(f"s_exo_raw{i}") for i in range(2)]
        s_ex_hi, s_ex_lo, s_pick = (sem(n) for n in ("s_ex_hi", "s_ex_lo", "s_pick"))
        s_front, s_relu, s_prod, s_weighted, s_hid, s_back = (sem(n) for n in (
            "s_front", "s_relu", "s_prod", "s_weighted", "s_hid", "s_back"))
        s_zeros, s_acc, s_out0, s_out0_added = (sem(n) for n in ("s_zeros", "s_acc", "s_out0", "s_out0_added"))
        N_M0 = 8

        def mix0_loads(sp):
            for dst, name in ((B0["router"], "m0_router"), (B0["gate_up"], "m0_gate_up"),
                              (B0["shared_out"], "m0_shared_out"), (B0["down"][:, :, 0:LAT], "m0_down"),
                              (B0["down"][:, :, LAT:2 * LAT], "m0_down"), (B0["lat_up"][0:LAT, :], "m0_lat_up"),
                              (B0["pick"][0:2 * E0, :, :], "m0_pick")):
                sp.dma_start(dst, a[name]).then_inc(s_m0_raw, 16)
            sp.dma_start(B0["route_bias"], a["m0_bias"].broadcast_to((P, E0))).then_inc(s_m0_raw, 16)

        def expert_loads(sp, e, par, first=False):
            if not first:
                sp.wait_ge(s_ex_lo, e - 1)
            for half in range(2):
                sp.dma_start(B0["expert"][half * LAT:(half + 1) * LAT, par, :],
                             a["m0_expert"][:, bass.ds(e, 1), :].rearrange("l o n -> l (o n)")).then_inc(s_ex_raw[par], 16)
            if not first:
                sp.wait_ge(s_back, 2 * e - 2)
            sp.dma_start(B0["expert_out"][:, par, :],
                         a["m0_expert_out"][:, bass.ds(e, 1), :].rearrange("l o n -> l (o n)")).then_inc(s_exo_raw[par], 16)

        def mix0_prepare(pool):
            pool.wait_ge(s_m0_raw, 16 * N_M0)
            pool.wait_ge(s_proj, NJ * GROUPS)
            pool.wait_ge(s_y_added, ATTN_DONE)
            nc.gpsimd.memset(zeros_bf[:, :], 0.0).then_inc(s_zeros, 1)
            k = 0
            for name in ("router", "down", "gate_up"):
                n = {"router": KC * E0, "down": KC * 2 * LAT, "gate_up": 2 * KC * HID}[name]
                flat = "p a b -> p (a b)" if name != "gate_up" else "p a b c -> p (a b c)"
                raw, hi, lo = (v.rearrange(flat) for v in (B0[name], M0[name + "_hi"], M0[name + "_lo"]))
                nc.gpsimd.tensor_tensor(hi, raw, one(n), ALU.mult).then_inc(s_m0_tmp, 1)
                k += 1
                pool.wait_ge(s_m0_tmp, k)
                nc.gpsimd.tensor_tensor(lo, raw, f(hi), ALU.subtract).then_inc(s_m0_w, 1)

        def expert_hi(pool, e, par, first=False):
            pool.wait_ge(s_ex_raw[par], 16 * (e - par) + 32)
            if not first:
                pool.wait_ge(s_front, 2 * e)
            nc.gpsimd.tensor_tensor(M0["expert"][:, par, :], B0["expert"][:, par, :], one(2 * HID),
                                    ALU.mult).then_inc(s_ex_hi, 1)

        def expert_lo(dve, e, par, first=False):
            dve.wait_ge(s_ex_hi, e + 1)
            w = M0["expert"][LAT:P, par, :]
            nc.vector.tensor_tensor(w, B0["expert"][LAT:P, par, :], f(w), ALU.subtract).then_inc(s_ex_lo, 1)
            nc.vector.tensor_scalar(M0["pick"][0:2 * E0, par, :],
                                    B0["pick"][0:2 * E0, bass.ds(e, 1), :].rearrange("p o n -> p (o n)"),
                                    1.0, None, ALU.mult).then_inc(s_pick, 1)

        def front(pe, n, par, x, first=False):
            if x == 0:
                pe.wait_ge(s_pick, (n // 2 if isinstance(n, int) else n // 2) + 1)
            half = slice(x * SEQ, (x + 1) * SEQ)
            pe.wait_ge(s_weighted, n) if not first else None
            for w, out in ((1, bank[x]), (0, bank[2 + x])):
                lhs = M0["expert"][:, par, w * HID:(w + 1) * HID]
                nc.tensor.matmul(out[:, :], lhs, M0["lat_hi"][:, half], start=True, stop=False)
                nc.tensor.matmul(out[:, :], lhs, M0["lat_lo"][:, half], start=False, stop=True)
            nc.tensor.matmul(bank[4 + x][:, :], M0["pick"][0:2 * E0, par, :], M0["wT"][0:2 * E0, half],
                             start=True, stop=True).then_inc(s_front, 1)

        def back_product(pe, n, par, x, raw_count, last=False):
            pe.wait_ge(s_hid, n + 3)
            if x == 0:
                pe.wait_ge(s_exo_raw[par], raw_count)
            nc.tensor.matmul(bank[6 + x][0:LAT, :], B0["expert_out"][:, par, :], B0["hid"][:, x, :],
                             start=False, stop=last, skip_group_check=True).then_inc(s_back, 1)

        def mix0_tensor(pe):
            pe.wait_ge(s_y_added, ATTN_DONE)
            pe.wait_ge(s_m0_w, 3)
            for t in range(NT):
                k = 0
                for xs, ws in ((xnT_hi, "router_hi"), (xnT_hi, "router_lo"), (xnT_lo, "router_hi")):
                    for c in range(KC):
                        mm = nc.tensor.matmul(bank[4][:, t * E0:(t + 1) * E0], xs[:, c, t * P:(t + 1) * P],
                                              M0[ws][:, c, :], start=(k == 0), stop=(k == 2 * KC + 1))
                        k += 1
            mm.then_inc(s_logit0, 1)
            for x in range(2):
                half = slice(x * SEQ, (x + 1) * SEQ)
                k = 0
                for ws, xs in (("down_hi", xnT_hi), ("down_hi", xnT_lo), ("down_lo", xnT_hi)):
                    for c in range(KC):
                        mm = nc.tensor.matmul(bank[6 + x][:, :], M0[ws][:, c, :], xs[:, c, half],
                                              start=(k == 0), stop=(k == 2 * KC + 1))
                        k += 1
                mm.then_inc(s_lat, 1)
            for x in range(2):
                half = slice(x * SEQ, (x + 1) * SEQ)
                for w, out in ((1, bank[x]), (0, bank[2 + x])):
                    k = 0
                    for ws, xs in (("gate_up_hi", xnT_hi), ("gate_up_hi", xnT_lo), ("gate_up_lo", xnT_hi)):
                        for c in range(KC):
                            mm = nc.tensor.matmul(out[:, :], M0[ws][:, w, c, :], xs[:, c, half],
                                                  start=(k == 0), stop=(k == 2 * KC + 1))
                            k += 1
                mm.then_inc(s_front, 1)
            pe.wait_ge(s_split0, 2)
            pe.wait_ge(s_e0, 1)
            for t in range(NT):
                mm = nc.tensor.transpose(bank[4 + t // 4][0:2 * E0, (t % 4) * P:(t % 4 + 1) * P],
                                         f(M0["w_split"][:, t, :]), ident[:, :])
                if t % 4 == 3:
                    mm.then_inc(s_wT_ps, 1)
            pe.wait_ge(s_wT, 2)
            pe.wait_ge(s_lat_lo, 2)
            pe.wait_ge(s_zeros, 1)
            for x in range(2):
                nc.tensor.matmul(bank[6 + x][0:LAT, :], zeros_bf[:, 0:LAT], zeros_bf[:, LAT:LAT + SEQ], start=True, stop=False,
                                 skip_group_check=True)
            pe.wait_ge(s_prod, 1)
            front(pe, 0, 0, 0, first=True)

            def pair(k, last=False):
                for s in range(4):
                    m = s + 1
                    if not (last and m == 4):
                        if m == 1:
                            pe.wait_ge(s_prod, 2) if isinstance(k, int) and k == 0 else None
                        front(pe, 4 * k + m, (m // 2) % 2, m % 2)
                    back_product(pe, 4 * k + s, s // 2, s % 2, 16 * (k + 1), last=last and s >= 2)

            with pe.Fori(0, E0 // 2 - 1) as k:
                pair(k)
            pair(E0 // 2 - 1, last=True)
            pe.wait_ge(s_acc, 2)
            for t in range(NT):
                out = bank[t // 2][:, (t % 2) * D:(t % 2 + 1) * D]
                ts = slice(t * P, (t + 1) * P)
                nc.tensor.matmul(out, N0["shared_hid"][:, ts], B0["shared_out"], start=True, stop=False)
                mm = nc.tensor.matmul(out, N0["acc"][0:LAT, ts], B0["lat_up"][0:LAT, :], start=False, stop=True)
                if t % 2:
                    mm.then_inc(s_out0, 1)

        def mix0_scalar(act):
            act.wait_ge(s_y_added, ATTN_DONE)
            act.wait_ge(s_logit0, 1)
            nc.scalar.activation(B0["e"].rearrange("p t e -> p (t e)"), bank[4][:, 0:NT * E0], ACT.Exp,
                                 scale=-1.0).then_inc(s_e0, 1)
            for x in range(2):
                act.wait_ge(s_lat, x + 1)
                nc.scalar.activation(M0["lat_hi"][:, x * SEQ:(x + 1) * SEQ], bank[6 + x][:, :],
                                     ACT.Identity).then_inc(s_lat_hi, 1)
            for x in range(2):
                act.wait_ge(s_front, x + 1)
                nc.scalar.activation(B0["gate"][:, x, :], bank[x][:, :], ACT.Relu).then_inc(s_relu, 1)
            for x in range(2):
                act.wait_ge(s_wT_ps, x + 1)
                nc.scalar.activation(M0["wT"][0:2 * E0, x * SEQ:(x + 1) * SEQ], bank[4 + x][0:2 * E0, :],
                                     ACT.Identity).then_inc(s_wT, 1)

            def pair(k, last=False):
                for s in range(4):
                    n = 4 * k + s
                    act.wait_ge(s_front, n + 3)
                    act.wait_ge(s_hid, n + 1)
                    nc.scalar.activation(B0["gate"][:, s % 2, :], bank[s % 2][:, :], ACT.Relu).then_inc(s_relu, 1)

            with act.Fori(0, E0 // 2 - 1) as k:
                pair(k)
            pair(E0 // 2 - 1, last=True)
            for x in range(2):
                act.wait_ge(s_back, 2 * E0 - 1 + x)
                nc.scalar.activation(N0["acc"][0:LAT, x * SEQ:(x + 1) * SEQ], bank[6 + x][0:LAT, :],
                                     ACT.Identity).then_inc(s_acc, 1)

        def mix0_vector(dve):
            done = [0]

            def step(ins):
                done[0] += 1
                ins.then_inc(s_route0, 1)
                dve.wait_ge(s_route0, done[0])

            def wide(v):
                return v.rearrange("p (t o) -> p t o", o=1).broadcast_to((P, NT, E0))

            e, p, b, left, chosen, w = (B0[n] for n in ("e", "p", "b", "left", "chosen", "w"))
            top, total = B0["top"], B0["total"]
            dve.wait_ge(s_m0_raw, 16 * N_M0)
            dve.wait_ge(s_e0, 1)
            step(nc.vector.tensor_scalar(e, e, 1.0, None, ALU.add))
            step(nc.vector.reciprocal(p, e))
            step(nc.vector.tensor_tensor(b, p, B0["route_bias"].rearrange("p (o e) -> p o e", o=1)
                                         .broadcast_to((P, NT, E0)), ALU.add))
            for t in range(NT):
                step(nc.vector.max(top[:, t, :], b[:, t, :]))
                step(nc.vector.match_replace(left[:, t, :], top[:, t, :], b[:, t, :], -3.0e38))
            step(nc.vector.tensor_tensor(chosen, left, b, ALU.not_equal))
            step(nc.vector.tensor_tensor(chosen, chosen, p, ALU.mult))
            step(nc.vector.tensor_reduce(total, chosen, X_AXIS, ALU.add))
            step(nc.vector.reciprocal(total, total))
            step(nc.vector.tensor_scalar(total, total, ROUTE_SCALE, None, ALU.mult))
            step(nc.vector.tensor_tensor(w, chosen, wide(total), ALU.mult))
            nc.vector.tensor_copy(M0["w_split"][:, :, 0:E0], w).then_inc(s_split0, 1)
            dve.wait_ge(s_split0, 1)
            nc.vector.tensor_tensor(M0["w_split"][:, :, E0:2 * E0], w, f(M0["w_split"][:, :, 0:E0]),
                                    ALU.subtract).then_inc(s_split0, 1)
            for x in range(2):
                dve.wait_ge(s_lat_hi, x + 1)
                half = slice(x * SEQ, (x + 1) * SEQ)
                nc.vector.tensor_tensor(M0["lat_lo"][:, half], bank[6 + x][:, :], f(M0["lat_hi"][:, half]),
                                        ALU.subtract).then_inc(s_lat_lo, 1)
            for x in range(2):
                dve.wait_ge(s_relu, x + 1)
                nc.vector.tensor_tensor(B0["prod"][:, x, :], bank[2 + x][:, :], B0["gate"][:, x, :],
                                        ALU.mult).then_inc(s_prod, 1)
            expert_lo(dve, 0, 0)

            def pair(k, last=False):
                for s in range(4):
                    n = 4 * k + s
                    if s == 0:
                        expert_lo(dve, 2 * k + 1, 1)
                    if s == 2 and not last:
                        expert_lo(dve, 2 * k + 2, 0)
                    dve.wait_ge(s_relu, n + 3)
                    dve.wait_ge(s_hid, n + 1)
                    nc.vector.tensor_tensor(B0["prod"][:, s % 2, :], bank[2 + s % 2][:, :], B0["gate"][:, s % 2, :],
                                            ALU.mult).then_inc(s_prod, 1)
                    dve.wait_ge(s_prod, n + 3)
                    nc.vector.tensor_tensor(B0["prod"][:, s % 2, :], bank[4 + s % 2][:, :], B0["prod"][:, s % 2, :],
                                            ALU.mult).then_inc(s_weighted, 1)

            with dve.Fori(0, E0 // 2 - 1) as k:
                pair(k)
            pair(E0 // 2 - 1, last=True)
            for r in range(NT // 2):
                dve.wait_ge(s_out0, r + 1)
                rows = X[:, 2 * r:2 * r + 2, :]
                nc.vector.tensor_tensor(rows, bank[r][:, :].rearrange("p (t d) -> p t d", t=2), rows,
                                        ALU.add).then_inc(s_out0_added, 1)

        def mix0_pool(pool):
            mix0_prepare(pool)
            expert_hi(pool, 0, 0, first=True)
            for x in range(2):
                pool.wait_ge(s_prod, x + 1)
                nc.gpsimd.tensor_tensor(N0["shared_hid"][:, x * SEQ:(x + 1) * SEQ], B0["prod"][:, x, :],
                                        B0["gate"][:, x, :], ALU.mult).then_inc(s_hid, 1)

            def pair(k, last=False):
                for s in range(4):
                    n = 4 * k + s
                    if s == 0:
                        expert_hi(pool, 2 * k + 1, 1)
                    if s == 2 and not last:
                        expert_hi(pool, 2 * k + 2, 0)
                    pool.wait_ge(s_weighted, n + 1)
                    if not (isinstance(k, int) and n < 2):
                        pool.wait_ge(s_back, n - 1)
                    nc.gpsimd.tensor_tensor(B0["hid"][:, s % 2, :], B0["prod"][:, s % 2, :], B0["gate"][:, s % 2, :],
                                            ALU.mult).then_inc(s_hid, 1)

            pair(0)
            with pool.Fori(1, E0 // 2 - 1) as k:
                pair(k)
            pair(E0 // 2 - 1, last=True)

        STEPS = BATCH * KC
        TILES = HM * QT
        L1a = layout(farena, FWORDS, rope=(4, SEQ), w_raw=(3, KC, D), cos=(SEQ,), sin=(SEQ,), blocks=(HM, DH1 + 1),
                     gate=(HEADS1,), w_out=(KC, D), rot=(2, KC, SEQ), low=(KC, SEQ), k_feat=(KC, SEQ),
                     memory=(STEPS, HM, DH1 + 1), q_feat=(STEPS, SEQ), k_rows=(NT, D),
                     values=(STEPS, QT, HM, DH1 + 1), attended=(STEPS, QT, HM, DH1 + 1))
        L1b = layout(farena, FWORDS, prob=(2, SEQ), head_values=(HM, QT, VW), z=(SEQ,), skip=(1024 + 552 + 1136,),
                     pT=(2, QT, SEQ))
        L1c = layout(farena, FWORDS, skip=(2048 + 1536 + 1024 + 136 + 16 + 512,), mixed=(KC, TOKENS), out=(2, 2, D),
                     inv=(2, 2, HEADS1), gates=(2, HEADS1))
        pick_raw = layout(farena, FWORDS, skip=(FWORDS - 4 * 4 * P - 584,), pick=(4, 4, P))["pick"]
        R1 = layout(rarena, RWORDS, w_hi=(3, KC, D), w_lo=(3, KC, D), qk_hi=(2, STEPS, SEQ), qk_lo=(2, STEPS, SEQ),
                    pick=(4, 4, P), pairs=(2, 4, SEQ))
        names = ("s_l1_raw s_l1_out_raw s_l1_tmp s_l1_w s_pick1 s_ones s_proj1 s_rope s_rot s_hi1 s_min1 s_exp1 s_lo1 s_feat "
                 "s_kT s_k_rows s_v1 s_values s_mem_ps s_mem s_sel_q s_sel_k s_pair_q s_pair_k s_hv s_score1 s_max1 "
                 "s_prob1 s_pT1 s_pT_even s_pT_odd s_pv1 s_z1 s_zT1 s_att s_gates s_memout s_inv1 s_mix_a s_mix_b "
                 "s_mix s_mixT s_mixT_sb s_wo1 s_att_added").split()
        (s_l1_raw, s_l1_out_raw, s_l1_tmp, s_l1_w, s_pick1, s_ones, s_proj1, s_rope, s_rot, s_hi1, s_min1, s_exp1, s_lo1, s_feat,
         s_kT, s_k_rows, s_v1, s_values, s_mem_ps, s_mem, s_sel_q, s_sel_k, s_pair_q, s_pair_k, s_hv, s_score1, s_max1,
         s_prob1, s_pT1, s_pT_even, s_pT_odd, s_pv1, s_z1, s_zT1, s_att, s_gates, s_memout, s_inv1, s_mix_a, s_mix_b,
         s_mix, s_mixT, s_mixT_sb, s_wo1, s_att_added) = (sem(n) for n in names)
        neg_max1 = small[:, 112:116]
        N_L1 = 5
        C = DH1 + 1

        def l1_loads(sp):
            for dst, name in ((L1a["w_raw"], "l1_w"), (L1a["cos"], "l1_cos"), (L1a["sin"], "l1_sin"),
                              (L1a["blocks"], "l1_blocks")):
                sp.dma_start(dst, a[name]).then_inc(s_l1_raw, 16)
            sp.dma_start(L1a["gate"], a["l1_gate"].broadcast_to((P, HEADS1))).then_inc(s_l1_raw, 16)
            sp.dma_start(L1a["w_out"], a["l1_w_out"]).then_inc(s_l1_out_raw, 16)
            sp.wait_ge(s_out0_added, 4)
            sp.wait_ge(s_xnt, 8)
            sp.dma_start(pick_raw, a["l1_pick"]).then_inc(s_l1_out_raw, 16)

        def l1_pool_project(pool):
            pool.wait_ge(s_l1_raw, 16 * N_L1)
            pool.wait_ge(s_out0_added, 4)
            for w in range(3):
                flat = "p c d -> p (c d)"
                raw, hi, lo = (v[:, w, :, :].rearrange(flat) for v in (L1a["w_raw"], R1["w_hi"], R1["w_lo"]))
                nc.gpsimd.tensor_tensor(hi, raw, one(KC * D), ALU.mult).then_inc(s_l1_tmp, 1)
                pool.wait_ge(s_l1_tmp, w + 1)
                nc.gpsimd.tensor_tensor(lo, raw, f(hi), ALU.subtract).then_inc(s_l1_w, 1)
            for j in range(2 * BATCH):
                pool.wait_ge(s_rope, 4 * (j + 1))
                if j >= 2:
                    pool.wait_ge(s_feat, j - 1)
                rot, t = L1a["rot"], L1a["rope"]
                nc.gpsimd.tensor_tensor(rot[:, j % 2, 0, :], t[:, 0, :], t[:, 1, :], ALU.subtract).then_inc(s_rot, 1)
                nc.gpsimd.tensor_tensor(rot[:, j % 2, 1, :], t[:, 2, :], t[:, 3, :], ALU.add).then_inc(s_rot, 1)
                if j == 0:
                    pool.wait_ge(s_l1_out_raw, 32)
                    nc.gpsimd.tensor_tensor(R1["pick"].rearrange("p a b c -> p (a b c)"),
                                            pick_raw.rearrange("p a b c -> p (a b c)"), one(16 * P),
                                            ALU.mult).then_inc(s_pick1, 1)
                    pool.wait_ge(s_pick1, 1)
                    nc.gpsimd.memset(L1a["values"].rearrange("p s k h c -> p (s k h) c")[:, :, DH1:C], 1.0).then_inc(s_ones, 1)
            pool.wait_ge(s_rot, 4 * BATCH)
            pool.wait_ge(s_lo1, 2 * BATCH)
            nc.gpsimd.memset(L1b["head_values"], 0.0).then_inc(s_ones, 1)

        def l1_tensor_project(pe):
            pe.wait_ge(s_xnl, 8)

            def three(out, left, right, k0=True):
                terms = [(l, r) for l, r in ((left[0], right[0]), (left[0], right[1]), (left[1], right[0]))]
                k = 0
                for l, r in terms:
                    for c in range(KC):
                        mm = nc.tensor.matmul(out, l(c), r(c), start=(k == 0), stop=(k == 2 * KC + 1))
                        k += 1
                return mm

            def turn_keys(b):
                pe.wait_ge(s_feat, 2 * b + 2)
                if b:
                    pe.wait_ge(s_k_rows, 2)
                for tt in range(QT):
                    for m in range(KC):
                        mm = nc.tensor.transpose(bank[6 + tt // 2][:, ((tt % 2) * KC + m) * P:((tt % 2) * KC + m + 1) * P],
                                                 L1a["k_feat"][:, m, tt * P:(tt + 1) * P], ident[:, :])
                    if tt % 2:
                        mm.then_inc(s_kT, 1)

            for j in range(2 * BATCH):
                b, w = j // 2, j % 2
                half = slice(b * SEQ, (b + 1) * SEQ)
                if j < 2:
                    pe.wait_ge(s_l1_w, j + 1)
                if j >= 2:
                    pe.wait_ge(s_rope, 4 * (j - 1))
                for m in range(KC):
                    mm = three(bank[2 * (j % 2) + m][:, :],
                               [lambda c, v=v, m=m: v[:, w, c, m * P:(m + 1) * P] for v in (R1["w_hi"], R1["w_lo"])],
                               [lambda c, v=v: v[:, c, half] for v in (xnT_hi, xnT_lo)])
                mm.then_inc(s_proj1, 1)
                if j == 0:
                    pe.wait_ge(s_l1_w, 3)
                for t in (2 * j, 2 * j + 1):
                    if j >= 2:
                        pe.wait_ge(s_values, 2 * (j - 1))
                    mm = three(bank[4 + j % 2][:, (t % 2) * D:(t % 2 + 1) * D],
                               [lambda c, v=v: v[:, c, t * P:(t + 1) * P] for v in (xnT_hi, xnT_lo)],
                               [lambda c, v=v: v[:, 2, c, :] for v in (R1["w_hi"], R1["w_lo"])])
                mm.then_inc(s_v1, 1)
                if j == 3:
                    turn_keys(0)
            turn_keys(1)
            pe.wait_ge(s_values, NT)
            pe.wait_ge(s_ones, 1)
            pe.wait_ge(s_k_rows, 4)
            pe.wait_ge(s_rope, 16)
            for st in range(STEPS):
                b, m = st // KC, st % KC
                for kt in range(QT):
                    mm = nc.tensor.matmul(bank[st][:, 0:HM * C], L1a["k_rows"][:, QT * b + kt, m * P:(m + 1) * P],
                                          L1a["values"][:, st, kt, :, :].rearrange("p h c -> p (h c)"),
                                          start=(kt == 0), stop=(kt == QT - 1))
                mm.then_inc(s_mem_ps, 1)

        def l1_scalar_project(act):
            def copy_values(j):
                act.wait_ge(s_v1, j + 1)
                for t in (2 * j, 2 * j + 1):
                    b, kt = t // QT, t % QT
                    nc.scalar.activation(L1a["values"][:, KC * b:KC * (b + 1), kt, :, 0:DH1],
                                         bank[4 + j % 2][:, (t % 2) * D:(t % 2 + 1) * D]
                                         .rearrange("p (m h d) -> p m h d", m=KC, h=HM), ACT.Identity).then_inc(s_values, 1)

            def copy_keys(b):
                for r in range(2):
                    act.wait_ge(s_kT, 2 * b + r + 1)
                    nc.scalar.activation(L1a["k_rows"][:, QT * b + 2 * r:QT * b + 2 * r + 2, :],
                                         bank[6 + r][:, :].rearrange("p (t d) -> p t d", t=2),
                                         ACT.Identity).then_inc(s_k_rows, 1)

            act.wait_ge(s_xnh, 8)
            for j in range(2 * BATCH):
                b, w = j // 2, j % 2
                act.wait_ge(s_rot, 2 * (j + 1))
                nc.scalar.activation(R1["qk_hi"][:, w, KC * b:KC * (b + 1), :], L1a["rot"][:, j % 2, :, :],
                                     ACT.Identity).then_inc(s_hi1, 1)
                if j == 0:
                    act.wait_ge(s_ones, 1)
                copy_values(j)
                act.wait_ge(s_min1, j + 1)
                nc.scalar.activation(L1a["low"], L1a["low"], ACT.Exp).then_inc(s_exp1, 1)
            copy_keys(0)
            copy_keys(1)
            nc.scalar.activation(L1a["gate"], L1a["gate"], ACT.Exp, scale=-1.0).then_inc(s_gates, 1)

        def l1_vector_project(dve):
            dve.wait_ge(s_l1_raw, 16 * N_L1)
            for j in range(2 * BATCH):
                b, w = j // 2, j % 2
                dve.wait_ge(s_proj1, j + 1)
                if j:
                    dve.wait_ge(s_rot, 2 * j)
                q0, q1 = bank[2 * (j % 2)][:, :], bank[2 * (j % 2) + 1][:, :]
                for k, (x, y) in enumerate(((q0, "cos"), (q1, "sin"), (q1, "cos"), (q0, "sin"))):
                    nc.vector.tensor_tensor(L1a["rope"][:, k, :], x, L1a[y], ALU.mult).then_inc(s_rope, 1)
                rot = L1a["rot"][:, j % 2, :, :]
                dve.wait_ge(s_rot, 2 * (j + 1))
                if j:
                    dve.wait_ge(s_feat, j)
                nc.vector.tensor_scalar(L1a["low"], rot, 0.0, None, ALU.min).then_inc(s_min1, 1)
                dve.wait_ge(s_hi1, j + 1)
                nc.vector.tensor_tensor(R1["qk_lo"][:, w, KC * b:KC * (b + 1), :], rot,
                                        f(R1["qk_hi"][:, w, KC * b:KC * (b + 1), :]), ALU.subtract).then_inc(s_lo1, 1)
                dve.wait_ge(s_exp1, j + 1)
                if j == 3:
                    dve.wait_ge(s_kT, 2)
                out = L1a["k_feat"] if w else L1a["q_feat"][:, KC * b:KC * (b + 1), :]
                nc.vector.scalar_tensor_tensor(out=out, in0=rot, scalar=0.0, in1=L1a["low"], op0=ALU.max,
                                               op1=ALU.add).then_inc(s_feat, 1)
            for st in range(STEPS):
                dve.wait_ge(s_mem_ps, st + 1)
                nc.vector.tensor_tensor(L1a["memory"][:, st, :, :].rearrange("p h c -> p (h c)"), bank[st][:, 0:HM * C],
                                        L1a["blocks"].rearrange("p h c -> p (h c)"), ALU.mult).then_inc(s_mem, 1)

        LAG_S, LAG_T, LAG_V = 4, 6, 11

        def behind(s, n, lag, first, tail):
            if (first and n < lag) or (tail and lag <= n):
                return None
            return (s, n - lag) if n >= lag else (s - 1, n - lag + TILES)

        def turned(s, n, first, tail):
            if n == 28 and not tail:
                return s, 0
            if n == 12 and not first:
                return s - 1, 1
            return None

        def pairs_tensor(pe, s, n, w):
            pr = n // 8
            if w == 0:
                pe.wait_ge(s_pair_q, 4 * s + pr)
                pe.wait_ge(s_att, 2 * s - (1 if pr < 2 else 0)) if not (isinstance(s, int) and s == 0) else None
            else:
                pe.wait_ge(s_pair_k, 4 * s + pr)
            out = bank[4 + w][:, :]
            nc.tensor.matmul(out, R1["pick"][:, pr, 2 * w, :], R1["qk_hi"][:, w, bass.ds(s, 1), :]
                             .rearrange("p o t -> p (o t)"), start=True, stop=False)
            nc.tensor.matmul(out, R1["pick"][:, pr, 2 * w + 1, :], R1["qk_lo"][:, w, bass.ds(s, 1), :]
                             .rearrange("p o t -> p (o t)"), start=False, stop=True).then_inc(s_sel_k if w else s_sel_q, 1)

        def l1_tensor_slot(pe, s, n, first=False, tail=False):
            if n % 8 == 0 and not tail:
                pairs_tensor(pe, s, n, 0)
                pairs_tensor(pe, s, n, 1)
            at = behind(s, n, LAG_S, first, tail)
            if at:
                ss, t = at
                h, i = t // QT, t % QT
                if t % 8 == 0:
                    pe.wait_ge(s_pair_q, 4 * ss + t // 8 + 1)
                    pe.wait_ge(s_pair_k, 4 * ss + t // 8 + 1)
                if not (first and t < 2):
                    pe.wait_ge(s_prob1, TILES * ss + t - 1)
                rows = slice(64 * (h % 2), 64 * (h % 2) + 64)
                nc.tensor.matmul(bank[t % 2][:, :], R1["pairs"][rows, 0, h // 2, i * P:(i + 1) * P],
                                 R1["pairs"][rows, 1, h // 2, :], start=True, stop=True).then_inc(s_score1, 1)
            at = behind(s, n, LAG_T, first, tail)
            if at:
                ss, t = at
                pe.wait_ge(s_prob1, TILES * ss + t + 1)
                if not (first and t < 2):
                    pe.wait_ge(s_pT_odd if t % 2 else s_pT_even, TILES // 2 * ss + t // 2)
                for kt in range(QT):
                    mm = nc.tensor.transpose(bank[2 + t % 2][:, kt * P:(kt + 1) * P],
                                             L1b["prob"][:, t % 2, kt * P:(kt + 1) * P], ident[:, :])
                mm.then_inc(s_pT1, 1)
            at = behind(s, n, LAG_V, first, tail)
            if at:
                ss, t = at
                h, kt = t // QT, t % QT
                if kt == 0:
                    pe.wait_ge(s_pT_even, TILES // 2 * ss + 2 * h + 2)
                    pe.wait_ge(s_pT_odd, TILES // 2 * ss + 2 * h + 2)
                    pe.wait_ge(s_hv, HM * ss + h + 1)
                    if h % 4 == 0 and not first:
                        pe.wait_ge(s_z1, 2 * ss + h // 4 - 1)
                g = h % 4
                nc.tensor.matmul(bank[6 + h // 4][g * VW:(g + 1) * VW, :], L1b["head_values"][:, h, kt, :],
                                 L1b["pT"][:, h % 2, kt, :], start=(kt == 0), stop=(kt == QT - 1)).then_inc(s_pv1, 1)
            at = turned(s, n, first, tail)
            if at:
                ss, g = at
                pe.wait_ge(s_z1, 2 * ss + g + 1)
                pe.wait_ge(s_pair_q, 4 * ss + 4 if g == 0 else 4 * ss + (4 if tail else 6))
                for i in range(QT):
                    mm = nc.tensor.transpose(bank[4][:, i * P:(i + 1) * P], L1b["z"][:, i * P:(i + 1) * P], ident[:, :])
                mm.then_inc(s_zT1, 1)

        def l1_scalar_slot(act, s, n, first=False, tail=False):
            if n % 8 == 0 and not tail:
                pr = n // 8
                act.wait_ge(s_sel_q, 4 * s + pr + 1)
                if not first:
                    act.wait_ge(s_score1, TILES * (s - 1) + 8 * (pr + 1))
                nc.scalar.activation(R1["pairs"][:, 0, pr, :], bank[4][:, :], ACT.Identity).then_inc(s_pair_q, 1)
            at = behind(s, n, LAG_S, first, tail)
            if at:
                ss, t = at
                act.wait_ge(s_max1, TILES * ss + t + 1)
                if not (first and t < 2):
                    act.wait_ge(s_pT1, TILES * ss + t - 1)
                nc.scalar.activation(L1b["prob"][:, t % 2, :], bank[t % 2][:, :], ACT.Exp,
                                     bias=neg_max1[:, t % 4:t % 4 + 1]).then_inc(s_prob1, 1)
            at = behind(s, n, LAG_T, first, tail)
            if at and at[1] % 2:
                ss, t = at
                turned_out(act, nc.scalar, ss, t, first)
            at = behind(s, n, LAG_V, first, tail)
            if at and at[1] % 16 == 15:
                ss, t = at
                act.wait_ge(s_pv1, TILES * ss + t + 1)
                if not (first and t < 16):
                    act.wait_ge(s_zT1, 2 * ss + t // 16)
                nc.scalar.activation(L1b["z"], bank[6 + t // 16][:, :], ACT.Identity).then_inc(s_z1, 1)

        def turned_out(eng, ops, ss, t, first):
            h, i = t // QT, t % QT
            eng.wait_ge(s_pT1, TILES * ss + t + 1)
            if not first or h >= 2:
                eng.wait_ge(s_pv1, TILES * ss + QT * (h - 1))
            out = L1b["pT"][:, h % 2, :, i * P:(i + 1) * P]
            src = bank[2 + t % 2][:, :].rearrange("p (k q) -> p k q", k=QT)
            if ops is nc.scalar:
                ops.activation(out, src, ACT.Identity).then_inc(s_pT_odd, 1)
            else:
                ops.tensor_copy(out, src).then_inc(s_pT_even, 1)

        def l1_vector_slot(dve, s, n, first=False, tail=False):
            if n % 8 == 0 and not tail:
                pr = n // 8
                dve.wait_ge(s_sel_k, 4 * s + pr + 1)
                if not first:
                    dve.wait_ge(s_score1, TILES * (s - 1) + 8 * (pr + 1))
                nc.vector.tensor_copy(R1["pairs"][:, 1, pr, :], bank[5][:, :]).then_inc(s_pair_k, 1)
            if n % QT == 2 and not tail:
                h = n // QT
                if not first:
                    dve.wait_ge(s_pv1, TILES * (s - 1) + QT * (h + 1))
                nc.vector.tensor_scalar(L1b["head_values"][:, h, :, 0:C],
                                        L1a["values"][:, bass.ds(s, 1), :, h, :].rearrange("p o k c -> p (o k) c"),
                                        1.0, None, ALU.mult).then_inc(s_hv, 1)
            at = behind(s, n, LAG_S, first, tail)
            if at:
                ss, t = at
                dve.wait_ge(s_score1, TILES * ss + t + 1)
                if not (first and t < 4):
                    dve.wait_ge(s_prob1, TILES * ss + t - 3)
                nc.vector.tensor_reduce(neg_max1[:, t % 4:t % 4 + 1], bank[t % 2][:, :], X_AXIS, ALU.max,
                                        negate=True).then_inc(s_max1, 1)
            at = behind(s, n, LAG_T, first, tail)
            if at and at[1] % 2 == 0:
                ss, t = at
                turned_out(dve, nc.vector, ss, t, first)
            at = turned(s, n, first, tail)
            if at:
                ss, g = at
                dve.wait_ge(s_zT1, 2 * ss + g + 1)
                for i in range(QT):
                    ins = nc.vector.tensor_scalar(
                        L1a["attended"][:, bass.ds(ss, 1), i, 4 * g:4 * g + 4, :].rearrange("p o h c -> p (o h) c"),
                        bank[4][:, i * P:(i + 1) * P].rearrange("p (h c) -> p h c", h=4)[:, :, 0:C],
                        1.0, None, ALU.mult)
                ins.then_inc(s_att, 1)

        def l1_run(eng, slot):
            for n in range(TILES):
                slot(eng, 0, n, first=True)
            with eng.Fori(1, STEPS) as s:
                for n in range(TILES):
                    slot(eng, s, n)
            for n in range(13):
                slot(eng, STEPS, n, tail=True)

        def mix_tensor(pe):
            pe.wait_ge(s_mem, STEPS)
            pe.wait_ge(s_l1_out_raw, 32)

            def turn(r):
                pe.wait_ge(s_mix, 2 * r + 2)
                if r >= 2:
                    pe.wait_ge(s_mixT_sb, r - 1)
                for c in range(KC):
                    for t in range(2):
                        mm = nc.tensor.transpose(bank[4 + r % 2][:, (2 * c + t) * P:(2 * c + t + 1) * P],
                                                 L1c["out"][:, t, 0, c * P:(c + 1) * P], ident[:, :])
                mm.then_inc(s_mixT, 1)

            def output(r):
                pe.wait_ge(s_mixT_sb, r + 1)
                if r >= 2:
                    pe.wait_ge(s_att_added, r - 1)
                for t in (2 * r, 2 * r + 1):
                    for c in range(KC):
                        mm = nc.tensor.matmul(bank[6 + r % 2][:, (t % 2) * D:(t % 2 + 1) * D],
                                              L1c["mixed"][:, c, t * P:(t + 1) * P], L1a["w_out"][:, c, :],
                                              start=(c == 0), stop=(c == KC - 1))
                mm.then_inc(s_wo1, 1)

            for t in range(NT):
                b, i = t // QT, t % QT
                if t >= 4:
                    pe.wait_ge(s_mix_a, t - 3)
                for m in range(KC):
                    mm = nc.tensor.matmul(bank[t % 4][:, m * HM * C:(m + 1) * HM * C],
                                          L1a["q_feat"][:, KC * b + m, i * P:(i + 1) * P],
                                          L1a["memory"][:, KC * b + m, :, :].rearrange("p h c -> p (h c)"),
                                          start=True, stop=True)
                mm.then_inc(s_memout, 1)
                if t >= 3 and t % 2:
                    turn((t - 3) // 2)
                if t >= 5 and t % 2:
                    output((t - 5) // 2)
            turn(3)
            output(2)
            output(3)

        def mix_scalar(act):
            for r in range(NT // 2):
                act.wait_ge(s_mixT, r + 1)
                nc.scalar.activation(L1c["mixed"][:, :, 2 * P * r:2 * P * (r + 1)],
                                     bank[4 + r % 2][:, :].rearrange("p (c t) -> p c t", c=KC),
                                     ACT.Identity).then_inc(s_mixT_sb, 1)

        def mix_vector(dve):
            done = [0]

            def step(ins):
                done[0] += 1
                ins.then_inc(s_inv1, 1)
                dve.wait_ge(s_inv1, done[0])

            gate, gates = L1a["gate"], L1c["gates"]
            dve.wait_ge(s_gates, 1)
            dve.wait_ge(s_pv1, STEPS * TILES)
            dve.wait_ge(s_att, 2 * STEPS)
            step(nc.vector.tensor_scalar(gate, gate, 1.0, None, ALU.add))
            step(nc.vector.reciprocal(gates[:, 0, :], gate))
            step(nc.vector.tensor_scalar(gates[:, 1, :], gates[:, 0, :], -1.0, 1.0, ALU.mult, ALU.add))
            for t in range(NT):
                b, i = t // QT, t % QT
                mem = bank[t % 4][:, 0:HEADS1 * C].rearrange("p (m h c) -> p m h c", m=KC, h=HM)
                att = L1a["attended"][:, KC * b:KC * (b + 1), i, :, :]
                inv = L1c["inv"][:, t % 2, :, :]
                dve.wait_ge(s_memout, t + 1)
                step(nc.vector.reciprocal(inv[:, 0, :].rearrange("p (m h) -> p m h", m=KC), mem[:, :, :, DH1]))
                step(nc.vector.reciprocal(inv[:, 1, :].rearrange("p (m h) -> p m h", m=KC), att[:, :, :, DH1]))
                step(nc.vector.tensor_tensor(inv, inv, gates, ALU.mult))
                if t >= 2:
                    dve.wait_ge(s_mixT, t // 2)
                out = L1c["out"][:, t % 2, :, :].rearrange("p w (m h d) -> p w m h d", m=KC, h=HM)
                for w, src in ((0, mem), (1, att)):
                    scale = inv[:, w, :].rearrange("p (m h o) -> p m h o", m=KC, o=1).broadcast_to((P, KC, HM, DH1))
                    ins = nc.vector.tensor_tensor(out[:, w, :, :, :], src[:, :, :, 0:DH1], scale, ALU.mult)
                    ins.then_inc(s_mix_a if w == 0 else s_mix_b, 1)
                dve.wait_ge(s_mix_a, t + 1)
                dve.wait_ge(s_mix_b, t + 1)
                rows = L1c["out"][:, t % 2, :, :]
                nc.vector.tensor_tensor(rows[:, 0, :], rows[:, 0, :], rows[:, 1, :], ALU.add).then_inc(s_mix, 1)
                if t >= 7:
                    added(0)
            for r in range(1, NT // 2):
                added(r)

        def added(r):
            nc.vector.wait_ge(s_wo1, r + 1)
            rows = X[:, 2 * r:2 * r + 2, :]
            nc.vector.tensor_tensor(rows, bank[6 + r % 2][:, :].rearrange("p (t d) -> p t d", t=2), rows,
                                    ALU.add).then_inc(s_att_added, 1)

        F_FREE = 2048 + 1536 + 1024 + 136 + 16 + 512 + 2048 + 1024 + 1024 + 544 + 2048
        B1 = layout(farena, FWORDS, chunk=(3, KC * P), router=(KC, E1), pick=(FC, P))
        D1 = layout(farena, FWORDS, skip=(F_FREE,), silu=(2, SEQ), prod=(2, SEQ), hid=(2, SEQ), logit=(NT, 16),
                    found=(NT, 8), wanted=(NT, 8), left=(NT, 16), w=(NT, E1), total=(NT,))
        R1_END = 2 * 3 * KC * D + 2 * 2 * STEPS * SEQ + 16 * P + 2 * 4 * SEQ
        M1 = layout(rarena, RWORDS, skip=(R1_END,), chunk_hi=(3, KC * P), chunk_lo=(3, KC * P), router_hi=(KC, E1),
                    router_lo=(KC, E1), pick=(P,), w_split=(NT, 2 * E1), wT=(TOKENS,), hid_hi=(2, SEQ), hid_lo=(2, SEQ))
        (s_m1_raw, s_m1_tmp, s_m1_router, s_logit1, s_lg, s_route1, s_ex1, s_exd1, s_split1, s_wT1_ps, s_wT1, s_pick2, s_gate1,
         s_up1, s_silu1, s_prod1, s_hid1, s_hid1_hi, s_hid1_lo, s_back1) = (sem(n) for n in (
             "s_m1_raw s_m1_tmp s_m1_router s_logit1 s_lg s_route1 s_ex1 s_exd1 s_split1 s_wT1_ps s_wT1 s_pick2 s_gate1 "
             "s_up1 s_silu1 s_prod1 s_hid1 s_hid1_hi s_hid1_lo s_back1").split())
        s_chunk_raw = [sem(f"s_chunk_raw{k}") for k in range(3)]
        s_chunk = [sem(f"s_chunk{k}") for k in range(3)]
        s_y1 = [sem(f"s_y1_{r}") for r in range(4)]
        GATE, UP, DOWN = range(3)
        ABSENT, TAKEN = -3.0e38, -3.2e38

        def chunk_load(sp, k, c, first=False):
            if not first:
                sp.wait_ge(s_chunk[k], c)
            sp.dma_start(B1["chunk"][:, k, :], a["m1_chunk"][:, bass.ds(c, 1), k, :]
                         .rearrange("p o n -> p (o n)")).then_inc(s_chunk_raw[k], 16)

        def mix1_loads(sp):
            sp.wait_ge(s_pv1, STEPS * TILES)
            sp.wait_ge(s_att, 2 * STEPS)
            sp.dma_start(B1["router"], a["m1_router"]).then_inc(s_m1_raw, 16)
            sp.dma_start(B1["pick"][0:2 * E1, :, :], a["m1_pick"]).then_inc(s_m1_raw, 16)
            for k in range(3):
                chunk_load(sp, k, 0, first=True)
            with sp.Fori(1, FC) as c:
                for k in range(3):
                    chunk_load(sp, k, c)

        def split_chunk(pool, k, c, used, first=False):
            pool.wait_ge(s_chunk_raw[k], 16 * (c + 1))
            if not first:
                pool.wait_ge(used, 2 * c)
            nc.gpsimd.tensor_tensor(M1["chunk_hi"][:, k, :], B1["chunk"][:, k, :], one(KC * P),
                                    ALU.mult).then_inc(s_m1_tmp, 1)
            pool.wait_ge(s_m1_tmp, 3 * c + k + 1)
            nc.gpsimd.tensor_tensor(M1["chunk_lo"][:, k, :], B1["chunk"][:, k, :], f(M1["chunk_hi"][:, k, :]),
                                    ALU.subtract).then_inc(s_chunk[k], 1)

        def mix1_pool(pool):
            pool.wait_ge(s_m1_raw, 32)
            flat = "p c e -> p (c e)"
            nc.gpsimd.tensor_tensor(M1["router_hi"].rearrange(flat), B1["router"].rearrange(flat), one(KC * E1),
                                    ALU.mult).then_inc(s_m1_router, 1)
            pool.wait_ge(s_m1_router, 1)
            nc.gpsimd.tensor_tensor(M1["router_lo"].rearrange(flat), B1["router"].rearrange(flat),
                                    f(M1["router_hi"].rearrange(flat)), ALU.subtract).then_inc(s_m1_router, 1)
            for k in range(3):
                split_chunk(pool, k, 0, None, first=True)

            def hid_lo(n, x, first=False):
                pool.wait_ge(s_hid1_hi, n + 1)
                if not first:
                    pool.wait_ge(s_back1, n - 1)
                nc.gpsimd.tensor_tensor(M1["hid_lo"][:, x, :], D1["hid"][:, x, :], f(M1["hid_hi"][:, x, :]),
                                        ALU.subtract).then_inc(s_hid1_lo, 1)

            def chunk(c, first=False, last=False):
                hid_lo(2 * c, 0, first)
                if not last:
                    split_chunk(pool, GATE, c + 1, s_gate1)
                    split_chunk(pool, UP, c + 1, s_up1)
                hid_lo(2 * c + 1, 1, first)
                if not last:
                    split_chunk(pool, DOWN, c + 1, s_back1)

            chunk(0, first=True)
            with pool.Fori(1, FC - 1) as c:
                chunk(c)
            chunk(FC - 1, last=True)

        def mix1_tensor(pe):
            pe.wait_ge(s_m1_router, 2)
            pe.wait_ge(s_mix_a, NT)
            for t in range(NT):
                k = 0
                for xs, ws in ((xnT_hi, "router_hi"), (xnT_hi, "router_lo"), (xnT_lo, "router_hi")):
                    for c in range(KC):
                        mm = nc.tensor.matmul(bank[2][:, t * E1:(t + 1) * E1], xs[:, c, t * P:(t + 1) * P],
                                              M1[ws][:, c, :], start=(k == 0), stop=(k == 2 * KC + 1))
                        k += 1
            mm.then_inc(s_logit1, 1)

            def terms(left, right):
                return ((left[0], right[0]), (left[0], right[1]), (left[1], right[0]))

            def projection(out, k, x):
                half = slice(x * SEQ, (x + 1) * SEQ)
                m = 0
                for w, v in terms((M1["chunk_hi"], M1["chunk_lo"]), (xnT_hi, xnT_lo)):
                    for c in range(KC):
                        mm = nc.tensor.matmul(out, w[:, k, c * P:(c + 1) * P], v[:, c, half], start=(m == 0),
                                              stop=(m == 2 * KC + 1))
                        m += 1
                return mm

            def gate_up(n, x, c, first=False):
                if x == 0:
                    pe.wait_ge(s_chunk[GATE], c + 1)
                if not first:
                    pe.wait_ge(s_silu1, n - 1)
                projection(bank[3 if x else 0][:, :], GATE, x).then_inc(s_gate1, 1)
                if x == 0:
                    pe.wait_ge(s_chunk[UP], c + 1)
                if not (first and x == 0):
                    pe.wait_ge(s_prod1, n)
                projection(bank[1][:, :], UP, x).then_inc(s_up1, 1)

            def weights(n, x, c, first=False):
                pe.wait_ge(s_pick2, c + 1)
                if not (first and x == 0):
                    pe.wait_ge(s_hid1, n)
                nc.tensor.matmul(bank[2][:, :], M1["pick"][0:2 * E1, :], M1["wT"][0:2 * E1, x * SEQ:(x + 1) * SEQ],
                                 start=True, stop=True).then_inc(s_ex1, 1)

            def back(n, x, c, last=False):
                pe.wait_ge(s_hid1_lo, n + 1)
                if x == 0:
                    pe.wait_ge(s_chunk[DOWN], c + 1)
                for i in range(QT):
                    r = 2 * x + i // 2
                    out = bank[4 + r][:, (i % 2) * D:(i % 2 + 1) * D]
                    for m, (h, w) in enumerate(terms((M1["hid_hi"], M1["hid_lo"]), (M1["chunk_hi"], M1["chunk_lo"]))):
                        mm = nc.tensor.matmul(out, h[:, x, i * P:(i + 1) * P], w[:, DOWN, :], start=False,
                                              stop=last and m == 2, skip_group_check=True)
                mm.then_inc(s_back1, 1)

            gate_up(0, 0, 0, first=True)
            pe.wait_ge(s_att_added, 4)
            for r in range(4):
                nc.tensor.matmul(bank[4 + r][:, :], zeros_bf[:, 0:P], zeros_bf[:, 0:SEQ], start=True, stop=False,
                                 skip_group_check=True)
            pe.wait_ge(s_split1, 2)
            pe.wait_ge(s_lg, 1)
            for t in range(NT):
                mm = nc.tensor.transpose(bank[2 if t < 4 else 3][0:2 * E1, (t % 4) * P:(t % 4 + 1) * P],
                                         f(M1["w_split"][:, t, :]), ident[:, :])
                if t % 4 == 3:
                    mm.then_inc(s_wT1_ps, 1)
            pe.wait_ge(s_wT1, 2)
            weights(0, 0, 0, first=True)
            gate_up(1, 1, 0, first=True)
            weights(1, 1, 0, first=True)
            back(0, 0, 0)
            with pe.Fori(1, FC) as c:
                gate_up(2 * c, 0, c)
                weights(2 * c, 0, c)
                back(2 * c - 1, 1, c - 1)
                gate_up(2 * c + 1, 1, c)
                weights(2 * c + 1, 1, c)
                back(2 * c, 0, c)
            back(2 * FC - 1, 1, FC - 1)

        def mix1_scalar(act):
            def silu(n, x, first=False):
                act.wait_ge(s_gate1, n + 1)
                if not first:
                    act.wait_ge(s_prod1, n - 1)
                nc.scalar.activation(D1["silu"][:, x, :], bank[3 if x else 0][:, :], ACT.Silu).then_inc(s_silu1, 1)

            def hid_hi(n, x, first=False):
                act.wait_ge(s_hid1, n + 1)
                if not first:
                    act.wait_ge(s_back1, n - 1)
                nc.scalar.activation(M1["hid_hi"][:, x, :], D1["hid"][:, x, :], ACT.Identity).then_inc(s_hid1_hi, 1)

            act.wait_ge(s_exd1, 1)
            nc.scalar.activation(D1["w"], D1["w"], ACT.Exp).then_inc(s_exd1, 1)
            silu(0, 0, first=True)
            for x in range(2):
                act.wait_ge(s_wT1_ps, x + 1)
                nc.scalar.activation(M1["wT"][0:2 * E1, x * SEQ:(x + 1) * SEQ], bank[2 + x][0:2 * E1, :],
                                     ACT.Identity).then_inc(s_wT1, 1)
            silu(1, 1, first=True)
            hid_hi(0, 0, first=True)
            hid_hi(1, 1, first=True)
            with act.Fori(1, FC) as c:
                for x in range(2):
                    silu(2 * c + x, x)
                    hid_hi(2 * c + x, x)

        def mix1_vector(dve):
            done = [0]

            def step(ins):
                done[0] += 1
                ins.then_inc(s_route1, 1)
                dve.wait_ge(s_route1, done[0])

            logit, found, wanted, left, w, total = (D1[n] for n in ("logit", "found", "wanted", "left", "w", "total"))

            def wide(v):
                return v.broadcast_to((P, NT, E1))

            step(nc.vector.memset(logit[:, :, E1:16], ABSENT))
            step(nc.vector.memset(wanted, ABSENT))
            dve.wait_ge(s_logit1, 1)
            nc.vector.tensor_copy(logit[:, :, 0:E1], bank[2][:, 0:NT * E1].rearrange("p (t e) -> p t e", t=NT)).then_inc(s_lg, 1)
            dve.wait_ge(s_lg, 1)
            for t in range(NT):
                step(nc.vector.max(found[:, t, :], logit[:, t, 0:E1]))
            step(nc.vector.tensor_copy(wanted[:, :, 0:2], found[:, :, 0:2]))
            for t in range(NT):
                step(nc.vector.match_replace(left[:, t, 0:14], wanted[:, t, :], logit[:, t, 0:14], TAKEN))
            dve.wait_ge(s_exp1, 2 * BATCH)
            nc.vector.tensor_tensor(w, logit[:, :, 0:E1], wide(found[:, :, 0:1]), ALU.subtract).then_inc(s_exd1, 1)
            step(nc.vector.tensor_tensor(left[:, :, 0:E1], left[:, :, 0:E1], logit[:, :, 0:E1], ALU.not_equal))
            dve.wait_ge(s_exd1, 2)
            step(nc.vector.tensor_tensor(w, w, left[:, :, 0:E1], ALU.mult))
            step(nc.vector.tensor_reduce(total, w, X_AXIS, ALU.add))
            step(nc.vector.reciprocal(total, total))
            step(nc.vector.tensor_tensor(w, w, wide(total.rearrange("p (t o) -> p t o", o=1)), ALU.mult))
            nc.vector.tensor_copy(M1["w_split"][:, :, 0:E1], w).then_inc(s_split1, 1)
            dve.wait_ge(s_split1, 1)
            nc.vector.tensor_tensor(M1["w_split"][:, :, E1:2 * E1], w, f(M1["w_split"][:, :, 0:E1]),
                                    ALU.subtract).then_inc(s_split1, 1)

            def pick(c):
                nc.vector.tensor_scalar(M1["pick"][0:2 * E1, :],
                                        B1["pick"][0:2 * E1, bass.ds(c, 1), :].rearrange("p o n -> p (o n)"),
                                        1.0, None, ALU.mult).then_inc(s_pick2, 1)

            def hidden(n, x, first=False):
                dve.wait_ge(s_silu1, n + 1)
                dve.wait_ge(s_up1, n + 1)
                if not first:
                    dve.wait_ge(s_hid1, n - 1)
                nc.vector.tensor_tensor(D1["prod"][:, x, :], bank[1][:, :], D1["silu"][:, x, :], ALU.mult).then_inc(s_prod1, 1)
                dve.wait_ge(s_ex1, n + 1)
                dve.wait_ge(s_prod1, n + 1)
                if not first:
                    dve.wait_ge(s_hid1_lo, n - 1)
                nc.vector.tensor_tensor(D1["hid"][:, x, :], bank[2][:, :], D1["prod"][:, x, :], ALU.mult).then_inc(s_hid1, 1)

            dve.wait_ge(s_m1_raw, 32)
            pick(0)
            hidden(0, 0, first=True)
            hidden(1, 1, first=True)
            with dve.Fori(1, FC) as c:
                pick(c)
                hidden(2 * c, 0)
                hidden(2 * c + 1, 1)
            for r in range(4):
                dve.wait_ge(s_back1, 2 * FC - 1 + r // 2)
                rows = X[:, 2 * r:2 * r + 2, :]
                nc.vector.tensor_tensor(rows, bank[4 + r][:, :].rearrange("p (t d) -> p t d", t=2), rows,
                                        ALU.add).then_inc(s_y1[r], 1)

        consts = [(ident, "ident"), (mask_neg, "mask_neg"), (ident_bf, "ident_bf"), (bias_qkv, "bias_qkv"),
                  (scale0, "scale0")]
        N_CONST = len(consts) + 1
        s_out = sem("s_out")

        block = ctx.enter_context(nc.Block())

        @block.sync
        def _(sp):
            for i in range(2):
                sp.dma_start(X[:, 4 * i:4 * i + 4, :], a["x"][:, 4 * i:4 * i + 4, :]).then_inc(s_x[i], 16)
            for dst, name in consts:
                sp.dma_start(dst[:], a[name]).then_inc(s_const, 16)
            sp.dma_start(bo_row[:], a["b_o"].broadcast_to((P, D))).then_inc(s_const, 16)
            attn_loads(sp, 0, first=True)
            with sp.Fori(1, GROUPS) as g:
                attn_loads(sp, g)
            mix0_loads(sp)
            for e in range(2):
                expert_loads(sp, e, e, first=True)
            with sp.Fori(1, E0 // 2) as k:
                for par in range(2):
                    expert_loads(sp, 2 * k + par, par)
            l1_loads(sp)
            mix1_loads(sp)
            for r in range(4):
                sp.wait_ge(s_y1[r], 1)
                sp.dma_start(a["out"][:, 2 * r:2 * r + 2, :], X[:, 2 * r:2 * r + 2, :]).then_inc(s_out, 16)
            sp.wait_ge(s_out, 64)

        @block.tensor
        def _(pe):
            norm_tensor(pe, 0)
            pe.wait_ge(s_xnl, 4)
            for u in range(UNITS):
                attn_tensor_slot(pe, 0, u, first=True)
            with pe.Fori(1, GROUPS) as g:
                for u in range(UNITS):
                    attn_tensor_slot(pe, g, u)
            for u in range(FINISHED):
                attn_tensor_slot(pe, GROUPS, u, tail=True)
            mix0_tensor(pe)
            norm_tensor(pe, 1)
            l1_tensor_project(pe)
            l1_run(pe, l1_tensor_slot)
            mix_tensor(pe)
            mix1_tensor(pe)

        @block.scalar
        def _(act):
            norm_scalar(act, 0)
            act.wait_ge(s_bk, 1)
            for u in range(UNITS):
                attn_scalar_slot(act, 0, u, first=True)
            with act.Fori(1, GROUPS) as g:
                for u in range(UNITS):
                    attn_scalar_slot(act, g, u)
            for u in range(FINISHED):
                attn_scalar_slot(act, GROUPS, u, tail=True)
            mix0_scalar(act)
            norm_scalar(act, 1)
            l1_scalar_project(act)
            l1_run(act, l1_scalar_slot)
            mix_scalar(act)
            mix1_scalar(act)

        @block.vector
        def _(dve):
            norm_vector(dve, 0)
            dve.wait_ge(s_const, 16 * N_CONST)
            nc.vector.tensor_scalar(bias_qkv[:, 1, :], bias_qkv[:, 1, :], scale0[:, 0:1], None, ALU.mult).then_inc(s_bk, 1)
            dve.wait_ge(s_bk, 1)
            nc.vector.tensor_copy(bias_now[:, 0, :], bias_qkv[:, :, 0]).then_inc(s_bias, 1)
            for u in range(UNITS):
                attn_vector_slot(dve, 0, u, first=True)
            with dve.Fori(1, GROUPS) as g:
                for u in range(UNITS):
                    attn_vector_slot(dve, g, u)
            for u in range(FINISHED):
                attn_vector_slot(dve, GROUPS, u, tail=True)
            mix0_vector(dve)
            dve.wait_ge(s_out0_added, 4)
            norm_vector(dve, 1)
            l1_vector_project(dve)
            dve.wait_ge(s_ones, 2)
            l1_run(dve, l1_vector_slot)
            mix_vector(dve)
            mix1_vector(dve)

        @block.gpsimd
        def _(pool):
            pool.wait_ge(s_const, 16 * N_CONST)
            attn_pool_early(pool, 0, first=True)
            with pool.Fori(0, GROUPS - 1) as g:
                attn_pool_late(pool, g)
                attn_pool_early(pool, g + 1)
            attn_pool_late(pool, GROUPS - 1, ahead=False)
            normalise(pool, GROUPS, 0)
            mix0_pool(pool)
            l1_pool_project(pool)
            mix1_pool(pool)


def kernel(**inputs):
    import numpy as np
    import concourse.bacc as bacc
    from concourse.bass_utils import run_bass_kernel_spmd

    def get(name):
        return np.asarray(inputs[name])

    bf16 = mybir.dt.np(BF16)
    wq, wk = get("L0_attn_W_Q"), get("L0_attn_W_K")
    wqk = np.stack([wq, wk], 1).reshape(HEADS0, 2, KC, P, DH0).transpose(0, 3, 1, 2, 4)
    wv = get("L0_attn_W_V").reshape(GROUPS, GROUP, KC, P, DH0).transpose(0, 3, 2, 1, 4)
    wo = get("L0_attn_W_O").reshape(GROUPS, GROUP, DH0, D).transpose(0, 2, 1, 3)
    bias = np.stack([get("L0_attn_b_Q"), get("L0_attn_b_K"), get("L0_attn_b_V")]).transpose(2, 0, 1)
    arrays = {
        "x": get("L0_attn_x").reshape(NT, P, D).transpose(1, 0, 2),
        "w_qk": wqk.reshape(HEADS0, P, 2 * KC * DH0),
        "w_v": wv.reshape(GROUPS, P, KC * GROUP * DH0),
        "w_o": wo.reshape(GROUPS, P, GROUP * D),
        "bias_qkv": bias,
        "b_o": get("L0_attn_b_O").reshape(1, D),
        "ident": np.eye(P, dtype=np.float32),
        "ident_bf": np.eye(P, dtype=np.float32).astype(bf16),
        "mask_neg": np.triu(np.full((P, P), MASKED, np.float32), 1).astype(bf16),
        "scale0": np.tile(np.array([[DH0 ** -0.5, 1.0]], np.float32), (P, 1)),
    }
    arrays |= {
        "m0_router": get("L0_ffn_Wg").T.reshape(KC, P, E0).transpose(1, 0, 2),
        "m0_down": get("L0_ffn_Wdown").T.reshape(KC, P, LAT).transpose(1, 0, 2),
        "m0_gate_up": np.stack([get("L0_ffn_sw1"), get("L0_ffn_swg")]).transpose(0, 2, 1)
        .reshape(2, KC, P, HID).transpose(2, 0, 1, 3),
        "m0_shared_out": get("L0_ffn_sw2").T,
        "m0_lat_up": get("L0_ffn_Wup").T,
        "m0_pick": np.tile(np.repeat(np.eye(E0, dtype=np.float32)[:, :, None], P, 2), (2, 1, 1)),
        "m0_bias": get("L0_ffn_biases").reshape(1, E0),
        "m0_expert": np.stack([get("L0_ffn_rw1"), get("L0_ffn_rwg")], 1).transpose(3, 0, 1, 2).reshape(LAT, E0, 2 * HID),
        "m0_expert_out": get("L0_ffn_rw2").transpose(2, 0, 1),
    }
    def rows(w):
        return w.reshape(KC, P, -1).transpose(1, 0, 2)

    freq = (np.float32(1.0) / np.float32(10000.0) ** (np.arange(0, D, 2, dtype=np.float32) / np.float32(D))).astype(np.float32)
    angle = (np.arange(SEQ, dtype=np.float32)[:, None] * freq[None, :]).astype(np.float32).T
    pick = np.zeros((P, 4, 4, P), np.float32)
    for pr in range(4):
        for kind, parts in enumerate(((0, 1), (2, 3), (0, 2), (1, 3))):
            for j in range(2):
                for part in parts:
                    for d in range(DH1):
                        pick[DH1 * (2 * pr + j) + d, pr, kind, 64 * j + DH1 * part + d] = DH1 ** -0.5 if kind < 2 else 1.0
    arrays |= {
        "l1_w": np.stack([rows(get(n).T) for n in ("L1_attn_Wq", "L1_attn_Wk", "L1_attn_Wv")], 1),
        "l1_cos": np.cos(angle),
        "l1_sin": np.sin(angle),
        "l1_blocks": np.repeat(np.repeat(np.eye(HM, dtype=np.float32), DH1, 0)[:, :, None], DH1 + 1, 2),
        "l1_gate": get("L1_attn_gate").reshape(1, HEADS1),
        "l1_w_out": rows(get("L1_attn_Wo").T),
        "l1_pick": pick,
    }
    expert_of = np.repeat(np.eye(E1, dtype=np.float32), F1, 1).reshape(E1, FC, P)
    gate = get("L1_ffn_gate_proj").reshape(FC, P, KC, P).transpose(3, 0, 2, 1)
    up = get("L1_ffn_up_proj").reshape(FC, P, KC, P).transpose(3, 0, 2, 1)
    down = get("L1_ffn_down_proj").transpose(0, 2, 1).reshape(FC, P, D).transpose(1, 0, 2)
    arrays |= {
        "m1_router": rows(get("L1_ffn_gate_w").T),
        "m1_pick": np.tile(expert_of, (2, 1, 1)),
        "m1_chunk": np.stack([gate.reshape(P, FC, KC * P), up.reshape(P, FC, KC * P), down], 2),
    }
    nc = bacc.Bacc("TRN2", target_bir_lowering=False, num_devices=1)
    aps, feed = {}, {}
    for name, v in arrays.items():
        v = np.ascontiguousarray(v)
        feed[f"in_{name}"] = v
        aps[name] = nc.dram_tensor(f"in_{name}", v.shape, mybir.dt.from_np(v.dtype), kind="ExternalInput").ap()
    aps["out"] = nc.dram_tensor("out_x", (P, NT, D), F32, kind="ExternalOutput").ap()
    program(nc, aps)
    r = run_bass_kernel_spmd(nc, [feed], core_ids=[0])
    got = np.asarray(r.results[0]["out_x"])
    return np.ascontiguousarray(got.transpose(1, 0, 2).reshape(BATCH, SEQ, D))
```

```python
from contextlib import ExitStack

import concourse.bass as bass
from concourse import mybir


F32 = mybir.dt.float32
F32R = mybir.dt.float32r
BF16 = mybir.dt.bfloat16
ALU = mybir.AluOpType
ACT = mybir.ActivationFunctionType
X_AXIS = mybir.AxisListType.X

P = 128
D = 256
KC = D // P
BATCH, SEQ = 2, 512
TOKENS = BATCH * SEQ
NT = TOKENS // P
QT = SEQ // P
EPS = 1e-5

HEADS0, DH0 = 16, 128
GROUP = 4
GROUPS = HEADS0 // GROUP
UNITS = BATCH * GROUP
TRI = QT * (QT + 1) // 2 * P
MASKED = -1e5

E0, TOP0, LAT, HID = 16, 8, 64, 128
ROUTE_SCALE = 2.5

HEADS1, DH1 = 16, 16
HM = P // DH1
VW = 32

E1, F1 = 8, 176
FC = E1 * F1 // P


def program(nc, a):
    with ExitStack() as ctx:
        def sb(name, shape, dt):
            return ctx.enter_context(nc.sbuf_tensor(name, shape, dt))

        def sem(name):
            return ctx.enter_context(nc.semaphore(name))

        bank = [ctx.enter_context(nc.psum_tensor(f"bank{i}", [P, 512], F32)) for i in range(8)]

        X = sb("X", [P, NT, D], F32)
        xnT_hi = sb("xnT_hi", [P, KC, TOKENS], F32R)
        xnT_lo = sb("xnT_lo", [P, KC, TOKENS], F32R)
        ident = sb("ident", [P, P], F32)
        small = sb("small", [P, 512], F32)
        bo_row = sb("bo_row", [P, D], F32)

        FWORDS, RWORDS = 18944, 26624
        farena = sb("farena", [P, FWORDS], F32)
        rarena = sb("rarena", [P, RWORDS], F32R)

        def layout(arena, limit, **shapes):
            at, views = 0, {}
            for name, shape in shapes.items():
                n = 1
                for s in shape:
                    n *= s
                v = arena[:, at:at + n]
                if len(shape) == 2:
                    v = v.rearrange("p (a b) -> p a b", a=shape[0])
                elif len(shape) == 3:
                    v = v.rearrange("p (a b c) -> p a b c", a=shape[0], b=shape[1])
                elif len(shape) == 4:
                    v = v.rearrange("p (a b c d) -> p a b c d", a=shape[0], b=shape[1], c=shape[2])
                views[name] = v
                at += n
            assert at <= limit, (at, limit)
            return views

        def f(v):
            return v.bitcast(F32)

        stats = small[:, 0:48].rearrange("p (t s) -> p t s", t=NT)
        mean_var = small[:, 48:64].rearrange("p (t s) -> p t s", t=NT)
        std = small[:, 64:72]
        rstd = small[:, 72:80]
        s_x = [sem(f"s_x{i}") for i in range(2)]
        s_const = sem("s_const")
        s_stats, s_aggr, s_eps, s_std, s_rstd = (sem(n) for n in ("s_stats", "s_aggr", "s_eps", "s_std", "s_rstd"))
        s_xn, s_xnt, s_xnh, s_xnl = (sem(n) for n in ("s_xn", "s_xnt", "s_xnh", "s_xnl"))
        xn = layout(farena, FWORDS, skip=(FWORDS - NT * D,), xn=(NT, D))["xn"]

        def norm_stats(t):
            nc.vector.bn_stats(stats[:, t, :], X[:, t, :]).then_inc(s_stats, 1)

        def norm_vector(dve, n):
            if n == 0:
                for t in range(NT):
                    if t % 4 == 0:
                        dve.wait_ge(s_x[t // 4], 16)
                    norm_stats(t)
            for t in range(NT):
                dve.wait_ge(s_stats, NT * n + t + 1)
                nc.vector.bn_aggr(mean_var[:, t, :], stats[:, t, :]).then_inc(s_aggr, 1)
            dve.wait_ge(s_aggr, NT * (n + 1))
            nc.vector.tensor_scalar(std, mean_var[:, :, 1], EPS, None, ALU.add).then_inc(s_eps, 1)
            dve.wait_ge(s_std, n + 1)
            nc.vector.reciprocal(rstd, std).then_inc(s_rstd, 1)
            dve.wait_ge(s_rstd, n + 1)
            for t in range(NT):
                nc.vector.tensor_scalar(xn[:, t, :], X[:, t, :], mean_var[:, t, 0:1], rstd[:, t:t + 1],
                                        ALU.subtract, ALU.mult).then_inc(s_xn, 1)
            for r in range(4):
                k = 4 * n + r
                dve.wait_ge(s_xnh, k + 1)
                nc.vector.tensor_tensor(xnT_lo[:, :, 2 * P * r:2 * P * (r + 1)],
                                        bank[r][:, :].rearrange("p (c t) -> p c t", c=KC),
                                        f(xnT_hi[:, :, 2 * P * r:2 * P * (r + 1)]),
                                        ALU.subtract).then_inc(s_xnl, 1)

        def norm_scalar(act, n):
            act.wait_ge(s_eps, n + 1)
            nc.scalar.activation(std, std, ACT.Sqrt).then_inc(s_std, 1)
            for r in range(4):
                act.wait_ge(s_xnt, 4 * n + r + 1)
                nc.scalar.activation(xnT_hi[:, :, 2 * P * r:2 * P * (r + 1)],
                                     bank[r][:, :].rearrange("p (c t) -> p c t", c=KC),
                                     ACT.Identity).then_inc(s_xnh, 1)

        def norm_tensor(pe, n):
            if n == 0:
                pe.wait_ge(s_const, 16 * N_CONST)
            for r in range(4):
                pe.wait_ge(s_xn, NT * n + 2 * r + 2)
                for c in range(KC):
                    for t in range(2):
                        mm = nc.tensor.transpose(bank[r][:, (2 * c + t) * P:(2 * c + t + 1) * P],
                                                 xn[:, 2 * r + t, c * P:(c + 1) * P], ident[:, :])
                mm.then_inc(s_xnt, 1)

        A = layout(farena, FWORDS, wqk_raw=(GROUP, 2, KC, P), wv_raw=(KC, GROUP * P), wo_raw=(GROUP, D),
                   k_scaled=(KC * P,), prob=(4, TRI))
        wqk_raw, wv_raw, wo_raw = A["wqk_raw"], A["wv_raw"], A["wo_raw"]
        k_scaled, prob = A["k_scaled"], A["prob"]
        R = layout(rarena, RWORDS, wqk_hi=(GROUP, 2, KC, P), wqk_lo=(GROUP, 2, KC, P),
                   wv_hi=(KC, GROUP * P), wv_lo=(KC, GROUP * P), wo_hi=(GROUP, D), wo_lo=(GROUP, D),
                   qk_hi=(2, 2, SEQ), qk_lo=(2, 2, SEQ), v_hi=(BATCH, QT, GROUP * P), v_lo=(BATCH, QT, GROUP * P),
                   pT_hi=(2, SEQ), pT_lo=(2, SEQ), zT_hi=(GROUP, SEQ), zT_lo=(GROUP, SEQ))
        wqk_hi, wqk_lo, wv_hi, wv_lo, wo_hi, wo_lo = (R[n] for n in ("wqk_hi", "wqk_lo", "wv_hi", "wv_lo", "wo_hi", "wo_lo"))
        qk_hi, qk_lo, v_hi, v_lo = (R[n] for n in ("qk_hi", "qk_lo", "v_hi", "v_lo"))
        pT_hi, pT_lo, zT_hi, zT_lo = (R[n] for n in ("pT_hi", "pT_lo", "zT_hi", "zT_lo"))
        bias_qkv = sb("bias_qkv", [P, 3, HEADS0], F32)
        scale0 = sb("scale0", [P, 2], F32)
        mask_neg = sb("mask_neg", [P, P], BF16)
        ident_bf = sb("ident_bf", [P, P], BF16)
        neg_max = small[:, 80:84]
        bias_now = small[:, 120:144].rearrange("p (u w) -> p u w", u=UNITS)
        row_sum = small[:, 84:92].rearrange("p (a b) -> p a b", a=2)
        row_inv = small[:, 92:100].rearrange("p (a b) -> p a b", a=2)

        s_wqk_raw = [sem(f"s_wqk_raw{h}") for h in range(GROUP)]
        s_wv_raw, s_wo_raw = sem("s_wv_raw"), sem("s_wo_raw")
        s_wtmp, s_wqk, s_wv, s_wo, s_bk = (sem(n) for n in ("s_wtmp", "s_wqk", "s_wv", "s_wo", "s_bk"))
        s_proj, s_proj_hi, s_proj_lo = (sem(n) for n in ("s_proj", "s_proj_hi", "s_proj_lo"))
        s_score, s_max, s_exp, s_inv, s_prob = (sem(n) for n in ("s_score", "s_max", "s_exp", "s_inv", "s_prob"))
        s_pT, s_pT_hi, s_pT_lo = (sem(n) for n in ("s_pT", "s_pT_hi", "s_pT_lo"))
        s_pv, s_z_hi, s_z_lo, s_y, s_y_added = (sem(n) for n in ("s_pv", "s_z_hi", "s_z_lo", "s_y", "s_y_added"))
        s_bo = sem("s_bo")
        s_bias = sem("s_bias")
        score_bank, pT_bank, proj_bank, z_bank, y_bank = bank[0:2], bank[2:4], bank[4:6], bank[6], bank[7]

        SCORED, TURNED, FINISHED = 1, 3, 4
        DEPTH = FINISHED + 1

        def jobs(u):
            return {0: [("q", 0, 0), ("k", 0, 2), ("v", 0, 3)],
                    1: [("q", 0, 0), ("v", 1, 1), ("k", 0, 2), ("v", 2, 3)],
                    2: [("q", 0, 0), ("v", 3, 1), ("k", 0, 2)],
                    3: [("q", 0, 0), ("k", 0, 2)]}[u % GROUP]

        JOBS = [(u, *job) for u in range(UNITS) for job in jobs(u)]
        NJ = len(JOBS)

        def job_number(u, kind, i=0):
            return next(n for n, j in enumerate(JOBS) if (j[0], j[1], j[2]) == (u, kind, i))

        def last_value_job(b):
            return job_number(GROUP * b + 2, "v", QT - 1)

        def slot_jobs(u, step):
            return [(n, kind, i) for n, (uu, kind, i, s) in enumerate(JOBS) if uu == u and s == step]

        def back(g, u, k):
            return (g, u - k) if u >= k else (g - 1, u - k + UNITS)

        def tri(i):
            return P * i * (i + 1) // 2

        def attn_tensor_slot(pe, g, u, first=False, tail=False, steps=range(QT)):
            has = [not tail or k > u for k in range(DEPTH)] if not first else [u >= k for k in range(DEPTH)]

            def unit(k):
                gg, uu = back(g, u, k)
                return gg, uu, UNITS * gg + uu

            def value_product(k, kt):
                gg, uu, v = unit(k)
                b, h = uu // GROUP, uu % GROUP
                pe.wait_ge(s_pT_lo, QT * v + kt + 1)
                if kt == 0:
                    pe.wait_ge(s_z_lo, v)
                    pe.wait_ge(s_proj_lo, NJ * gg + last_value_job(b) + 1)
                n = kt % 2
                w = SEQ - kt * P
                hs = slice(h * P, (h + 1) * P)
                out = z_bank[:, kt * P:SEQ]
                nc.tensor.matmul(out, v_hi[:, b, kt, hs], pT_hi[:, n, 0:w], start=(kt == 0), stop=False)
                nc.tensor.matmul(out, v_hi[:, b, kt, hs], pT_lo[:, n, 0:w], start=False, stop=False)
                nc.tensor.matmul(out, v_lo[:, b, kt, hs], pT_hi[:, n, 0:w], start=False,
                                 stop=(kt == QT - 1)).then_inc(s_pv, 1)

            def output_product(gg, b, pair):
                n = 2 * (BATCH * gg + b) + pair
                if pair == 0:
                    pe.wait_ge(s_wo, 2 * (gg + 1))
                pe.wait_ge(s_z_lo, UNITS * gg + GROUP * (b + 1))
                pe.wait_ge(s_y_added, n)
                for t in range(2):
                    i = 2 * pair + t
                    ts = slice(i * P, (i + 1) * P)
                    for h in range(GROUP):
                        out = y_bank[:, t * D:(t + 1) * D]
                        nc.tensor.matmul(out, zT_hi[:, h, ts], wo_hi[:, h, :], start=(h == 0), stop=False)
                        nc.tensor.matmul(out, zT_hi[:, h, ts], wo_lo[:, h, :], start=False, stop=False)
                        mm = nc.tensor.matmul(out, zT_lo[:, h, ts], wo_hi[:, h, :], start=False,
                                              stop=(h == GROUP - 1))
                mm.then_inc(s_y, 1)

            for i in steps:
                if has[TURNED]:
                    gg, uu, v = unit(TURNED)
                    pe.wait_ge(s_prob, QT * (v + 1))
                    if not (first and u == TURNED and i < 2):
                        pe.wait_ge(s_pT_lo, QT * v + i - 1)
                    for q in range(i, QT):
                        mm = nc.tensor.transpose(pT_bank[i % 2][:, (q - i) * P:(q - i + 1) * P],
                                                 prob[:, uu % 4, tri(q) + i * P:tri(q) + (i + 1) * P], ident[:, :])
                    mm.then_inc(s_pT, 1)
                if has[SCORED]:
                    gg, uu, v = unit(SCORED)
                    if i == 0:
                        pe.wait_ge(s_proj_lo, NJ * gg + job_number(uu, "k") + 1)
                    if not (first and u == SCORED and i < 2):
                        pe.wait_ge(s_exp, QT * v + i - 1)
                    w = (i + 1) * P
                    par = uu % 2
                    qs = slice(i * P, (i + 1) * P)
                    out = score_bank[i % 2]
                    nc.tensor.matmul(out[:, 0:w], qk_hi[:, par, 0, qs], qk_hi[:, par, 1, 0:w], start=True, stop=False)
                    nc.tensor.matmul(out[:, i * P:w], ident_bf[:, :], mask_neg[:, :], start=False, stop=False)
                    nc.tensor.matmul(out[:, 0:w], qk_hi[:, par, 0, qs], qk_lo[:, par, 1, 0:w], start=False, stop=False)
                    nc.tensor.matmul(out[:, 0:w], qk_lo[:, par, 0, qs], qk_hi[:, par, 1, 0:w], start=False,
                                     stop=True).then_inc(s_score, 1)
                if i == 0 and has[FINISHED]:
                    value_product(FINISHED, QT - 1)
                if has[0]:
                    for n, kind, j in slot_jobs(u, i):
                        if not (first and n < 2):
                            pe.wait_ge(s_proj_lo, NJ * g + n - 1)
                        out = proj_bank[n % 2][:, :]
                        b, h = u // GROUP, u % GROUP
                        if kind == "v":
                            pe.wait_ge(s_wv, 2 * (g + 1))
                            tok = slice((QT * b + j) * P, (QT * b + j + 1) * P)
                            terms = [(xh[:, c, tok], wh[:, c, :]) for xh, wh in
                                     ((xnT_hi, wv_hi), (xnT_hi, wv_lo), (xnT_lo, wv_hi)) for c in range(KC)]
                        else:
                            pe.wait_ge(s_wqk, GROUP * g + h + 1)
                            tok = slice(SEQ * b, SEQ * (b + 1))
                            w = 0 if kind == "q" else 1
                            terms = [(wh[:, h, w, c, :], xh[:, c, tok]) for wh, xh in
                                     ((wqk_hi, xnT_hi), (wqk_hi, xnT_lo), (wqk_lo, xnT_hi)) for c in range(KC)]
                        for m, (lhs, rhs) in enumerate(terms):
                            mm = nc.tensor.matmul(out, lhs, rhs, start=(m == 0), stop=(m == len(terms) - 1))
                        mm.then_inc(s_proj, 1)
                if i >= 1 and has[TURNED]:
                    value_product(TURNED, i - 1)
                if u % GROUP == GROUP - 1 and i >= 2 and has[FINISHED]:
                    gg, uu, _ = unit(FINISHED)
                    output_product(gg, uu // GROUP, i - 2)

        def attn_scalar_slot(act, g, u, first=False, tail=False, steps=range(QT)):
            has = [not tail or k > u for k in range(DEPTH)] if not first else [u >= k for k in range(DEPTH)]

            def unit(k):
                gg, uu = back(g, u, k)
                return gg, uu, UNITS * gg + uu

            for i in steps:
                if has[TURNED]:
                    gg, uu, v = unit(TURNED)
                    act.wait_ge(s_pT, QT * v + i + 1)
                    if not (first and u == TURNED and i < 2):
                        act.wait_ge(s_pv, QT * v + i - 1)
                    w = SEQ - i * P
                    nc.scalar.activation(pT_hi[:, i % 2, 0:w], pT_bank[i % 2][:, 0:w], ACT.Identity).then_inc(s_pT_hi, 1)
                if has[SCORED]:
                    gg, uu, v = unit(SCORED)
                    act.wait_ge(s_max, QT * v + i + 1)
                    if not first or u >= 5:
                        act.wait_ge(s_pT, QT * (v - 3))
                    w = (i + 1) * P
                    nc.scalar.activation(prob[:, uu % 4, tri(i):tri(i) + w], score_bank[i % 2][:, 0:w], ACT.Exp,
                                         bias=neg_max[:, i:i + 1],
                                         accum_out=row_sum[:, uu % 2, i:i + 1]).then_inc(s_exp, 1)
                if i == 0 and has[FINISHED]:
                    gg, uu, v = unit(FINISHED)
                    act.wait_ge(s_pv, QT * (v + 1))
                    if not first or uu >= GROUP:
                        act.wait_ge(s_y, 2 * (BATCH * gg + uu // GROUP))
                    nc.scalar.activation(zT_hi[:, uu % GROUP, :], z_bank[:, :], ACT.Identity,
                                         bias=bias_now[:, uu, 2:3]).then_inc(s_z_hi, 1)
                if has[0]:
                    for n, kind, j in slot_jobs(u, i):
                        act.wait_ge(s_proj, NJ * g + n + 1)
                        b, h = u // GROUP, u % GROUP
                        out, bias = job_target(u, kind, j, qk_hi, v_hi), 0.0
                        if kind == "v":
                            if not first:
                                act.wait_ge(s_pv, QT * (UNITS * g - (GROUP if b == 0 else 0)))
                        else:
                            if not first or u >= 2:
                                act.wait_ge(s_score, QT * (UNITS * g + u - 1))
                            act.wait_ge(s_bias, UNITS * g + u + 1)
                            bias = bias_now[:, u, 0:1] if kind == "q" else bias_now[:, u, 1:2]
                        nc.scalar.activation(out, proj_bank[n % 2][:, :], ACT.Identity, bias=bias).then_inc(s_proj_hi, 1)

        def job_target(u, kind, j, qk, v):
            return v[:, u // GROUP, j, :] if kind == "v" else qk[:, u % 2, 0 if kind == "q" else 1, :]

        def attn_vector_slot(dve, g, u, first=False, tail=False, steps=range(QT)):
            has = [not tail or k > u for k in range(DEPTH)] if not first else [u >= k for k in range(DEPTH)]

            def unit(k):
                gg, uu = back(g, u, k)
                return gg, uu, UNITS * gg + uu

            if has[0] and not (first and u == 0):
                nc.vector.tensor_copy(bias_now[:, u, :], bias_qkv[:, :, bass.ds(GROUP * g + u % GROUP, 1)]
                                      .rearrange("p w o -> p (w o)")).then_inc(s_bias, 1)
            for i in steps:
                if has[SCORED]:
                    gg, uu, v = unit(SCORED)
                    dve.wait_ge(s_score, QT * v + i + 1)
                    if not (first and u == SCORED):
                        dve.wait_ge(s_exp, QT * (v - 1) + i + 1)
                    nc.vector.tensor_reduce(neg_max[:, i:i + 1], score_bank[i % 2][:, 0:(i + 1) * P], X_AXIS,
                                            ALU.max, negate=True).then_inc(s_max, 1)
                if has[TURNED]:
                    gg, uu, v = unit(TURNED)
                    dve.wait_ge(s_pT_hi, QT * v + i + 1)
                    w = SEQ - i * P
                    nc.vector.tensor_tensor(pT_lo[:, i % 2, 0:w], pT_bank[i % 2][:, 0:w], f(pT_hi[:, i % 2, 0:w]),
                                            ALU.subtract).then_inc(s_pT_lo, 1)
                if i == 0 and has[FINISHED]:
                    gg, uu, v = unit(FINISHED)
                    dve.wait_ge(s_z_hi, v + 1)
                    nc.vector.scalar_tensor_tensor(
                        out=zT_lo[:, uu % GROUP, :], in0=z_bank[:, :],
                        scalar=bias_now[:, uu, 2:3],
                        in1=f(zT_hi[:, uu % GROUP, :]), op0=ALU.add, op1=ALU.subtract).then_inc(s_z_lo, 1)
                if has[SCORED]:
                    gg, uu, v = unit(SCORED)
                    dve.wait_ge(s_exp, QT * v + i + 1)
                    if not first or u >= 3:
                        dve.wait_ge(s_prob, QT * (v - 2) + i + 1)
                    nc.vector.reciprocal(row_inv[:, uu % 2, i:i + 1], row_sum[:, uu % 2, i:i + 1]).then_inc(s_inv, 1)
                if has[0]:
                    for n, kind, j in slot_jobs(u, i):
                        dve.wait_ge(s_proj_hi, NJ * g + n + 1)
                        h = u % GROUP
                        hi, lo = job_target(u, kind, j, qk_hi, v_hi), job_target(u, kind, j, qk_lo, v_lo)
                        if kind == "v":
                            nc.vector.tensor_tensor(lo, proj_bank[n % 2][:, :], f(hi), ALU.subtract).then_inc(s_proj_lo, 1)
                        else:
                            if kind == "q":
                                dve.wait_ge(s_bias, UNITS * g + u + 1)
                            nc.vector.scalar_tensor_tensor(
                                out=lo, in0=proj_bank[n % 2][:, :],
                                scalar=bias_now[:, u, 0:1] if kind == "q" else bias_now[:, u, 1:2],
                                in1=f(hi), op0=ALU.add, op1=ALU.subtract).then_inc(s_proj_lo, 1)
                if u % GROUP == GROUP - 1 and i >= 2 and has[FINISHED]:
                    gg, uu, _ = unit(FINISHED)
                    b, pair = uu // GROUP, i - 2
                    n = 2 * (BATCH * gg + b) + pair
                    dve.wait_ge(s_y, n + 1)
                    rows = X[:, QT * b + 2 * pair:QT * b + 2 * pair + 2, :]
                    if first and n == 0:
                        dve.wait_ge(s_bo, 1)
                    nc.vector.tensor_tensor(rows, y_bank[:, :].rearrange("p (t d) -> p t d", t=2), rows,
                                            ALU.add).then_inc(s_y_added, 1)

        def one(n):
            return scale0[:, 1:2].broadcast_to((P, n))

        def split_qk(pool, g, h, count):
            pool.wait_ge(s_wqk_raw[h], 16 * (g + 1))
            nc.gpsimd.tensor_tensor(wqk_hi[:, h, 0, :, :].rearrange("p c e -> p (c e)"),
                                    wqk_raw[:, h, 0, :, :].rearrange("p c e -> p (c e)"),
                                    one(KC * P), ALU.mult).then_inc(s_wtmp, 1)
            nc.gpsimd.tensor_tensor(k_scaled, wqk_raw[:, h, 1, :, :].rearrange("p c e -> p (c e)"),
                                    scale0[:, 0:1].broadcast_to((P, KC * P)), ALU.mult).then_inc(s_wtmp, 1)
            pool.wait_ge(s_wtmp, count + 2)
            nc.gpsimd.tensor_tensor(wqk_hi[:, h, 1, :, :].rearrange("p c e -> p (c e)"), k_scaled, one(KC * P),
                                    ALU.mult).then_inc(s_wtmp, 1)
            nc.gpsimd.tensor_tensor(wqk_lo[:, h, 0, :, :], wqk_raw[:, h, 0, :, :], f(wqk_hi[:, h, 0, :, :]),
                                    ALU.subtract).then_inc(s_wtmp, 1)
            pool.wait_ge(s_wtmp, count + 4)
            nc.gpsimd.tensor_tensor(wqk_lo[:, h, 1, :, :].rearrange("p c e -> p (c e)"), k_scaled,
                                    f(wqk_hi[:, h, 1, :, :]).rearrange("p c e -> p (c e)"),
                                    ALU.subtract).then_inc(s_wqk, 1)
            pool.wait_ge(s_wqk, GROUP * g + h + 1)

        def split_half(pool, s_raw, s_done, g, half, hi, lo, raw, count):
            pool.wait_ge(s_raw, 16 * (g + 1))
            nc.gpsimd.tensor_tensor(hi, raw, one(GROUP * P), ALU.mult).then_inc(s_wtmp, 1)
            pool.wait_ge(s_wtmp, count + 1)
            nc.gpsimd.tensor_tensor(lo, raw, f(hi), ALU.subtract).then_inc(s_done, 1)

        W_STEPS = GROUP * 4 + 4

        def split_v(pool, g, c, count):
            split_half(pool, s_wv_raw, s_wv, g, c, wv_hi[:, c, :], wv_lo[:, c, :], wv_raw[:, c, :], count)

        def split_o(pool, g, c, count):
            hs = slice(2 * c, 2 * c + 2)
            hi, lo, raw = (w[:, hs, :].rearrange("p h d -> p (h d)") for w in (wo_hi, wo_lo, wo_raw))
            split_half(pool, s_wo_raw, s_wo, g, c, hi, lo, raw, count)

        def normalise(pool, g, u, first=False):
            gg, uu = back(g, u, 1)
            v = UNITS * gg + uu
            for i in range(QT):
                pool.wait_ge(s_inv, QT * v + i + 1)
                p = prob[:, uu % 4, tri(i):tri(i) + (i + 1) * P]
                nc.gpsimd.tensor_tensor(p, p, row_inv[:, uu % 2, i:i + 1].broadcast_to((P, (i + 1) * P)),
                                        ALU.mult).then_inc(s_prob, 1)

        def attn_pool_early(pool, g, first=False):
            base = W_STEPS * g
            if first:
                split_qk(pool, g, 0, base)
                split_qk(pool, g, 1, base + 4)
                split_v(pool, g, 0, base + 8)
                split_v(pool, g, 1, base + 9)
                split_qk(pool, g, 2, base + 10)
                normalise(pool, g, 1, first)
                split_qk(pool, g, 3, base + 14)
                pool.wait_ge(s_xnt, 4)
                nc.gpsimd.tensor_tensor(X[:], X[:], bo_row[:, :].rearrange("p (o d) -> p o d", o=1)
                                        .broadcast_to((P, NT, D)), ALU.add).then_inc(s_bo, 1)
            else:
                normalise(pool, g, 0)
                pool.wait_ge(s_proj, NJ * (g - 1) + job_number(UNITS - 1, "k") + 1)
                split_qk(pool, g, 3, base + 14)
                normalise(pool, g, 1)
            normalise(pool, g, 2, first)
            normalise(pool, g, 3, first)
            normalise(pool, g, 4, first)
            if not first:
                pool.wait_ge(s_y, 4 * g)
            split_o(pool, g, 0, base + 18)
            split_o(pool, g, 1, base + 19)

        def attn_pool_late(pool, g, ahead=True):
            base = W_STEPS * (g + 1)
            for u in range(5, UNITS):
                normalise(pool, g, u)
                if u == 6 and not ahead:
                    mix0_prepare(pool)
                if ahead:
                    h = u - 5
                    pool.wait_ge(s_proj, NJ * g + job_number(GROUP + h, "k") + 1)
                    if u < 7:
                        split_qk(pool, g + 1, h, base + 4 * h)
                    else:
                        pool.wait_ge(s_proj, NJ * g + last_value_job(1) + 1)
                        split_v(pool, g + 1, 0, base + 8)
                        split_v(pool, g + 1, 1, base + 9)
                        split_qk(pool, g + 1, 2, base + 10)

        def attn_loads(sp, g, first=False):
            for h in range(GROUP):
                if not first:
                    sp.wait_ge(s_wqk, GROUP * (g - 1) + h + 1)
                sp.dma_start(wqk_raw[:, h, :, :, :].rearrange("p a c e -> p (a c e)"),
                             a["w_qk"][bass.ds(GROUP * g + h, 1), :, :].rearrange("o p n -> p (o n)")).then_inc(s_wqk_raw[h], 16)
                if h == 1:
                    if not first:
                        sp.wait_ge(s_wv, 2 * g)
                    sp.dma_start(wv_raw.rearrange("p c e -> p (c e)"),
                                 a["w_v"][bass.ds(g, 1), :, :].rearrange("o p n -> p (o n)")).then_inc(s_wv_raw, 16)
            if not first:
                sp.wait_ge(s_wo, 2 * g)
            sp.dma_start(wo_raw.rearrange("p c e -> p (c e)"),
                         a["w_o"][bass.ds(g, 1), :, :].rearrange("o p n -> p (o n)")).then_inc(s_wo_raw, 16)

        ATTN_F = 2048 + 1024 + 1024 + 256 + 4 * TRI
        ATTN_DONE = 4 * GROUPS

        RING = 4
        B0 = layout(farena, FWORDS, skip=(ATTN_F,), router=(KC, E0), down=(KC, 2 * LAT), gate_up=(2, KC, HID),
                    shared_out=(D,), lat_up=(D,), pick=(E0, P), route_bias=(E0,),
                    expert=(RING, 2 * HID), expert_out=(RING, LAT), e=(NT, E0), p=(NT, E0), b=(NT, E0), left=(NT, E0),
                    chosen=(NT, E0), w=(NT, E0), top=(NT, 8), total=(NT,), hid=(RING, SEQ))
        QK_R, V_R, O_R = 2 * GROUP * 2 * KC * P, 2 * KC * GROUP * P, 2 * GROUP * D
        M0 = layout(rarena, QK_R, expert=(RING, 2 * HID), pick=(RING, P), lat_hi=(TOKENS,), lat_lo=(TOKENS,))
        M0 |= layout(rarena, QK_R + V_R, skip=(QK_R,), w_split=(NT, 2 * E0), router_hi=(KC, E0), router_lo=(KC, E0),
                     down_hi=(KC, 2 * LAT), down_lo=(KC, 2 * LAT), gate_up_hi=(2, KC, HID), gate_up_lo=(2, KC, HID))
        M0 |= layout(rarena, RWORDS, skip=(QK_R + V_R + O_R,), wT=(TOKENS,))
        N0 = layout(farena, ATTN_F, shared_hid=(TOKENS,), acc=(TOKENS,), shared_gate=(2, SEQ), shared_prod=(2, SEQ))
        G0 = layout(farena, ATTN_F, skip=(2048 + 1536 + 1024 + 136 + 16 + 512,), gate=(RING, SEQ), prod=(RING, SEQ))
        zeros_bf = sb("zeros_bf", [P, LAT + SEQ], BF16)
        s_m0_raw, s_m0_w, s_m0_tmp = sem("s_m0_raw"), sem("s_m0_w"), sem("s_m0_tmp")
        s_logit0, s_e0, s_route0, s_split0, s_wT_ps, s_wT = (sem(n) for n in (
            "s_logit0", "s_e0", "s_route0", "s_split0", "s_wT_ps", "s_wT"))
        s_gate0, s_value0 = sem("s_gate0"), sem("s_value0")
        s_lat, s_lat_hi, s_lat_lo = (sem(n) for n in ("s_lat", "s_lat_hi", "s_lat_lo"))
        s_ex_raw = [sem(f"s_ex_raw{i}") for i in range(RING)]
        s_exo_raw = [sem(f"s_exo_raw{i}") for i in range(RING)]
        s_ex_hi, s_ex_lo, s_pick = (sem(n) for n in ("s_ex_hi", "s_ex_lo", "s_pick"))
        s_front, s_relu, s_prod, s_weighted, s_hid, s_back = (sem(n) for n in (
            "s_front", "s_relu", "s_prod", "s_weighted", "s_hid", "s_back"))
        s_zeros, s_acc, s_out0, s_out0_added = (sem(n) for n in ("s_zeros", "s_acc", "s_out0", "s_out0_added"))
        N_M0 = 8

        def mix0_loads(sp):
            for dst, name in ((B0["router"], "m0_router"), (B0["gate_up"], "m0_gate_up"),
                              (B0["shared_out"], "m0_shared_out"), (B0["down"][:, :, 0:LAT], "m0_down"),
                              (B0["down"][:, :, LAT:2 * LAT], "m0_down"), (B0["lat_up"][0:LAT, :], "m0_lat_up"),
                              (B0["pick"][0:2 * E0, :, :], "m0_pick")):
                sp.dma_start(dst, a[name]).then_inc(s_m0_raw, 16)
            sp.dma_start(B0["route_bias"], a["m0_bias"].broadcast_to((P, E0))).then_inc(s_m0_raw, 16)

        def expert_loads(sp, e, par, first=False):
            if not first:
                sp.wait_ge(s_ex_lo, e - (RING - 1))
            for half in range(2):
                sp.dma_start(B0["expert"][half * LAT:(half + 1) * LAT, par, :],
                             a["m0_expert"][:, bass.ds(e, 1), :].rearrange("l o n -> l (o n)")).then_inc(s_ex_raw[par], 16)
            if not first:
                sp.wait_ge(s_back, 2 * e - 2 * (RING - 1))
            sp.dma_start(B0["expert_out"][:, par, :],
                         a["m0_expert_out"][:, bass.ds(e, 1), :].rearrange("l o n -> l (o n)")).then_inc(s_exo_raw[par], 16)

        def mix0_prepare(pool):
            pool.wait_ge(s_m0_raw, 16 * N_M0)
            pool.wait_ge(s_proj, NJ * (GROUPS - 1) + last_value_job(1) + 1)
            k = 0
            for name in ("router", "down", "gate_up"):
                n = {"router": KC * E0, "down": KC * 2 * LAT, "gate_up": 2 * KC * HID}[name]
                flat = "p a b -> p (a b)" if name != "gate_up" else "p a b c -> p (a b c)"
                raw, hi, lo = (v.rearrange(flat) for v in (B0[name], M0[name + "_hi"], M0[name + "_lo"]))
                nc.gpsimd.tensor_tensor(hi, raw, one(n), ALU.mult).then_inc(s_m0_tmp, 1)
                k += 1
                pool.wait_ge(s_m0_tmp, k)
                nc.gpsimd.tensor_tensor(lo, raw, f(hi), ALU.subtract).then_inc(s_m0_w, 1)

        def expert_hi(pool, e, par, first=False):
            pool.wait_ge(s_ex_raw[par], 8 * (e - par) + 32)
            if not first:
                pool.wait_ge(s_front, 2 * e - 4)
            nc.gpsimd.tensor_tensor(M0["expert"][:, par, :], B0["expert"][:, par, :], one(2 * HID),
                                    ALU.mult).then_inc(s_ex_hi, 1)

        def expert_lo(dve, e, par):
            dve.wait_ge(s_ex_hi, e + 1)
            w = M0["expert"][LAT:P, par, :]
            nc.vector.tensor_tensor(w, B0["expert"][LAT:P, par, :], f(w), ALU.subtract).then_inc(s_ex_lo, 1)

        def expert_pick(e, par):
            nc.vector.tensor_scalar(M0["pick"][0:2 * E0, par, :],
                                    B0["pick"][0:2 * E0, bass.ds(e, 1), :].rearrange("p o n -> p (o n)"),
                                    1.0, None, ALU.mult).then_inc(s_pick, 1)

        BLOCK = 2 * RING
        BLOCKS = 2 * E0 // BLOCK
        BACK_LAG = 3

        def mix0_blocks(eng, block_of):
            block_of(0, first=True)
            with eng.Fori(1, BLOCKS - 1) as k:
                block_of(k)
            block_of(BLOCKS - 1, last=True)

        def front(pe, n, j):
            x, par = j % 2, j // 2
            half = slice(x * SEQ, (x + 1) * SEQ)
            for w, out, done in ((1, bank[x], s_gate0), (0, bank[2 + x], s_value0)):
                lhs = M0["expert"][:, par, w * HID:(w + 1) * HID]
                nc.tensor.matmul(out[:, :], lhs, M0["lat_hi"][:, half], start=True, stop=False)
                nc.tensor.matmul(out[:, :], lhs, M0["lat_lo"][:, half], start=False, stop=True).then_inc(done, 1)
            nc.tensor.matmul(bank[4 + x][:, :], M0["pick"][0:2 * E0, par, :], M0["wT"][0:2 * E0, half],
                             start=True, stop=True).then_inc(s_front, 1)

        def back_product(pe, n, j, k, last=False):
            x, par = j % 2, j // 2
            pe.wait_ge(s_hid, n + 3)
            if x == 0:
                pe.wait_ge(s_exo_raw[par], 16 * (k + 1))
            nc.tensor.matmul(bank[6 + x][0:LAT, :], B0["expert_out"][:, par, :], B0["hid"][:, j % RING, :],
                             start=False, stop=last, skip_group_check=True).then_inc(s_back, 1)

        def mix0_logits():
            nc.tensor.wait_ge(s_m0_w, 1)
            nc.tensor.wait_ge(s_proj_lo, NJ * GROUPS)
            for t in range(NT):
                k = 0
                for xs, ws in ((xnT_hi, "router_hi"), (xnT_hi, "router_lo"), (xnT_lo, "router_hi")):
                    for c in range(KC):
                        mm = nc.tensor.matmul(bank[4][:, t * E0:(t + 1) * E0], xs[:, c, t * P:(t + 1) * P],
                                              M0[ws][:, c, :], start=(k == 0), stop=(k == 2 * KC + 1))
                        k += 1
            mm.then_inc(s_logit0, 1)

        def mix0_latent(x):
            if x == 0:
                nc.tensor.wait_ge(s_m0_w, 2)
            else:
                nc.tensor.wait_ge(s_e0, 1)
            half = slice(x * SEQ, (x + 1) * SEQ)
            k = 0
            for ws, xs in (("down_hi", xnT_hi), ("down_hi", xnT_lo), ("down_lo", xnT_hi)):
                for c in range(KC):
                    mm = nc.tensor.matmul(bank[5 - x][:, :], M0[ws][:, c, :], xs[:, c, half],
                                          start=(k == 0), stop=(k == 2 * KC + 1))
                    k += 1
            mm.then_inc(s_lat, 1)

        def mix0_shared(x, w):
            half = slice(x * SEQ, (x + 1) * SEQ)
            nc.tensor.wait_ge(s_m0_w, 3)
            nc.tensor.wait_ge(s_exp, QT * UNITS * GROUPS)
            nc.tensor.wait_ge(s_lat_lo, x + 1)
            out = bank[x] if w else bank[5 - x]
            k = 0
            for ws, xs in (("gate_up_hi", xnT_hi), ("gate_up_hi", xnT_lo), ("gate_up_lo", xnT_hi)):
                for c in range(KC):
                    mm = nc.tensor.matmul(out[:, :], M0[ws][:, w, c, :], xs[:, c, half],
                                          start=(k == 0), stop=(k == 2 * KC + 1))
                    k += 1
            mm.then_inc(s_gate0 if w else s_value0, 1)

        def mix0_turn_weights():
            nc.tensor.wait_ge(s_split0, 2)
            nc.tensor.wait_ge(s_pT_lo, QT * UNITS * GROUPS)
            for t in range(NT):
                mm = nc.tensor.transpose(bank[2 + t // 4][0:2 * E0, (t % 4) * P:(t % 4 + 1) * P],
                                         f(M0["w_split"][:, t, :]), ident[:, :])
                if t % 4 == 3:
                    mm.then_inc(s_wT_ps, 1)

        def mix0_tensor(pe):
            def block_of(k, first=False, last=False):
                for j in range(BLOCK):
                    n = BLOCK * k + j
                    if j % 2 == 0:
                        pe.wait_ge(s_pick, RING * k + j // 2 + 1)
                    if not (first and j < 2):
                        pe.wait_ge(s_weighted, n - 1)
                    front(pe, n, j)
                    if first and j == 1:
                        attn_tensor_slot(pe, GROUPS, 3, tail=True, steps=(1, 2, 3))
                    if first and j == 2:
                        pe.wait_ge(s_y_added, ATTN_DONE)
                        pe.wait_ge(s_zeros, 1)
                        for x in range(2):
                            nc.tensor.matmul(bank[6 + x][0:LAT, :], zeros_bf[:, 0:LAT], zeros_bf[:, LAT:LAT + SEQ],
                                             start=True, stop=False, skip_group_check=True)
                    if j >= BACK_LAG:
                        back_product(pe, n - BACK_LAG, j - BACK_LAG, k)
                    elif not first:
                        back_product(pe, n - BACK_LAG, j - BACK_LAG + BLOCK, k - 1)

            def shared_out(r):
                nc.tensor.matmul(bank[r][:, :], zeros_bf[:, 0:P], zeros_bf[:, 0:SEQ], start=True, stop=False,
                                 skip_group_check=True)
                for t in (2 * r, 2 * r + 1):
                    nc.tensor.matmul(bank[r][:, (t % 2) * D:(t % 2 + 1) * D], N0["shared_hid"][:, t * P:(t + 1) * P],
                                     B0["shared_out"], start=False, stop=False, skip_group_check=True)

            pe.wait_ge(s_wT, 2)
            pe.wait_ge(s_prod, 2)
            mix0_blocks(pe, block_of)
            last = 2 * E0 - 1
            pe.wait_ge(s_weighted, last)
            shared_out(0)
            back_product(pe, last - 2, BLOCK - 3, BLOCKS - 1)
            shared_out(2)
            back_product(pe, last - 1, BLOCK - 2, BLOCKS - 1, last=True)
            pe.wait_ge(s_weighted, last + 1)
            shared_out(1)
            shared_out(3)
            back_product(pe, last, BLOCK - 1, BLOCKS - 1, last=True)
            for t in range(NT):
                if t % 4 == 0:
                    pe.wait_ge(s_acc, t // 4 + 1)
                mm = nc.tensor.matmul(bank[t // 2][:, (t % 2) * D:(t % 2 + 1) * D], N0["acc"][0:LAT, t * P:(t + 1) * P],
                                      B0["lat_up"][0:LAT, :], start=False, stop=True, skip_group_check=True)
                if t % 2:
                    mm.then_inc(s_out0, 1)

        def mix0_sigmoid():
            nc.scalar.wait_ge(s_logit0, 1)
            nc.scalar.activation(B0["e"].rearrange("p t e -> p (t e)"), bank[4][:, 0:NT * E0], ACT.Exp,
                                 scale=-1.0).then_inc(s_e0, 1)

        def mix0_latent_hi(x):
            nc.scalar.wait_ge(s_lat, x + 1)
            nc.scalar.activation(M0["lat_hi"][:, x * SEQ:(x + 1) * SEQ], bank[5 - x][:, :],
                                 ACT.Identity).then_inc(s_lat_hi, 1)

        def mix0_shared_relu(x):
            nc.scalar.wait_ge(s_gate0, x + 1)
            nc.scalar.activation(N0["shared_gate"][:, x, :], bank[x][:, :], ACT.Relu).then_inc(s_relu, 1)

        def mix0_weights_out():
            for x in range(2):
                nc.scalar.wait_ge(s_wT_ps, x + 1)
                nc.scalar.activation(M0["wT"][0:2 * E0, x * SEQ:(x + 1) * SEQ], bank[2 + x][0:2 * E0, :],
                                     ACT.Identity).then_inc(s_wT, 1)

        def mix0_scalar(act):
            def block_of(k, first=False, last=False):
                for j in range(BLOCK):
                    n = BLOCK * k + j
                    act.wait_ge(s_gate0, n + 3)
                    if not (first and j < RING):
                        act.wait_ge(s_hid, n - 1)
                    nc.scalar.activation(G0["gate"][:, j % RING, :], bank[j % 2][:, :], ACT.Relu).then_inc(s_relu, 1)

            mix0_blocks(act, block_of)
            for x in range(2):
                act.wait_ge(s_back, 2 * E0 - 1 + x)
                nc.scalar.activation(N0["acc"][0:LAT, x * SEQ:(x + 1) * SEQ], bank[6 + x][0:LAT, :],
                                     ACT.Identity).then_inc(s_acc, 1)

        route0_steps = [0]

        def route0(dve, ins):
            route0_steps[0] += 1
            ins.then_inc(s_route0, 1)
            dve.wait_ge(s_route0, route0_steps[0])

        def mix0_choose(dve):
            e, p, b, left, top = (B0[n] for n in ("e", "p", "b", "left", "top"))
            dve.wait_ge(s_m0_raw, 16 * N_M0)
            dve.wait_ge(s_e0, 1)
            route0(dve, nc.vector.tensor_scalar(e, e, 1.0, None, ALU.add))
            route0(dve, nc.vector.reciprocal(p, e))
            route0(dve, nc.vector.tensor_tensor(b, p, B0["route_bias"].rearrange("p (o e) -> p o e", o=1)
                                                .broadcast_to((P, NT, E0)), ALU.add))
            for t in range(NT):
                nc.vector.max(top[:, t, :], b[:, t, :]).then_inc(s_route0, 1)
            route0_steps[0] += NT
            dve.wait_ge(s_route0, route0_steps[0])
            for t in range(NT):
                nc.vector.match_replace(left[:, t, :], top[:, t, :], b[:, t, :], -3.0e38).then_inc(s_route0, 1)
            route0_steps[0] += NT

        def mix0_route(dve):
            p, b, left, chosen, w, total = (B0[n] for n in ("p", "b", "left", "chosen", "w", "total"))
            dve.wait_ge(s_route0, route0_steps[0])
            route0(dve, nc.vector.tensor_tensor(chosen, left, b, ALU.not_equal))
            route0(dve, nc.vector.tensor_tensor(chosen, chosen, p, ALU.mult))
            route0(dve, nc.vector.tensor_reduce(total, chosen, X_AXIS, ALU.add))
            route0(dve, nc.vector.reciprocal(total, total))
            route0(dve, nc.vector.tensor_scalar(total, total, ROUTE_SCALE, None, ALU.mult))
            route0(dve, nc.vector.tensor_tensor(w, chosen, total.rearrange("p (t o) -> p t o", o=1)
                                                .broadcast_to((P, NT, E0)), ALU.mult))
            nc.vector.tensor_copy(M0["w_split"][:, :, 0:E0], w).then_inc(s_split0, 1)
            dve.wait_ge(s_split0, 1)
            nc.vector.tensor_tensor(M0["w_split"][:, :, E0:2 * E0], w, f(M0["w_split"][:, :, 0:E0]),
                                    ALU.subtract).then_inc(s_split0, 1)

        def mix0_latent_lo(x):
            nc.vector.wait_ge(s_lat_hi, x + 1)
            half = slice(x * SEQ, (x + 1) * SEQ)
            nc.vector.tensor_tensor(M0["lat_lo"][:, half], bank[5 - x][:, :], f(M0["lat_hi"][:, half]),
                                    ALU.subtract).then_inc(s_lat_lo, 1)

        def mix0_shared_prod(x):
            nc.vector.wait_ge(s_relu, x + 1)
            nc.vector.wait_ge(s_value0, x + 1)
            nc.vector.tensor_tensor(N0["shared_prod"][:, x, :], bank[5 - x][:, :], N0["shared_gate"][:, x, :],
                                    ALU.mult).then_inc(s_prod, 1)

        def mix0_vector(dve):
            for e in range(2):
                expert_lo(dve, e, e)
                expert_pick(e, e)

            def block_of(k, first=False, last=False):
                for j in range(BLOCK):
                    n = BLOCK * k + j
                    dve.wait_ge(s_relu, n + 3)
                    dve.wait_ge(s_value0, n + 3)
                    if not (first and j < RING):
                        dve.wait_ge(s_hid, n - 1)
                    nc.vector.tensor_tensor(G0["prod"][:, j % RING, :], bank[2 + j % 2][:, :], G0["gate"][:, j % RING, :],
                                            ALU.mult).then_inc(s_prod, 1)
                    if not (last and j >= BLOCK - 4):
                        ahead = RING * k + j // 2 + 2
                        par = (j // 2 + 2) % RING
                        if j % 2 == 0:
                            expert_lo(dve, ahead, par)
                        else:
                            expert_pick(ahead, par)
                    dve.wait_ge(s_front, n + 1)
                    dve.wait_ge(s_prod, n + 3)
                    nc.vector.tensor_tensor(G0["prod"][:, j % RING, :], bank[4 + j % 2][:, :], G0["prod"][:, j % RING, :],
                                            ALU.mult).then_inc(s_weighted, 1)
                    if first and j == 1:
                        attn_vector_slot(dve, GROUPS, 3, tail=True, steps=(1, 2, 3))

            mix0_blocks(dve, block_of)
            for r in range(NT // 2):
                dve.wait_ge(s_out0, r + 1)
                rows = X[:, 2 * r:2 * r + 2, :]
                nc.vector.tensor_tensor(rows, bank[r][:, :].rearrange("p (t d) -> p t d", t=2), rows,
                                        ALU.add).then_inc(s_out0_added, 1)
                dve.wait_ge(s_out0_added, r + 1)
                norm_stats(2 * r)
                norm_stats(2 * r + 1)

        def mix0_pool(pool):
            nc.gpsimd.memset(zeros_bf[:, :], 0.0).then_inc(s_zeros, 1)
            pool.wait_ge(s_proj, NJ * GROUPS)
            for e in range(2):
                expert_hi(pool, e, e, first=True)
            for x in range(2):
                pool.wait_ge(s_prod, x + 1)
                nc.gpsimd.tensor_tensor(N0["shared_hid"][:, x * SEQ:(x + 1) * SEQ], N0["shared_prod"][:, x, :],
                                        N0["shared_gate"][:, x, :], ALU.mult).then_inc(s_hid, 1)

            def block_of(k, first=False, last=False):
                for j in range(BLOCK):
                    n = BLOCK * k + j
                    if j % 2 == 0 and not (last and j >= BLOCK - 4):
                        expert_hi(pool, RING * k + j // 2 + 2, (j // 2 + 2) % RING, first=first and j < 4)
                    pool.wait_ge(s_weighted, n + 1)
                    if not (first and j < RING):
                        pool.wait_ge(s_back, n - 3)
                    nc.gpsimd.tensor_tensor(B0["hid"][:, j % RING, :], G0["prod"][:, j % RING, :],
                                            G0["gate"][:, j % RING, :], ALU.mult).then_inc(s_hid, 1)

            mix0_blocks(pool, block_of)

        M0_END = QK_R + V_R
        STEPS = BATCH * KC
        TILES = HM * QT
        L1a = layout(farena, FWORDS, rope=(4, SEQ), w_raw=(3, KC, D), cos=(SEQ,), sin=(SEQ,), blocks=(HM, DH1 + 1),
                     gate=(HEADS1,), w_out=(KC, D), rot=(2, KC, SEQ), low=(KC, SEQ), k_feat=(KC, SEQ),
                     memory=(STEPS, HM, DH1 + 1), q_feat=(STEPS, SEQ), k_rows=(NT, D),
                     values=(STEPS, QT, HM, DH1 + 1), attended=(STEPS, QT, HM, DH1 + 1))
        L1b = layout(farena, FWORDS, prob=(4, SEQ), head_values=(HM, QT, VW), z=(SEQ,), skip=(1024 + 136 + 16 + 512,),
                     pT=(2, QT, SEQ))
        L1c = layout(farena, FWORDS, skip=(2048 + 1536 + 1024 + 136 + 16 + 512,), mixed=(KC, TOKENS), out=(2, 2, D),
                     inv=(2, 2, HEADS1), gates=(2, HEADS1))
        pick_raw = layout(farena, FWORDS, skip=(FWORDS - 4 * 4 * P - 584,), pick=(4, 4, P))["pick"]
        R1 = layout(rarena, RWORDS, skip=(M0_END,), w_hi=(3, KC, D), w_lo=(3, KC, D), qk_hi=(2, STEPS, SEQ), qk_lo=(2, STEPS, SEQ),
                    pick=(4, 4, P), pairs=(2, 4, SEQ))
        names = ("s_l1_raw s_l1_out_raw s_l1_tmp s_l1_w s_pick1 s_ones s_proj1 s_rope s_rot s_hi1 s_neg1 s_exp1 s_lo1_even s_lo1_odd s_feat "
                 "s_kT s_k_rows s_v1 s_values s_mem_ps s_mem s_sel_q s_sel_k s_pair_q s_pair_k s_hv s_score1 s_max1 "
                 "s_prob1 s_pT1 s_pT_even s_pT_odd s_pv1 s_z1 s_zT1 s_att s_gates s_memout s_inv1 s_mix_a s_mix_b "
                 "s_mix s_mixT s_mixT_sb s_wo1 s_att_added").split()
        (s_l1_raw, s_l1_out_raw, s_l1_tmp, s_l1_w, s_pick1, s_ones, s_proj1, s_rope, s_rot, s_hi1, s_neg1, s_exp1, s_lo1_even, s_lo1_odd, s_feat,
         s_kT, s_k_rows, s_v1, s_values, s_mem_ps, s_mem, s_sel_q, s_sel_k, s_pair_q, s_pair_k, s_hv, s_score1, s_max1,
         s_prob1, s_pT1, s_pT_even, s_pT_odd, s_pv1, s_z1, s_zT1, s_att, s_gates, s_memout, s_inv1, s_mix_a, s_mix_b,
         s_mix, s_mixT, s_mixT_sb, s_wo1, s_att_added) = (sem(n) for n in names)
        neg_max1 = small[:, 112:116]
        N_L1 = 5
        C = DH1 + 1

        def l1_loads(sp):
            sp.wait_ge(s_hid, 2)
            sp.wait_ge(s_pT, QT * UNITS * GROUPS)
            for dst, name in ((L1a["w_raw"], "l1_w"), (L1a["cos"], "l1_cos"), (L1a["sin"], "l1_sin"),
                              (L1a["blocks"], "l1_blocks")):
                sp.dma_start(dst, a[name]).then_inc(s_l1_raw, 16)
            sp.dma_start(L1a["gate"], a["l1_gate"].broadcast_to((P, HEADS1))).then_inc(s_l1_raw, 16)
            sp.dma_start(L1a["w_out"], a["l1_w_out"]).then_inc(s_l1_out_raw, 16)

        def l1_pick_load(sp):
            sp.wait_ge(s_out0_added, 4)
            sp.wait_ge(s_xnt, 8)
            sp.dma_start(pick_raw, a["l1_pick"]).then_inc(s_l1_out_raw, 16)

        CHUNKS = 2 * BATCH * KC
        rope_pair = [L1a["rope"][:, 0:2, :], L1a["rope"][:, 2:4, :],
                     L1a["w_raw"].rearrange("p w c d -> p (w c d)")[:, 0:2 * SEQ].rearrange("p (k t) -> p k t", k=2)]
        rot = L1a["rot"].rearrange("p a c t -> p (a c) t")

        def l1_pool_project(pool):
            pool.wait_ge(s_l1_raw, 16 * N_L1)
            pool.wait_ge(s_y_added, ATTN_DONE)
            for w in range(3):
                flat = "p c d -> p (c d)"
                raw, hi, lo = (v[:, w, :, :].rearrange(flat) for v in (L1a["w_raw"], R1["w_hi"], R1["w_lo"]))
                nc.gpsimd.tensor_tensor(hi, raw, one(KC * D), ALU.mult).then_inc(s_l1_tmp, 1)
                pool.wait_ge(s_l1_tmp, w + 1)
                nc.gpsimd.tensor_tensor(lo, raw, f(hi), ALU.subtract).then_inc(s_l1_w, 1)
            pool.wait_ge(s_out0_added, 4)
            nc.gpsimd.memset(L1a["values"].rearrange("p s k h c -> p (s k h) c")[:, :, DH1:C], 1.0).then_inc(s_ones, 1)
            for c in range(CHUNKS + 1):
                if c < CHUNKS:
                    pool.wait_ge(s_rope, 2 * (c + 1))
                    if c >= 4:
                        pool.wait_ge(s_feat, c - 3)
                    t = rope_pair[c % 3]
                    nc.gpsimd.tensor_tensor(rot[:, c % 4, :], t[:, 0, :], t[:, 1, :],
                                            ALU.add if c % 2 else ALU.subtract).then_inc(s_rot, 1)
                if c % 2:
                    rotated_lo(pool, nc.gpsimd, c - 1, s_lo1_even)
            pool.wait_ge(s_l1_out_raw, 32)
            nc.gpsimd.tensor_tensor(R1["pick"].rearrange("p a b c -> p (a b c)"),
                                    pick_raw.rearrange("p a b c -> p (a b c)"), one(16 * P),
                                    ALU.mult).then_inc(s_pick1, 1)
            pool.wait_ge(s_rot, CHUNKS)
            nc.gpsimd.memset(L1b["head_values"], 0.0).then_inc(s_ones, 1)
            pool.wait_ge(s_pick1, 1)

        def rotated_lo(eng, ops, c, done):
            b, w, m = c // 4, c // 2 % 2, c % 2
            eng.wait_ge(s_hi1, c + 1)
            ops.tensor_tensor(R1["qk_lo"][:, w, KC * b + m, :], rot[:, c % 4, :],
                              f(R1["qk_hi"][:, w, KC * b + m, :]), ALU.subtract).then_inc(done, 1)

        def l1_tensor_project(pe):
            pe.wait_ge(s_xnl, 8)

            def three(out, left, right, k0=True):
                terms = [(l, r) for l, r in ((left[0], right[0]), (left[0], right[1]), (left[1], right[0]))]
                k = 0
                for l, r in terms:
                    for c in range(KC):
                        mm = nc.tensor.matmul(out, l(c), r(c), start=(k == 0), stop=(k == 2 * KC + 1))
                        k += 1
                return mm

            def turn_keys(b):
                pe.wait_ge(s_feat, 4 * b + 4)
                if b:
                    pe.wait_ge(s_k_rows, 2)
                for tt in range(QT):
                    for m in range(KC):
                        mm = nc.tensor.transpose(bank[tt // 2][:, ((tt % 2) * KC + m) * P:((tt % 2) * KC + m + 1) * P],
                                                 L1a["k_feat"][:, m, tt * P:(tt + 1) * P], ident[:, :])
                    if tt % 2:
                        mm.then_inc(s_kT, 1)

            def project(j):
                b, w = j // 2, j % 2
                half = slice(b * SEQ, (b + 1) * SEQ)
                pe.wait_ge(s_xnl, 6 + 2 * b)
                if j < 2:
                    pe.wait_ge(s_l1_w, j + 1)
                else:
                    pe.wait_ge(s_rope, 4 * (j - 1))
                for m in range(KC):
                    mm = three(bank[4 + 2 * (j % 2) + m][:, :],
                               [lambda c, v=v, m=m: v[:, w, c, m * P:(m + 1) * P] for v in (R1["w_hi"], R1["w_lo"])],
                               [lambda c, v=v: v[:, c, half] for v in (xnT_hi, xnT_lo)])
                mm.then_inc(s_proj1, 1)

            def project_values(j):
                pe.wait_ge(s_xnl, min(8, 7 + j))
                if j == 0:
                    pe.wait_ge(s_l1_w, 3)
                if j >= 2:
                    pe.wait_ge(s_values, 2 * (j - 1))
                for t in (2 * j, 2 * j + 1):
                    mm = three(bank[2 + j % 2][:, (t % 2) * D:(t % 2 + 1) * D],
                               [lambda c, v=v: v[:, c, t * P:(t + 1) * P] for v in (xnT_hi, xnT_lo)],
                               [lambda c, v=v: v[:, 2, c, :] for v in (R1["w_hi"], R1["w_lo"])])
                mm.then_inc(s_v1, 1)

            def memory(b):
                pe.wait_ge(s_values, QT * (b + 1))
                pe.wait_ge(s_k_rows, 2 * b + 2)
                if b:
                    pe.wait_ge(s_values, NT)
                for m in range(KC):
                    st = KC * b + m
                    for kt in range(QT):
                        mm = nc.tensor.matmul(bank[4 + st][:, 0:HM * C], L1a["k_rows"][:, QT * b + kt, m * P:(m + 1) * P],
                                              L1a["values"][:, st, kt, :, :].rearrange("p h c -> p (h c)"),
                                              start=(kt == 0), stop=(kt == QT - 1))
                    mm.then_inc(s_mem_ps, 1)

            project(0)
            project(1)
            project_values(0)
            project(2)
            project_values(1)
            project(3)
            turn_keys(0)
            project_values(2)
            project_values(3)
            turn_keys(1)
            pe.wait_ge(s_ones, 1)
            pe.wait_ge(s_rope, 2 * CHUNKS)
            memory(0)
            memory(1)
            pe.wait_ge(s_lo1_even, CHUNKS // 2)
            pe.wait_ge(s_lo1_odd, CHUNKS // 2)
            pe.wait_ge(s_pick1, 1)
            pe.wait_ge(s_mem, STEPS)

        def l1_scalar_project(act):
            def copy_values(j):
                act.wait_ge(s_v1, j + 1)
                for t in (2 * j, 2 * j + 1):
                    b, kt = t // QT, t % QT
                    nc.scalar.activation(L1a["values"][:, KC * b:KC * (b + 1), kt, :, 0:DH1],
                                         bank[2 + j % 2][:, (t % 2) * D:(t % 2 + 1) * D]
                                         .rearrange("p (m h d) -> p m h d", m=KC, h=HM), ACT.Identity).then_inc(s_values, 1)

            def copy_keys(b):
                for r in range(2):
                    act.wait_ge(s_kT, 2 * b + r + 1)
                    nc.scalar.activation(L1a["k_rows"][:, QT * b + 2 * r:QT * b + 2 * r + 2, :],
                                         bank[r][:, :].rearrange("p (t d) -> p t d", t=2),
                                         ACT.Identity).then_inc(s_k_rows, 1)

            for c in range(CHUNKS):
                b, w, m = c // 4, c // 2 % 2, c % 2
                act.wait_ge(s_rot, c + 1)
                if c >= 2:
                    act.wait_ge(s_feat, c - 1)
                nc.scalar.activation(L1a["low"][:, m, :], rot[:, c % 4, :], ACT.Relu, scale=-1.0).then_inc(s_neg1, 1)
                nc.scalar.activation(R1["qk_hi"][:, w, KC * b + m, :], rot[:, c % 4, :], ACT.Identity).then_inc(s_hi1, 1)
                act.wait_ge(s_neg1, c + 1)
                nc.scalar.activation(L1a["low"][:, m, :], L1a["low"][:, m, :], ACT.Exp, scale=-1.0).then_inc(s_exp1, 1)
                if c == 2:
                    act.wait_ge(s_ones, 1)
                if c in (2, 4, 6, 7):
                    copy_values((c - 1) // 2)
                if c == 6:
                    copy_keys(0)
            copy_keys(1)
            nc.scalar.activation(L1a["gate"], L1a["gate"], ACT.Exp, scale=-1.0).then_inc(s_gates, 1)

        def l1_vector_project(dve):
            dve.wait_ge(s_l1_raw, 16 * N_L1)
            dve.wait_ge(s_l1_w, 3)
            for c in range(CHUNKS + 2):
                if c < CHUNKS:
                    j, m = c // 2, c % 2
                    dve.wait_ge(s_proj1, j + 1)
                    if c >= 3:
                        dve.wait_ge(s_rot, c - 2)
                    q0, q1 = bank[4 + 2 * (j % 2)][:, :], bank[4 + 2 * (j % 2) + 1][:, :]
                    products = ((q1, "cos"), (q0, "sin")) if m else ((q0, "cos"), (q1, "sin"))
                    for k, (x, y) in enumerate(products):
                        nc.vector.tensor_tensor(rope_pair[c % 3][:, k, :], x, L1a[y], ALU.mult).then_inc(s_rope, 1)
                if c >= 2:
                    d = c - 2
                    b, w, m = d // 4, d // 2 % 2, d % 2
                    if m:
                        rotated_lo(dve, nc.vector, d, s_lo1_odd)
                    dve.wait_ge(s_exp1, d + 1)
                    if d == 6:
                        dve.wait_ge(s_kT, 2)
                    out = L1a["k_feat"][:, m, :] if w else L1a["q_feat"][:, KC * b + m, :]
                    nc.vector.scalar_tensor_tensor(out=out, in0=rot[:, d % 4, :], scalar=0.0, in1=L1a["low"][:, m, :],
                                                   op0=ALU.max, op1=ALU.add).then_inc(s_feat, 1)
            for st in range(STEPS):
                dve.wait_ge(s_mem_ps, st + 1)
                nc.vector.tensor_tensor(L1a["memory"][:, st, :, :].rearrange("p h c -> p (h c)"), bank[4 + st][:, 0:HM * C],
                                        L1a["blocks"].rearrange("p h c -> p (h c)"), ALU.mult).then_inc(s_mem, 1)

        LAG_S, LAG_T, LAG_V = 6, 9, 14
        TAIL1 = 24
        score1_bank, turn1_bank, side_bank, z1_bank = bank[0:3], (bank[3], bank[5], bank[7]), bank[4], bank[6]

        def in_bank_before(t):
            return 2 if t < 2 else 5 if t == 2 else 3

        def behind(s, n, lag, first, tail):
            if (first and n < lag) or (tail and lag <= n):
                return None
            return (s, n - lag) if n >= lag else (s - 1, n - lag + TILES)

        def turned(s, n, first, tail, delay=0):
            if first or n - delay not in (5, 21):
                return None
            return s - 1, (n - delay) // 16

        def pair_rows(pe, s, pr, w):
            if w == 0:
                pe.wait_ge(s_pair_k, 4 * s + pr)
                if pr % 2 and not (isinstance(s, int) and s == 0):
                    pe.wait_ge(s_att, 2 * s - (1 if pr == 1 else 0))
            else:
                pe.wait_ge(s_pair_q, 4 * s + pr + 1)
            nc.tensor.matmul(side_bank[:, :], R1["pick"][:, pr, 2 * w, :], R1["qk_hi"][:, w, bass.ds(s, 1), :]
                             .rearrange("p o t -> p (o t)"), start=True, stop=False)
            nc.tensor.matmul(side_bank[:, :], R1["pick"][:, pr, 2 * w + 1, :], R1["qk_lo"][:, w, bass.ds(s, 1), :]
                             .rearrange("p o t -> p (o t)"), start=False, stop=True).then_inc(s_sel_k if w else s_sel_q, 1)

        def l1_tensor_slot(pe, s, n, first=False, tail=False):
            if n % 8 in (0, 3) and not tail:
                pair_rows(pe, s, n // 8, n % 8 // 3)
            at = behind(s, n, LAG_T, first, tail)
            if at:
                ss, t = at
                pe.wait_ge(s_prob1, TILES * ss + t + 1)
                if not (first and t < 3):
                    old = t - in_bank_before(t)
                    pe.wait_ge(s_pT_odd if old % 2 else s_pT_even, TILES // 2 * ss + old // 2 + 1)
                for kt in range(QT):
                    mm = nc.tensor.transpose(turn1_bank[t % 3][:, kt * P:(kt + 1) * P],
                                             L1b["prob"][:, t % 4, kt * P:(kt + 1) * P], ident[:, :])
                mm.then_inc(s_pT1, 1)
            at = behind(s, n, LAG_S, first, tail)
            if at:
                ss, t = at
                h, i = t // QT, t % QT
                if t % 8 == 0:
                    pe.wait_ge(s_pair_k, 4 * ss + t // 8 + 1)
                if not (first and t < 3):
                    pe.wait_ge(s_prob1, TILES * ss + t - in_bank_before(t) + 1)
                rows = slice(64 * (h % 2), 64 * (h % 2) + 64)
                nc.tensor.matmul(score1_bank[t % 3][:, :], R1["pairs"][rows, 0, h // 2, i * P:(i + 1) * P],
                                 R1["pairs"][rows, 1, h // 2, :], start=True, stop=True).then_inc(s_score1, 1)
            at = behind(s, n, LAG_V, first, tail)
            if at:
                ss, t = at
                h, kt = t // QT, t % QT
                if kt == 0:
                    pe.wait_ge(s_pT_even, TILES // 2 * ss + 2 * h + 2)
                    pe.wait_ge(s_pT_odd, TILES // 2 * ss + 2 * h + 2)
                    pe.wait_ge(s_hv, HM * ss + h + 1)
                    if h % 2 == 0 and not (first and h < 4):
                        pe.wait_ge(s_z1, 4 * ss + h // 2 - 1)
                g = h % 4
                nc.tensor.matmul(z1_bank[g * VW:(g + 1) * VW, :], L1b["head_values"][:, h, kt, :],
                                 L1b["pT"][:, h % 2, kt, :], start=(kt == 0), stop=(kt == QT - 1)).then_inc(s_pv1, 1)
            at = turned(s, n, first, tail)
            if at:
                ss, g = at
                pe.wait_ge(s_z1, 4 * ss + 2 * g + 2)
                pe.wait_ge(s_pair_k, 4 * ss + (4 if tail else 5 + 2 * g))
                for i in range(QT):
                    mm = nc.tensor.transpose(side_bank[:, i * P:(i + 1) * P], L1b["z"][:, i * P:(i + 1) * P], ident[:, :])
                mm.then_inc(s_zT1, 1)

        def l1_scalar_slot(act, s, n, first=False, tail=False):
            if n % 8 in (1, 4) and not tail:
                pr, w = n // 8, n % 8 // 4
                act.wait_ge(s_sel_k if w else s_sel_q, 4 * s + pr + 1)
                if not first:
                    act.wait_ge(s_score1, TILES * (s - 1) + 8 * (pr + 1))
                nc.scalar.activation(R1["pairs"][:, w, pr, :], side_bank[:, :],
                                     ACT.Identity).then_inc(s_pair_k if w else s_pair_q, 1)
            at = behind(s, n, LAG_T, first, tail)
            if at and at[1] % 2:
                ss, t = at
                turned_out(act, nc.scalar, ss, t, first)
            at = behind(s, n, LAG_S, first, tail)
            if at:
                ss, t = at
                act.wait_ge(s_max1, TILES * ss + t + 1)
                if not (first and t < 4):
                    act.wait_ge(s_pT1, TILES * ss + t - 3)
                nc.scalar.activation(L1b["prob"][:, t % 4, :], score1_bank[t % 3][:, :], ACT.Exp,
                                     bias=neg_max1[:, t % 4:t % 4 + 1]).then_inc(s_prob1, 1)
            at = behind(s, n, LAG_V, first, tail)
            if at and at[1] % 8 == 7:
                ss, t = at
                act.wait_ge(s_pv1, TILES * ss + t + 1)
                if not (first and t < 16):
                    act.wait_ge(s_zT1, 2 * ss + t // 16)
                half = slice(64 * (t // 8 % 2), 64 * (t // 8 % 2) + 64)
                nc.scalar.activation(L1b["z"][half, :], z1_bank[half, :], ACT.Identity).then_inc(s_z1, 1)

        def turned_out(eng, ops, ss, t, first):
            h, i = t // QT, t % QT
            eng.wait_ge(s_pT1, TILES * ss + t + 1)
            if not first or h >= 2:
                eng.wait_ge(s_pv1, TILES * ss + QT * (h - 1))
            out = L1b["pT"][:, h % 2, :, i * P:(i + 1) * P]
            src = turn1_bank[t % 3][:, :].rearrange("p (k q) -> p k q", k=QT)
            if ops is nc.scalar:
                ops.activation(out, src, ACT.Identity).then_inc(s_pT_odd, 1)
            else:
                ops.tensor_copy(out, src).then_inc(s_pT_even, 1)

        def l1_vector_slot(dve, s, n, first=False, tail=False):
            at = turned(s, n, first, tail, delay=1)
            if at:
                ss, g = at
                dve.wait_ge(s_zT1, 2 * ss + g + 1)
                for i in range(QT):
                    ins = nc.vector.tensor_scalar(
                        L1a["attended"][:, bass.ds(ss, 1), i, 4 * g:4 * g + 4, :].rearrange("p o h c -> p (o h) c"),
                        side_bank[:, i * P:(i + 1) * P].rearrange("p (h c) -> p h c", h=4)[:, :, 0:C],
                        1.0, None, ALU.mult)
                ins.then_inc(s_att, 1)
            at = behind(s, n, LAG_S, first, tail)
            if at:
                ss, t = at
                dve.wait_ge(s_score1, TILES * ss + t + 1)
                if not (first and t < 4):
                    dve.wait_ge(s_prob1, TILES * ss + t - 3)
                nc.vector.tensor_reduce(neg_max1[:, t % 4:t % 4 + 1], score1_bank[t % 3][:, :], X_AXIS, ALU.max,
                                        negate=True).then_inc(s_max1, 1)
            at = behind(s, n, LAG_T, first, tail)
            if at and at[1] % 2 == 0:
                ss, t = at
                turned_out(dve, nc.vector, ss, t, first)
            if n % QT == 2 and not tail:
                h = n // QT
                if not first:
                    dve.wait_ge(s_pv1, TILES * (s - 1) + QT * (h + 1))
                nc.vector.tensor_scalar(L1b["head_values"][:, h, :, 0:C],
                                        L1a["values"][:, bass.ds(s, 1), :, h, :].rearrange("p o k c -> p (o k) c"),
                                        1.0, None, ALU.mult).then_inc(s_hv, 1)

        def l1_run(eng, slot):
            for n in range(TILES):
                slot(eng, 0, n, first=True)
            with eng.Fori(1, STEPS) as s:
                for n in range(TILES):
                    slot(eng, s, n)
            for n in range(TAIL1):
                slot(eng, STEPS, n, tail=True)

        def mix_tensor(pe):
            pe.wait_ge(s_mem, STEPS)
            pe.wait_ge(s_l1_out_raw, 32)

            def turn(r):
                pe.wait_ge(s_mix, 2 * r + 2)
                if r >= 2:
                    pe.wait_ge(s_mixT_sb, r - 1)
                for c in range(KC):
                    for t in range(2):
                        mm = nc.tensor.transpose(bank[4 + r % 2][:, (2 * c + t) * P:(2 * c + t + 1) * P],
                                                 L1c["out"][:, t, 0, c * P:(c + 1) * P], ident[:, :])
                mm.then_inc(s_mixT, 1)

            def output(r):
                pe.wait_ge(s_mixT_sb, r + 1)
                if r >= 2:
                    pe.wait_ge(s_att_added, r - 1)
                for t in (2 * r, 2 * r + 1):
                    for c in range(KC):
                        mm = nc.tensor.matmul(bank[6 + r % 2][:, (t % 2) * D:(t % 2 + 1) * D],
                                              L1c["mixed"][:, c, t * P:(t + 1) * P], L1a["w_out"][:, c, :],
                                              start=(c == 0), stop=(c == KC - 1))
                mm.then_inc(s_wo1, 1)

            for t in range(NT):
                b, i = t // QT, t % QT
                if t >= 4:
                    pe.wait_ge(s_mix_a, t - 3)
                for m in range(KC):
                    mm = nc.tensor.matmul(bank[t % 4][:, m * HM * C:(m + 1) * HM * C],
                                          L1a["q_feat"][:, KC * b + m, i * P:(i + 1) * P],
                                          L1a["memory"][:, KC * b + m, :, :].rearrange("p h c -> p (h c)"),
                                          start=True, stop=True)
                mm.then_inc(s_memout, 1)
                if t >= 3 and t % 2:
                    turn((t - 3) // 2)
                if t >= 5 and t % 2:
                    output((t - 5) // 2)
            turn(3)
            output(2)
            output(3)

        def mix_scalar(act):
            for r in range(NT // 2):
                act.wait_ge(s_mixT, r + 1)
                nc.scalar.activation(L1c["mixed"][:, :, 2 * P * r:2 * P * (r + 1)],
                                     bank[4 + r % 2][:, :].rearrange("p (c t) -> p c t", c=KC),
                                     ACT.Identity).then_inc(s_mixT_sb, 1)

        def mix_vector(dve):
            done = [0]

            def step(ins):
                done[0] += 1
                ins.then_inc(s_inv1, 1)
                dve.wait_ge(s_inv1, done[0])

            gate, gates = L1a["gate"], L1c["gates"]
            dve.wait_ge(s_gates, 1)
            dve.wait_ge(s_pv1, STEPS * TILES)
            dve.wait_ge(s_att, 2 * STEPS)
            step(nc.vector.tensor_scalar(gate, gate, 1.0, None, ALU.add))
            step(nc.vector.reciprocal(gates[:, 0, :], gate))
            step(nc.vector.tensor_scalar(gates[:, 1, :], gates[:, 0, :], -1.0, 1.0, ALU.mult, ALU.add))
            for t in range(NT):
                b, i = t // QT, t % QT
                mem = bank[t % 4][:, 0:HEADS1 * C].rearrange("p (m h c) -> p m h c", m=KC, h=HM)
                att = L1a["attended"][:, KC * b:KC * (b + 1), i, :, :]
                inv = L1c["inv"][:, t % 2, :, :]
                dve.wait_ge(s_memout, t + 1)
                step(nc.vector.reciprocal(inv[:, 0, :].rearrange("p (m h) -> p m h", m=KC), mem[:, :, :, DH1]))
                step(nc.vector.reciprocal(inv[:, 1, :].rearrange("p (m h) -> p m h", m=KC), att[:, :, :, DH1]))
                step(nc.vector.tensor_tensor(inv, inv, gates, ALU.mult))
                if t >= 2:
                    dve.wait_ge(s_mixT, t // 2)
                out = L1c["out"][:, t % 2, :, :].rearrange("p w (m h d) -> p w m h d", m=KC, h=HM)
                for w, src in ((0, mem), (1, att)):
                    scale = inv[:, w, :].rearrange("p (m h o) -> p m h o", m=KC, o=1).broadcast_to((P, KC, HM, DH1))
                    ins = nc.vector.tensor_tensor(out[:, w, :, :, :], src[:, :, :, 0:DH1], scale, ALU.mult)
                    ins.then_inc(s_mix_a if w == 0 else s_mix_b, 1)
                dve.wait_ge(s_mix_a, t + 1)
                dve.wait_ge(s_mix_b, t + 1)
                rows = L1c["out"][:, t % 2, :, :]
                nc.vector.tensor_tensor(rows[:, 0, :], rows[:, 0, :], rows[:, 1, :], ALU.add).then_inc(s_mix, 1)
                if t >= 7:
                    added(0)
            for r in range(1, NT // 2):
                added(r)

        def added(r):
            nc.vector.wait_ge(s_wo1, r + 1)
            rows = X[:, 2 * r:2 * r + 2, :]
            nc.vector.tensor_tensor(rows, bank[6 + r % 2][:, :].rearrange("p (t d) -> p t d", t=2), rows,
                                    ALU.add).then_inc(s_att_added, 1)

        F_FREE = 2048 + 1536 + 1024 + 136 + 16 + 512 + 2048 + 1024 + 1024 + 544 + 2048
        B1 = layout(farena, FWORDS, chunk=(3, KC * P), router=(KC, E1), pick=(FC, P))
        D1 = layout(farena, FWORDS, skip=(F_FREE,), silu=(2, SEQ), prod=(2, SEQ), hid=(2, SEQ), logit=(NT, 16),
                    found=(NT, 8), wanted=(NT, 8), left=(NT, 16), w=(NT, E1), total=(NT,))
        M1 = layout(rarena, M0_END, chunk_hi=(3, KC * P), chunk_lo=(3, KC * P), router_hi=(KC, E1),
                    router_lo=(KC, E1), pick=(P,), w_split=(NT, 2 * E1), wT=(TOKENS,), hid_hi=(2, SEQ), hid_lo=(2, SEQ))
        (s_m1_raw, s_m1_tmp, s_m1_router, s_logit1, s_lg, s_route1, s_ex1, s_exd1, s_split1, s_wT1_ps, s_wT1, s_pick2, s_gate1,
         s_up1, s_silu1, s_prod1, s_hid1, s_hid1_hi, s_hid1_lo, s_back1) = (sem(n) for n in (
             "s_m1_raw s_m1_tmp s_m1_router s_logit1 s_lg s_route1 s_ex1 s_exd1 s_split1 s_wT1_ps s_wT1 s_pick2 s_gate1 "
             "s_up1 s_silu1 s_prod1 s_hid1 s_hid1_hi s_hid1_lo s_back1").split())
        s_chunk_raw = [sem(f"s_chunk_raw{k}") for k in range(3)]
        s_chunk = [sem(f"s_chunk{k}") for k in range(3)]
        s_y1 = [sem(f"s_y1_{r}") for r in range(4)]
        GATE, UP, DOWN = range(3)
        ABSENT, TAKEN = -3.0e38, -3.2e38

        def chunk_load(sp, k, c, first=False):
            if not first:
                sp.wait_ge(s_chunk[k], c)
            sp.dma_start(B1["chunk"][:, k, :], a["m1_chunk"][:, bass.ds(c, 1), k, :]
                         .rearrange("p o n -> p (o n)")).then_inc(s_chunk_raw[k], 16)

        def mix1_loads(sp):
            sp.wait_ge(s_pv1, STEPS * TILES)
            sp.wait_ge(s_att, 2 * STEPS)
            sp.dma_start(B1["router"], a["m1_router"]).then_inc(s_m1_raw, 16)
            sp.dma_start(B1["pick"][0:2 * E1, :, :], a["m1_pick"]).then_inc(s_m1_raw, 16)
            for k in range(3):
                chunk_load(sp, k, 0, first=True)
            with sp.Fori(1, FC) as c:
                for k in range(3):
                    chunk_load(sp, k, c)

        def split_chunk(pool, k, c, used, first=False):
            pool.wait_ge(s_chunk_raw[k], 16 * (c + 1))
            if not first:
                pool.wait_ge(used, 2 * c)
            nc.gpsimd.tensor_tensor(M1["chunk_hi"][:, k, :], B1["chunk"][:, k, :], one(KC * P),
                                    ALU.mult).then_inc(s_m1_tmp, 1)
            pool.wait_ge(s_m1_tmp, 3 * c + k + 1)
            nc.gpsimd.tensor_tensor(M1["chunk_lo"][:, k, :], B1["chunk"][:, k, :], f(M1["chunk_hi"][:, k, :]),
                                    ALU.subtract).then_inc(s_chunk[k], 1)

        def mix1_pool(pool):
            pool.wait_ge(s_m1_raw, 32)
            flat = "p c e -> p (c e)"
            nc.gpsimd.tensor_tensor(M1["router_hi"].rearrange(flat), B1["router"].rearrange(flat), one(KC * E1),
                                    ALU.mult).then_inc(s_m1_router, 1)
            pool.wait_ge(s_m1_router, 1)
            nc.gpsimd.tensor_tensor(M1["router_lo"].rearrange(flat), B1["router"].rearrange(flat),
                                    f(M1["router_hi"].rearrange(flat)), ALU.subtract).then_inc(s_m1_router, 1)
            for k in range(3):
                split_chunk(pool, k, 0, None, first=True)

            def hid_lo(n, x, first=False):
                pool.wait_ge(s_hid1_hi, n + 1)
                if not first:
                    pool.wait_ge(s_back1, n - 1)
                nc.gpsimd.tensor_tensor(M1["hid_lo"][:, x, :], D1["hid"][:, x, :], f(M1["hid_hi"][:, x, :]),
                                        ALU.subtract).then_inc(s_hid1_lo, 1)

            def chunk(c, first=False, last=False):
                hid_lo(2 * c, 0, first)
                if not last:
                    split_chunk(pool, GATE, c + 1, s_gate1)
                    split_chunk(pool, UP, c + 1, s_up1)
                hid_lo(2 * c + 1, 1, first)
                if not last:
                    split_chunk(pool, DOWN, c + 1, s_back1)

            chunk(0, first=True)
            with pool.Fori(1, FC - 1) as c:
                chunk(c)
            chunk(FC - 1, last=True)

        def mix1_tensor(pe):
            pe.wait_ge(s_m1_router, 2)
            pe.wait_ge(s_mix_a, NT)
            for t in range(NT):
                k = 0
                for xs, ws in ((xnT_hi, "router_hi"), (xnT_hi, "router_lo"), (xnT_lo, "router_hi")):
                    for c in range(KC):
                        mm = nc.tensor.matmul(bank[2][:, t * E1:(t + 1) * E1], xs[:, c, t * P:(t + 1) * P],
                                              M1[ws][:, c, :], start=(k == 0), stop=(k == 2 * KC + 1))
                        k += 1
            mm.then_inc(s_logit1, 1)

            def terms(left, right):
                return ((left[0], right[0]), (left[0], right[1]), (left[1], right[0]))

            def projection(out, k, x):
                half = slice(x * SEQ, (x + 1) * SEQ)
                m = 0
                for w, v in terms((M1["chunk_hi"], M1["chunk_lo"]), (xnT_hi, xnT_lo)):
                    for c in range(KC):
                        mm = nc.tensor.matmul(out, w[:, k, c * P:(c + 1) * P], v[:, c, half], start=(m == 0),
                                              stop=(m == 2 * KC + 1))
                        m += 1
                return mm

            def gate_up(n, x, c, first=False):
                if x == 0:
                    pe.wait_ge(s_chunk[GATE], c + 1)
                if not first:
                    pe.wait_ge(s_silu1, n - 1)
                projection(bank[3 if x else 0][:, :], GATE, x).then_inc(s_gate1, 1)
                if x == 0:
                    pe.wait_ge(s_chunk[UP], c + 1)
                if not (first and x == 0):
                    pe.wait_ge(s_prod1, n)
                projection(bank[1][:, :], UP, x).then_inc(s_up1, 1)

            def weights(n, x, c, first=False):
                pe.wait_ge(s_pick2, c + 1)
                if not (first and x == 0):
                    pe.wait_ge(s_hid1, n)
                nc.tensor.matmul(bank[2][:, :], M1["pick"][0:2 * E1, :], M1["wT"][0:2 * E1, x * SEQ:(x + 1) * SEQ],
                                 start=True, stop=True).then_inc(s_ex1, 1)

            def back(n, x, c, last=False):
                pe.wait_ge(s_hid1_lo, n + 1)
                if x == 0:
                    pe.wait_ge(s_chunk[DOWN], c + 1)
                for i in range(QT):
                    r = 2 * x + i // 2
                    out = bank[4 + r][:, (i % 2) * D:(i % 2 + 1) * D]
                    for m, (h, w) in enumerate(terms((M1["hid_hi"], M1["hid_lo"]), (M1["chunk_hi"], M1["chunk_lo"]))):
                        mm = nc.tensor.matmul(out, h[:, x, i * P:(i + 1) * P], w[:, DOWN, :], start=False,
                                              stop=last and m == 2, skip_group_check=True)
                mm.then_inc(s_back1, 1)

            gate_up(0, 0, 0, first=True)
            pe.wait_ge(s_att_added, 4)
            for r in range(4):
                nc.tensor.matmul(bank[4 + r][:, :], zeros_bf[:, 0:P], zeros_bf[:, 0:SEQ], start=True, stop=False,
                                 skip_group_check=True)
            pe.wait_ge(s_split1, 2)
            pe.wait_ge(s_lg, 1)
            for t in range(NT):
                mm = nc.tensor.transpose(bank[2 if t < 4 else 3][0:2 * E1, (t % 4) * P:(t % 4 + 1) * P],
                                         f(M1["w_split"][:, t, :]), ident[:, :])
                if t % 4 == 3:
                    mm.then_inc(s_wT1_ps, 1)
            pe.wait_ge(s_wT1, 2)
            weights(0, 0, 0, first=True)
            gate_up(1, 1, 0, first=True)
            weights(1, 1, 0, first=True)
            back(0, 0, 0)
            with pe.Fori(1, FC) as c:
                gate_up(2 * c, 0, c)
                weights(2 * c, 0, c)
                back(2 * c - 1, 1, c - 1)
                gate_up(2 * c + 1, 1, c)
                weights(2 * c + 1, 1, c)
                back(2 * c, 0, c)
            back(2 * FC - 1, 1, FC - 1)

        def mix1_scalar(act):
            def silu(n, x, first=False):
                act.wait_ge(s_gate1, n + 1)
                if not first:
                    act.wait_ge(s_prod1, n - 1)
                nc.scalar.activation(D1["silu"][:, x, :], bank[3 if x else 0][:, :], ACT.Silu).then_inc(s_silu1, 1)

            def hid_hi(n, x, first=False):
                act.wait_ge(s_hid1, n + 1)
                if not first:
                    act.wait_ge(s_back1, n - 1)
                nc.scalar.activation(M1["hid_hi"][:, x, :], D1["hid"][:, x, :], ACT.Identity).then_inc(s_hid1_hi, 1)

            act.wait_ge(s_exd1, 1)
            nc.scalar.activation(D1["w"], D1["w"], ACT.Exp).then_inc(s_exd1, 1)
            silu(0, 0, first=True)
            for x in range(2):
                act.wait_ge(s_wT1_ps, x + 1)
                nc.scalar.activation(M1["wT"][0:2 * E1, x * SEQ:(x + 1) * SEQ], bank[2 + x][0:2 * E1, :],
                                     ACT.Identity).then_inc(s_wT1, 1)
            silu(1, 1, first=True)
            hid_hi(0, 0, first=True)
            hid_hi(1, 1, first=True)
            with act.Fori(1, FC) as c:
                for x in range(2):
                    silu(2 * c + x, x)
                    hid_hi(2 * c + x, x)

        def mix1_vector(dve):
            done = [0]

            def step(ins):
                done[0] += 1
                ins.then_inc(s_route1, 1)
                dve.wait_ge(s_route1, done[0])

            logit, found, wanted, left, w, total = (D1[n] for n in ("logit", "found", "wanted", "left", "w", "total"))

            def wide(v):
                return v.broadcast_to((P, NT, E1))

            step(nc.vector.memset(logit[:, :, E1:16], ABSENT))
            step(nc.vector.memset(wanted, ABSENT))
            dve.wait_ge(s_logit1, 1)
            nc.vector.tensor_copy(logit[:, :, 0:E1], bank[2][:, 0:NT * E1].rearrange("p (t e) -> p t e", t=NT)).then_inc(s_lg, 1)
            dve.wait_ge(s_lg, 1)
            for t in range(NT):
                step(nc.vector.max(found[:, t, :], logit[:, t, 0:E1]))
            step(nc.vector.tensor_copy(wanted[:, :, 0:2], found[:, :, 0:2]))
            for t in range(NT):
                step(nc.vector.match_replace(left[:, t, 0:14], wanted[:, t, :], logit[:, t, 0:14], TAKEN))
            dve.wait_ge(s_exp1, CHUNKS)
            nc.vector.tensor_tensor(w, logit[:, :, 0:E1], wide(found[:, :, 0:1]), ALU.subtract).then_inc(s_exd1, 1)
            step(nc.vector.tensor_tensor(left[:, :, 0:E1], left[:, :, 0:E1], logit[:, :, 0:E1], ALU.not_equal))
            dve.wait_ge(s_exd1, 2)
            step(nc.vector.tensor_tensor(w, w, left[:, :, 0:E1], ALU.mult))
            step(nc.vector.tensor_reduce(total, w, X_AXIS, ALU.add))
            step(nc.vector.reciprocal(total, total))
            step(nc.vector.tensor_tensor(w, w, wide(total.rearrange("p (t o) -> p t o", o=1)), ALU.mult))
            nc.vector.tensor_copy(M1["w_split"][:, :, 0:E1], w).then_inc(s_split1, 1)
            dve.wait_ge(s_split1, 1)
            nc.vector.tensor_tensor(M1["w_split"][:, :, E1:2 * E1], w, f(M1["w_split"][:, :, 0:E1]),
                                    ALU.subtract).then_inc(s_split1, 1)

            def pick(c):
                nc.vector.tensor_scalar(M1["pick"][0:2 * E1, :],
                                        B1["pick"][0:2 * E1, bass.ds(c, 1), :].rearrange("p o n -> p (o n)"),
                                        1.0, None, ALU.mult).then_inc(s_pick2, 1)

            def hidden(n, x, first=False):
                dve.wait_ge(s_silu1, n + 1)
                dve.wait_ge(s_up1, n + 1)
                if not first:
                    dve.wait_ge(s_hid1, n - 1)
                nc.vector.tensor_tensor(D1["prod"][:, x, :], bank[1][:, :], D1["silu"][:, x, :], ALU.mult).then_inc(s_prod1, 1)
                dve.wait_ge(s_ex1, n + 1)
                dve.wait_ge(s_prod1, n + 1)
                if not first:
                    dve.wait_ge(s_hid1_lo, n - 1)
                nc.vector.tensor_tensor(D1["hid"][:, x, :], bank[2][:, :], D1["prod"][:, x, :], ALU.mult).then_inc(s_hid1, 1)

            dve.wait_ge(s_m1_raw, 32)
            pick(0)
            hidden(0, 0, first=True)
            hidden(1, 1, first=True)
            with dve.Fori(1, FC) as c:
                pick(c)
                hidden(2 * c, 0)
                hidden(2 * c + 1, 1)
            for r in range(4):
                dve.wait_ge(s_back1, 2 * FC - 1 + r // 2)
                rows = X[:, 2 * r:2 * r + 2, :]
                nc.vector.tensor_tensor(rows, bank[4 + r][:, :].rearrange("p (t d) -> p t d", t=2), rows,
                                        ALU.add).then_inc(s_y1[r], 1)

        consts = [(ident, "ident"), (mask_neg, "mask_neg"), (ident_bf, "ident_bf"), (bias_qkv, "bias_qkv"),
                  (scale0, "scale0")]
        N_CONST = len(consts) + 1
        s_out = sem("s_out")

        block = ctx.enter_context(nc.Block())

        @block.sync
        def _(sp):
            for i in range(2):
                sp.dma_start(X[:, 4 * i:4 * i + 4, :], a["x"][:, 4 * i:4 * i + 4, :]).then_inc(s_x[i], 16)
            for dst, name in consts:
                sp.dma_start(dst[:], a[name]).then_inc(s_const, 16)
            sp.dma_start(bo_row[:], a["b_o"].broadcast_to((P, D))).then_inc(s_const, 16)
            attn_loads(sp, 0, first=True)
            with sp.Fori(1, GROUPS) as g:
                attn_loads(sp, g)
            mix0_loads(sp)
            for e in range(RING):
                expert_loads(sp, e, e, first=True)
            l1_loads(sp)
            with sp.Fori(1, E0 // RING) as k:
                for par in range(RING):
                    expert_loads(sp, RING * k + par, par)
            l1_pick_load(sp)
            mix1_loads(sp)
            for r in range(4):
                sp.wait_ge(s_y1[r], 1)
                sp.dma_start(a["out"][:, 2 * r:2 * r + 2, :], X[:, 2 * r:2 * r + 2, :]).then_inc(s_out, 16)
            sp.wait_ge(s_out, 64)

        @block.tensor
        def _(pe):
            norm_tensor(pe, 0)
            pe.wait_ge(s_xnl, 4)
            for u in range(UNITS):
                attn_tensor_slot(pe, 0, u, first=True)
            with pe.Fori(1, GROUPS) as g:
                for u in range(UNITS):
                    attn_tensor_slot(pe, g, u)
            mix0_logits()
            mix0_latent(0)
            attn_tensor_slot(pe, GROUPS, 0, tail=True)
            mix0_latent(1)
            for x in range(2):
                attn_tensor_slot(pe, GROUPS, 1 + x, tail=True, steps=(0,))
                mix0_shared(x, 1)
                attn_tensor_slot(pe, GROUPS, 1 + x, tail=True, steps=(1,))
                mix0_shared(x, 0)
                attn_tensor_slot(pe, GROUPS, 1 + x, tail=True, steps=(2, 3))
            mix0_turn_weights()
            attn_tensor_slot(pe, GROUPS, 3, tail=True, steps=(0,))
            mix0_tensor(pe)
            norm_tensor(pe, 1)
            l1_tensor_project(pe)
            l1_run(pe, l1_tensor_slot)
            mix_tensor(pe)
            mix1_tensor(pe)

        @block.scalar
        def _(act):
            norm_scalar(act, 0)
            act.wait_ge(s_bk, 1)
            for u in range(UNITS):
                attn_scalar_slot(act, 0, u, first=True)
            with act.Fori(1, GROUPS) as g:
                for u in range(UNITS):
                    attn_scalar_slot(act, g, u)
            mix0_sigmoid()
            mix0_latent_hi(0)
            attn_scalar_slot(act, GROUPS, 0, tail=True)
            mix0_latent_hi(1)
            for x in range(2):
                attn_scalar_slot(act, GROUPS, 1 + x, tail=True, steps=(0, 1))
                mix0_shared_relu(x)
                attn_scalar_slot(act, GROUPS, 1 + x, tail=True, steps=(2, 3))
            attn_scalar_slot(act, GROUPS, 3, tail=True)
            mix0_weights_out()
            mix0_scalar(act)
            norm_scalar(act, 1)
            l1_scalar_project(act)
            act.wait_ge(s_ones, 2)
            l1_run(act, l1_scalar_slot)
            mix_scalar(act)
            mix1_scalar(act)

        @block.vector
        def _(dve):
            norm_vector(dve, 0)
            dve.wait_ge(s_const, 16 * N_CONST)
            nc.vector.tensor_scalar(bias_qkv[:, 1, :], bias_qkv[:, 1, :], scale0[:, 0:1], None, ALU.mult).then_inc(s_bk, 1)
            dve.wait_ge(s_bk, 1)
            nc.vector.tensor_copy(bias_now[:, 0, :], bias_qkv[:, :, 0]).then_inc(s_bias, 1)
            for u in range(UNITS):
                attn_vector_slot(dve, 0, u, first=True)
            with dve.Fori(1, GROUPS) as g:
                for u in range(UNITS):
                    attn_vector_slot(dve, g, u)
            mix0_choose(dve)
            mix0_latent_lo(0)
            attn_vector_slot(dve, GROUPS, 0, tail=True)
            mix0_latent_lo(1)
            mix0_route(dve)
            for x in range(2):
                attn_vector_slot(dve, GROUPS, 1 + x, tail=True)
                mix0_shared_prod(x)
            attn_vector_slot(dve, GROUPS, 3, tail=True, steps=(0,))
            mix0_vector(dve)
            norm_vector(dve, 1)
            l1_vector_project(dve)
            dve.wait_ge(s_ones, 2)
            l1_run(dve, l1_vector_slot)
            mix_vector(dve)
            mix1_vector(dve)

        @block.gpsimd
        def _(pool):
            pool.wait_ge(s_const, 16 * N_CONST)
            attn_pool_early(pool, 0, first=True)
            with pool.Fori(0, GROUPS - 1) as g:
                attn_pool_late(pool, g)
                attn_pool_early(pool, g + 1)
            attn_pool_late(pool, GROUPS - 1, ahead=False)
            normalise(pool, GROUPS, 0)
            mix0_pool(pool)
            l1_pool_project(pool)
            mix1_pool(pool)


def kernel(**inputs):
    import numpy as np
    import concourse.bacc as bacc
    from concourse.bass_utils import run_bass_kernel_spmd

    def get(name):
        return np.asarray(inputs[name])

    bf16 = mybir.dt.np(BF16)
    wq, wk = get("L0_attn_W_Q"), get("L0_attn_W_K")
    wqk = np.stack([wq, wk], 1).reshape(HEADS0, 2, KC, P, DH0).transpose(0, 3, 1, 2, 4)
    wv = get("L0_attn_W_V").reshape(GROUPS, GROUP, KC, P, DH0).transpose(0, 3, 2, 1, 4)
    wo = get("L0_attn_W_O").reshape(GROUPS, GROUP, DH0, D).transpose(0, 2, 1, 3)
    bias = np.stack([get("L0_attn_b_Q"), get("L0_attn_b_K"), get("L0_attn_b_V")]).transpose(2, 0, 1)
    arrays = {
        "x": get("L0_attn_x").reshape(NT, P, D).transpose(1, 0, 2),
        "w_qk": wqk.reshape(HEADS0, P, 2 * KC * DH0),
        "w_v": wv.reshape(GROUPS, P, KC * GROUP * DH0),
        "w_o": wo.reshape(GROUPS, P, GROUP * D),
        "bias_qkv": bias,
        "b_o": get("L0_attn_b_O").reshape(1, D),
        "ident": np.eye(P, dtype=np.float32),
        "ident_bf": np.eye(P, dtype=np.float32).astype(bf16),
        "mask_neg": np.triu(np.full((P, P), MASKED, np.float32), 1).astype(bf16),
        "scale0": np.tile(np.array([[DH0 ** -0.5, 1.0]], np.float32), (P, 1)),
    }
    arrays |= {
        "m0_router": get("L0_ffn_Wg").T.reshape(KC, P, E0).transpose(1, 0, 2),
        "m0_down": get("L0_ffn_Wdown").T.reshape(KC, P, LAT).transpose(1, 0, 2),
        "m0_gate_up": np.stack([get("L0_ffn_sw1"), get("L0_ffn_swg")]).transpose(0, 2, 1)
        .reshape(2, KC, P, HID).transpose(2, 0, 1, 3),
        "m0_shared_out": get("L0_ffn_sw2").T,
        "m0_lat_up": get("L0_ffn_Wup").T,
        "m0_pick": np.tile(np.repeat(np.eye(E0, dtype=np.float32)[:, :, None], P, 2), (2, 1, 1)),
        "m0_bias": get("L0_ffn_biases").reshape(1, E0),
        "m0_expert": np.stack([get("L0_ffn_rw1"), get("L0_ffn_rwg")], 1).transpose(3, 0, 1, 2).reshape(LAT, E0, 2 * HID),
        "m0_expert_out": get("L0_ffn_rw2").transpose(2, 0, 1),
    }
    def rows(w):
        return w.reshape(KC, P, -1).transpose(1, 0, 2)

    freq = (np.float32(1.0) / np.float32(10000.0) ** (np.arange(0, D, 2, dtype=np.float32) / np.float32(D))).astype(np.float32)
    angle = (np.arange(SEQ, dtype=np.float32)[:, None] * freq[None, :]).astype(np.float32).T
    pick = np.zeros((P, 4, 4, P), np.float32)
    for pr in range(4):
        for kind, parts in enumerate(((0, 1), (2, 3), (0, 2), (1, 3))):
            for j in range(2):
                for part in parts:
                    for d in range(DH1):
                        pick[DH1 * (2 * pr + j) + d, pr, kind, 64 * j + DH1 * part + d] = DH1 ** -0.5 if kind < 2 else 1.0
    arrays |= {
        "l1_w": np.stack([rows(get(n).T) for n in ("L1_attn_Wq", "L1_attn_Wk", "L1_attn_Wv")], 1),
        "l1_cos": np.cos(angle),
        "l1_sin": np.sin(angle),
        "l1_blocks": np.repeat(np.repeat(np.eye(HM, dtype=np.float32), DH1, 0)[:, :, None], DH1 + 1, 2),
        "l1_gate": get("L1_attn_gate").reshape(1, HEADS1),
        "l1_w_out": rows(get("L1_attn_Wo").T),
        "l1_pick": pick,
    }
    expert_of = np.repeat(np.eye(E1, dtype=np.float32), F1, 1).reshape(E1, FC, P)
    gate = get("L1_ffn_gate_proj").reshape(FC, P, KC, P).transpose(3, 0, 2, 1)
    up = get("L1_ffn_up_proj").reshape(FC, P, KC, P).transpose(3, 0, 2, 1)
    down = get("L1_ffn_down_proj").transpose(0, 2, 1).reshape(FC, P, D).transpose(1, 0, 2)
    arrays |= {
        "m1_router": rows(get("L1_ffn_gate_w").T),
        "m1_pick": np.tile(expert_of, (2, 1, 1)),
        "m1_chunk": np.stack([gate.reshape(P, FC, KC * P), up.reshape(P, FC, KC * P), down], 2),
    }
    nc = bacc.Bacc("TRN2", target_bir_lowering=False, num_devices=1)
    aps, feed = {}, {}
    for name, v in arrays.items():
        v = np.ascontiguousarray(v)
        feed[f"in_{name}"] = v
        aps[name] = nc.dram_tensor(f"in_{name}", v.shape, mybir.dt.from_np(v.dtype), kind="ExternalInput").ap()
    aps["out"] = nc.dram_tensor("out_x", (P, NT, D), F32, kind="ExternalOutput").ap()
    program(nc, aps)
    r = run_bass_kernel_spmd(nc, [feed], core_ids=[0])
    got = np.asarray(r.results[0]["out_x"])
    return np.ascontiguousarray(got.transpose(1, 0, 2).reshape(BATCH, SEQ, D))
```

```python
from contextlib import ExitStack

import concourse.bass as bass
from concourse import mybir


F32 = mybir.dt.float32
F32R = mybir.dt.float32r
BF16 = mybir.dt.bfloat16
ALU = mybir.AluOpType
ACT = mybir.ActivationFunctionType
X_AXIS = mybir.AxisListType.X

P = 128
D = 256
KC = D // P
BATCH, SEQ = 2, 512
TOKENS = BATCH * SEQ
NT = TOKENS // P
QT = SEQ // P
EPS = 1e-5

HEADS0, DH0 = 16, 128
GROUP = 4
GROUPS = HEADS0 // GROUP
UNITS = BATCH * GROUP
TRI = QT * (QT + 1) // 2 * P
MASKED = -1e5

E0, TOP0, LAT, HID = 16, 8, 64, 128
ROUTE_SCALE = 2.5

HEADS1, DH1 = 16, 16
HM = P // DH1
VW = 32

E1, F1 = 8, 176
FC = E1 * F1 // P


def program(nc, a):
    with ExitStack() as ctx:
        def sb(name, shape, dt):
            return ctx.enter_context(nc.sbuf_tensor(name, shape, dt))

        def sem(name):
            return ctx.enter_context(nc.semaphore(name))

        bank = [ctx.enter_context(nc.psum_tensor(f"bank{i}", [P, 512], F32)) for i in range(8)]

        X = sb("X", [P, NT, D], F32)
        xnT_hi = sb("xnT_hi", [P, KC, TOKENS], F32R)
        xnT_lo = sb("xnT_lo", [P, KC, TOKENS], F32R)
        ident = sb("ident", [P, P], F32)
        small = sb("small", [P, 512], F32)
        bo_row = sb("bo_row", [P, D], F32)

        FWORDS, RWORDS = 18944, 26624
        farena = sb("farena", [P, FWORDS], F32)
        rarena = sb("rarena", [P, RWORDS], F32R)

        def layout(arena, limit, **shapes):
            at, views = 0, {}
            for name, shape in shapes.items():
                n = 1
                for s in shape:
                    n *= s
                v = arena[:, at:at + n]
                if len(shape) == 2:
                    v = v.rearrange("p (a b) -> p a b", a=shape[0])
                elif len(shape) == 3:
                    v = v.rearrange("p (a b c) -> p a b c", a=shape[0], b=shape[1])
                elif len(shape) == 4:
                    v = v.rearrange("p (a b c d) -> p a b c d", a=shape[0], b=shape[1], c=shape[2])
                views[name] = v
                at += n
            assert at <= limit, (at, limit)
            return views

        def f(v):
            return v.bitcast(F32)

        stats = small[:, 0:48].rearrange("p (t s) -> p t s", t=NT)
        mean_var = small[:, 48:64].rearrange("p (t s) -> p t s", t=NT)
        std = small[:, 64:72]
        rstd = small[:, 72:80]
        s_x = [sem(f"s_x{i}") for i in range(2)]
        s_const = sem("s_const")
        s_stats, s_aggr, s_eps, s_std, s_rstd = (sem(n) for n in ("s_stats", "s_aggr", "s_eps", "s_std", "s_rstd"))
        s_xn, s_xnt, s_xnh, s_xnl = (sem(n) for n in ("s_xn", "s_xnt", "s_xnh", "s_xnl"))
        xn = layout(farena, FWORDS, skip=(FWORDS - NT * D,), xn=(NT, D))["xn"]

        def norm_variance(dve, n, h):
            tiles = slice(QT * h, QT * (h + 1))
            for t in range(QT * h, QT * (h + 1)):
                dve.wait_ge(s_stats, NT * n + t + 1)
                nc.vector.bn_aggr(mean_var[:, t, :], stats[:, t, :]).then_inc(s_aggr, 1)
            dve.wait_ge(s_aggr, NT * n + QT * (h + 1))
            nc.vector.tensor_scalar(std[:, tiles], mean_var[:, tiles, 1], EPS, None, ALU.add).then_inc(s_eps, 1)

        def norm_rows(dve, n, h):
            dve.wait_ge(s_std, 2 * n + h + 1)
            tiles = slice(QT * h, QT * (h + 1))
            nc.vector.reciprocal(rstd[:, tiles], std[:, tiles]).then_inc(s_rstd, 1)
            dve.wait_ge(s_rstd, 2 * n + h + 1)
            for t in range(QT * h, QT * (h + 1)):
                nc.vector.tensor_scalar(xn[:, t, :], X[:, t, :], mean_var[:, t, 0:1], rstd[:, t:t + 1],
                                        ALU.subtract, ALU.mult).then_inc(s_xn, 1)

        def norm_lo(dve, n, h):
            for r in (2 * h, 2 * h + 1):
                dve.wait_ge(s_xnh, 4 * n + r + 1)
                nc.vector.tensor_tensor(xnT_lo[:, :, 2 * P * r:2 * P * (r + 1)],
                                        bank[r][:, :].rearrange("p (c t) -> p c t", c=KC),
                                        f(xnT_hi[:, :, 2 * P * r:2 * P * (r + 1)]),
                                        ALU.subtract).then_inc(s_xnl, 1)

        def norm_vector(dve, n):
            for h in range(BATCH):
                for r in (2 * h, 2 * h + 1):
                    if n == 0:
                        dve.wait_ge(s_x[h], 16)
                    else:
                        dve.wait_ge(s_out0, r + 1)
                        rows = X[:, 2 * r:2 * r + 2, :]
                        nc.vector.tensor_tensor(rows, bank[r][:, :].rearrange("p (t d) -> p t d", t=2), rows,
                                                ALU.add).then_inc(s_out0_added, 1)
                        dve.wait_ge(s_out0_added, r + 1)
                    for t in (2 * r, 2 * r + 1):
                        nc.vector.bn_stats(stats[:, t, :], X[:, t, :]).then_inc(s_stats, 1)
                if n == 1 and h == 0:
                    norm_variance(dve, n, 0)
            if n == 0:
                norm_variance(dve, n, 0)
            norm_variance(dve, n, 1)
            norm_rows(dve, n, 0)
            if n == 1:
                norm_lo(dve, n, 0)
            norm_rows(dve, n, 1)
            if n == 0:
                norm_lo(dve, n, 0)

        def norm_scalar(act, n):
            for h in range(BATCH):
                tiles = slice(QT * h, QT * (h + 1))
                act.wait_ge(s_eps, 2 * n + h + 1)
                nc.scalar.activation(std[:, tiles], std[:, tiles], ACT.Sqrt).then_inc(s_std, 1)

        def norm_hi(act, n, h):
            for r in (2 * h, 2 * h + 1):
                act.wait_ge(s_xnt, 4 * n + r + 1)
                nc.scalar.activation(xnT_hi[:, :, 2 * P * r:2 * P * (r + 1)],
                                     bank[r][:, :].rearrange("p (c t) -> p c t", c=KC),
                                     ACT.Identity).then_inc(s_xnh, 1)

        def norm_tensor(pe, n, h):
            if n == 0:
                pe.wait_ge(s_const, 16 * N_CONST)
            for r in (2 * h, 2 * h + 1):
                pe.wait_ge(s_xn, NT * n + 2 * r + 2)
                for c in range(KC):
                    for t in range(2):
                        mm = nc.tensor.transpose(bank[r][:, (2 * c + t) * P:(2 * c + t + 1) * P],
                                                 xn[:, 2 * r + t, c * P:(c + 1) * P], ident[:, :])
                mm.then_inc(s_xnt, 1)

        A = layout(farena, FWORDS, wqk_raw=(GROUP, 2, KC, P), wv_raw=(KC, GROUP * P), wo_raw=(GROUP, D),
                   k_scaled=(KC * P,), prob=(4, TRI))
        wqk_raw, wv_raw, wo_raw = A["wqk_raw"], A["wv_raw"], A["wo_raw"]
        k_scaled, prob = A["k_scaled"], A["prob"]
        R = layout(rarena, RWORDS, wqk_hi=(GROUP, 2, KC, P), wqk_lo=(GROUP, 2, KC, P),
                   wv_hi=(KC, GROUP * P), wv_lo=(KC, GROUP * P), wo_hi=(GROUP, D), wo_lo=(GROUP, D),
                   qk_hi=(2, 2, SEQ), qk_lo=(2, 2, SEQ), v_hi=(BATCH, QT, GROUP * P), v_lo=(BATCH, QT, GROUP * P),
                   pT_hi=(2, SEQ), pT_lo=(2, SEQ), zT_hi=(GROUP, SEQ), zT_lo=(GROUP, SEQ))
        wqk_hi, wqk_lo, wv_hi, wv_lo, wo_hi, wo_lo = (R[n] for n in ("wqk_hi", "wqk_lo", "wv_hi", "wv_lo", "wo_hi", "wo_lo"))
        qk_hi, qk_lo, v_hi, v_lo = (R[n] for n in ("qk_hi", "qk_lo", "v_hi", "v_lo"))
        pT_hi, pT_lo, zT_hi, zT_lo = (R[n] for n in ("pT_hi", "pT_lo", "zT_hi", "zT_lo"))
        bias_qkv = sb("bias_qkv", [P, 3, HEADS0], F32)
        scale0 = sb("scale0", [P, 2], F32)
        mask_neg = sb("mask_neg", [P, P], BF16)
        ident_bf = sb("ident_bf", [P, P], BF16)
        neg_max = small[:, 80:84]
        bias_now = small[:, 120:144].rearrange("p (u w) -> p u w", u=UNITS)
        row_sum = small[:, 84:92].rearrange("p (a b) -> p a b", a=2)
        row_inv = small[:, 92:100].rearrange("p (a b) -> p a b", a=2)

        s_wqk_raw = [sem(f"s_wqk_raw{h}") for h in range(GROUP)]
        s_wv_raw, s_wo_raw = sem("s_wv_raw"), sem("s_wo_raw")
        s_wtmp, s_wqk, s_wv, s_wo, s_bk = (sem(n) for n in ("s_wtmp", "s_wqk", "s_wv", "s_wo", "s_bk"))
        s_proj, s_proj_hi, s_proj_lo = (sem(n) for n in ("s_proj", "s_proj_hi", "s_proj_lo"))
        s_score, s_max, s_exp, s_inv, s_prob = (sem(n) for n in ("s_score", "s_max", "s_exp", "s_inv", "s_prob"))
        s_pT, s_pT_hi, s_pT_lo = (sem(n) for n in ("s_pT", "s_pT_hi", "s_pT_lo"))
        s_pv, s_z_hi, s_z_lo, s_y, s_y_added = (sem(n) for n in ("s_pv", "s_z_hi", "s_z_lo", "s_y", "s_y_added"))
        s_bo = sem("s_bo")
        s_bias = sem("s_bias")
        score_bank, pT_bank, proj_bank, z_bank, y_bank = bank[0:2], bank[2:4], bank[4:6], bank[6], bank[7]

        SCORED, TURNED, FINISHED = 1, 3, 4
        DEPTH = FINISHED + 1

        def jobs(u):
            return {0: [("q", 0, 0), ("k", 0, 2), ("v", 0, 3)],
                    1: [("q", 0, 0), ("v", 1, 1), ("k", 0, 2), ("v", 2, 3)],
                    2: [("q", 0, 0), ("v", 3, 1), ("k", 0, 2)],
                    3: [("q", 0, 0), ("k", 0, 2)]}[u % GROUP]

        JOBS = [(u, *job) for u in range(UNITS) for job in jobs(u)]
        NJ = len(JOBS)

        def job_number(u, kind, i=0):
            return next(n for n, j in enumerate(JOBS) if (j[0], j[1], j[2]) == (u, kind, i))

        def last_value_job(b):
            return job_number(GROUP * b + 2, "v", QT - 1)

        def slot_jobs(u, step):
            return [(n, kind, i) for n, (uu, kind, i, s) in enumerate(JOBS) if uu == u and s == step]

        def back(g, u, k):
            return (g, u - k) if u >= k else (g - 1, u - k + UNITS)

        def tri(i):
            return P * i * (i + 1) // 2

        def attn_tensor_slot(pe, g, u, first=False, tail=False, steps=range(QT)):
            has = [not tail or k > u for k in range(DEPTH)] if not first else [u >= k for k in range(DEPTH)]

            def unit(k):
                gg, uu = back(g, u, k)
                return gg, uu, UNITS * gg + uu

            def value_product(k, kt):
                gg, uu, v = unit(k)
                b, h = uu // GROUP, uu % GROUP
                pe.wait_ge(s_pT_lo, QT * v + kt + 1)
                if kt == 0:
                    pe.wait_ge(s_z_lo, v)
                    pe.wait_ge(s_proj_lo, NJ * gg + last_value_job(b) + 1)
                n = kt % 2
                w = SEQ - kt * P
                hs = slice(h * P, (h + 1) * P)
                out = z_bank[:, kt * P:SEQ]
                nc.tensor.matmul(out, v_hi[:, b, kt, hs], pT_hi[:, n, 0:w], start=(kt == 0), stop=False)
                nc.tensor.matmul(out, v_hi[:, b, kt, hs], pT_lo[:, n, 0:w], start=False, stop=False)
                nc.tensor.matmul(out, v_lo[:, b, kt, hs], pT_hi[:, n, 0:w], start=False,
                                 stop=(kt == QT - 1)).then_inc(s_pv, 1)

            def output_product(gg, b, pair):
                n = 2 * (BATCH * gg + b) + pair
                if pair == 0:
                    pe.wait_ge(s_wo, 2 * (gg + 1))
                pe.wait_ge(s_z_lo, UNITS * gg + GROUP * (b + 1))
                pe.wait_ge(s_y_added, n)
                for t in range(2):
                    i = 2 * pair + t
                    ts = slice(i * P, (i + 1) * P)
                    for h in range(GROUP):
                        out = y_bank[:, t * D:(t + 1) * D]
                        nc.tensor.matmul(out, zT_hi[:, h, ts], wo_hi[:, h, :], start=(h == 0), stop=False)
                        nc.tensor.matmul(out, zT_hi[:, h, ts], wo_lo[:, h, :], start=False, stop=False)
                        mm = nc.tensor.matmul(out, zT_lo[:, h, ts], wo_hi[:, h, :], start=False,
                                              stop=(h == GROUP - 1))
                mm.then_inc(s_y, 1)

            for i in steps:
                if has[TURNED]:
                    gg, uu, v = unit(TURNED)
                    pe.wait_ge(s_prob, QT * (v + 1))
                    if not (first and u == TURNED and i < 2):
                        pe.wait_ge(s_pT_lo, QT * v + i - 1)
                    for q in range(i, QT):
                        mm = nc.tensor.transpose(pT_bank[i % 2][:, (q - i) * P:(q - i + 1) * P],
                                                 prob[:, uu % 4, tri(q) + i * P:tri(q) + (i + 1) * P], ident[:, :])
                    mm.then_inc(s_pT, 1)
                if has[SCORED]:
                    gg, uu, v = unit(SCORED)
                    if i == 0:
                        pe.wait_ge(s_proj_lo, NJ * gg + job_number(uu, "k") + 1)
                    if not (first and u == SCORED and i < 2):
                        pe.wait_ge(s_exp, QT * v + i - 1)
                    w = (i + 1) * P
                    par = uu % 2
                    qs = slice(i * P, (i + 1) * P)
                    out = score_bank[i % 2]
                    nc.tensor.matmul(out[:, 0:w], qk_hi[:, par, 0, qs], qk_hi[:, par, 1, 0:w], start=True, stop=False)
                    nc.tensor.matmul(out[:, i * P:w], ident_bf[:, :], mask_neg[:, :], start=False, stop=False)
                    nc.tensor.matmul(out[:, 0:w], qk_hi[:, par, 0, qs], qk_lo[:, par, 1, 0:w], start=False, stop=False)
                    nc.tensor.matmul(out[:, 0:w], qk_lo[:, par, 0, qs], qk_hi[:, par, 1, 0:w], start=False,
                                     stop=True).then_inc(s_score, 1)
                if i == 0 and has[FINISHED]:
                    value_product(FINISHED, QT - 1)
                if has[0]:
                    for n, kind, j in slot_jobs(u, i):
                        if not (first and n < 2):
                            pe.wait_ge(s_proj_lo, NJ * g + n - 1)
                        out = proj_bank[n % 2][:, :]
                        b, h = u // GROUP, u % GROUP
                        if kind == "v":
                            pe.wait_ge(s_wv, 2 * (g + 1))
                            tok = slice((QT * b + j) * P, (QT * b + j + 1) * P)
                            terms = [(xh[:, c, tok], wh[:, c, :]) for xh, wh in
                                     ((xnT_hi, wv_hi), (xnT_hi, wv_lo), (xnT_lo, wv_hi)) for c in range(KC)]
                        else:
                            pe.wait_ge(s_wqk, GROUP * g + h + 1)
                            tok = slice(SEQ * b, SEQ * (b + 1))
                            w = 0 if kind == "q" else 1
                            terms = [(wh[:, h, w, c, :], xh[:, c, tok]) for wh, xh in
                                     ((wqk_hi, xnT_hi), (wqk_hi, xnT_lo), (wqk_lo, xnT_hi)) for c in range(KC)]
                        for m, (lhs, rhs) in enumerate(terms):
                            mm = nc.tensor.matmul(out, lhs, rhs, start=(m == 0), stop=(m == len(terms) - 1))
                        mm.then_inc(s_proj, 1)
                if i >= 1 and has[TURNED]:
                    value_product(TURNED, i - 1)
                if u % GROUP == GROUP - 1 and i >= 2 and has[FINISHED]:
                    gg, uu, _ = unit(FINISHED)
                    output_product(gg, uu // GROUP, i - 2)

        def attn_scalar_slot(act, g, u, first=False, tail=False, steps=range(QT)):
            has = [not tail or k > u for k in range(DEPTH)] if not first else [u >= k for k in range(DEPTH)]

            def unit(k):
                gg, uu = back(g, u, k)
                return gg, uu, UNITS * gg + uu

            for i in steps:
                if has[TURNED]:
                    gg, uu, v = unit(TURNED)
                    act.wait_ge(s_pT, QT * v + i + 1)
                    if not (first and u == TURNED and i < 2):
                        act.wait_ge(s_pv, QT * v + i - 1)
                    w = SEQ - i * P
                    nc.scalar.activation(pT_hi[:, i % 2, 0:w], pT_bank[i % 2][:, 0:w], ACT.Identity).then_inc(s_pT_hi, 1)
                if has[SCORED]:
                    gg, uu, v = unit(SCORED)
                    act.wait_ge(s_max, QT * v + i + 1)
                    if not first or u >= 5:
                        act.wait_ge(s_pT, QT * (v - 3))
                    w = (i + 1) * P
                    nc.scalar.activation(prob[:, uu % 4, tri(i):tri(i) + w], score_bank[i % 2][:, 0:w], ACT.Exp,
                                         bias=neg_max[:, i:i + 1],
                                         accum_out=row_sum[:, uu % 2, i:i + 1]).then_inc(s_exp, 1)
                if i == 0 and has[FINISHED]:
                    gg, uu, v = unit(FINISHED)
                    act.wait_ge(s_pv, QT * (v + 1))
                    if not first or uu >= GROUP:
                        act.wait_ge(s_y, 2 * (BATCH * gg + uu // GROUP))
                    nc.scalar.activation(zT_hi[:, uu % GROUP, :], z_bank[:, :], ACT.Identity,
                                         bias=bias_now[:, uu, 2:3]).then_inc(s_z_hi, 1)
                if has[0]:
                    for n, kind, j in slot_jobs(u, i):
                        act.wait_ge(s_proj, NJ * g + n + 1)
                        b, h = u // GROUP, u % GROUP
                        out, bias = job_target(u, kind, j, qk_hi, v_hi), 0.0
                        if kind == "v":
                            if not first:
                                act.wait_ge(s_pv, QT * (UNITS * g - (GROUP if b == 0 else 0)))
                        else:
                            if not first or u >= 2:
                                act.wait_ge(s_score, QT * (UNITS * g + u - 1))
                            act.wait_ge(s_bias, UNITS * g + u + 1)
                            bias = bias_now[:, u, 0:1] if kind == "q" else bias_now[:, u, 1:2]
                        nc.scalar.activation(out, proj_bank[n % 2][:, :], ACT.Identity, bias=bias).then_inc(s_proj_hi, 1)

        def job_target(u, kind, j, qk, v):
            return v[:, u // GROUP, j, :] if kind == "v" else qk[:, u % 2, 0 if kind == "q" else 1, :]

        def attn_vector_slot(dve, g, u, first=False, tail=False, steps=range(QT)):
            has = [not tail or k > u for k in range(DEPTH)] if not first else [u >= k for k in range(DEPTH)]

            def unit(k):
                gg, uu = back(g, u, k)
                return gg, uu, UNITS * gg + uu

            if has[0] and not (first and u == 0):
                nc.vector.tensor_copy(bias_now[:, u, :], bias_qkv[:, :, bass.ds(GROUP * g + u % GROUP, 1)]
                                      .rearrange("p w o -> p (w o)")).then_inc(s_bias, 1)
            for i in steps:
                if has[SCORED]:
                    gg, uu, v = unit(SCORED)
                    dve.wait_ge(s_score, QT * v + i + 1)
                    if not (first and u == SCORED):
                        dve.wait_ge(s_exp, QT * (v - 1) + i + 1)
                    nc.vector.tensor_reduce(neg_max[:, i:i + 1], score_bank[i % 2][:, 0:(i + 1) * P], X_AXIS,
                                            ALU.max, negate=True).then_inc(s_max, 1)
                if has[TURNED]:
                    gg, uu, v = unit(TURNED)
                    dve.wait_ge(s_pT_hi, QT * v + i + 1)
                    w = SEQ - i * P
                    nc.vector.tensor_tensor(pT_lo[:, i % 2, 0:w], pT_bank[i % 2][:, 0:w], f(pT_hi[:, i % 2, 0:w]),
                                            ALU.subtract).then_inc(s_pT_lo, 1)
                if i == 0 and has[FINISHED]:
                    gg, uu, v = unit(FINISHED)
                    dve.wait_ge(s_z_hi, v + 1)
                    nc.vector.scalar_tensor_tensor(
                        out=zT_lo[:, uu % GROUP, :], in0=z_bank[:, :],
                        scalar=bias_now[:, uu, 2:3],
                        in1=f(zT_hi[:, uu % GROUP, :]), op0=ALU.add, op1=ALU.subtract).then_inc(s_z_lo, 1)
                if has[SCORED]:
                    gg, uu, v = unit(SCORED)
                    dve.wait_ge(s_exp, QT * v + i + 1)
                    if not first or u >= 3:
                        dve.wait_ge(s_prob, QT * (v - 2) + i + 1)
                    nc.vector.reciprocal(row_inv[:, uu % 2, i:i + 1], row_sum[:, uu % 2, i:i + 1]).then_inc(s_inv, 1)
                if has[0]:
                    for n, kind, j in slot_jobs(u, i):
                        dve.wait_ge(s_proj_hi, NJ * g + n + 1)
                        h = u % GROUP
                        hi, lo = job_target(u, kind, j, qk_hi, v_hi), job_target(u, kind, j, qk_lo, v_lo)
                        if kind == "v":
                            nc.vector.tensor_tensor(lo, proj_bank[n % 2][:, :], f(hi), ALU.subtract).then_inc(s_proj_lo, 1)
                        else:
                            if kind == "q":
                                dve.wait_ge(s_bias, UNITS * g + u + 1)
                            nc.vector.scalar_tensor_tensor(
                                out=lo, in0=proj_bank[n % 2][:, :],
                                scalar=bias_now[:, u, 0:1] if kind == "q" else bias_now[:, u, 1:2],
                                in1=f(hi), op0=ALU.add, op1=ALU.subtract).then_inc(s_proj_lo, 1)
                if u % GROUP == GROUP - 1 and i >= 2 and has[FINISHED]:
                    gg, uu, _ = unit(FINISHED)
                    b, pair = uu // GROUP, i - 2
                    n = 2 * (BATCH * gg + b) + pair
                    dve.wait_ge(s_y, n + 1)
                    rows = X[:, QT * b + 2 * pair:QT * b + 2 * pair + 2, :]
                    if first and n == 0:
                        dve.wait_ge(s_bo, 1)
                    nc.vector.tensor_tensor(rows, y_bank[:, :].rearrange("p (t d) -> p t d", t=2), rows,
                                            ALU.add).then_inc(s_y_added, 1)

        def one(n):
            return scale0[:, 1:2].broadcast_to((P, n))

        def split_qk(pool, g, h, count):
            pool.wait_ge(s_wqk_raw[h], 16 * (g + 1))
            nc.gpsimd.tensor_tensor(wqk_hi[:, h, 0, :, :].rearrange("p c e -> p (c e)"),
                                    wqk_raw[:, h, 0, :, :].rearrange("p c e -> p (c e)"),
                                    one(KC * P), ALU.mult).then_inc(s_wtmp, 1)
            nc.gpsimd.tensor_tensor(k_scaled, wqk_raw[:, h, 1, :, :].rearrange("p c e -> p (c e)"),
                                    scale0[:, 0:1].broadcast_to((P, KC * P)), ALU.mult).then_inc(s_wtmp, 1)
            pool.wait_ge(s_wtmp, count + 2)
            nc.gpsimd.tensor_tensor(wqk_hi[:, h, 1, :, :].rearrange("p c e -> p (c e)"), k_scaled, one(KC * P),
                                    ALU.mult).then_inc(s_wtmp, 1)
            nc.gpsimd.tensor_tensor(wqk_lo[:, h, 0, :, :], wqk_raw[:, h, 0, :, :], f(wqk_hi[:, h, 0, :, :]),
                                    ALU.subtract).then_inc(s_wtmp, 1)
            pool.wait_ge(s_wtmp, count + 4)
            nc.gpsimd.tensor_tensor(wqk_lo[:, h, 1, :, :].rearrange("p c e -> p (c e)"), k_scaled,
                                    f(wqk_hi[:, h, 1, :, :]).rearrange("p c e -> p (c e)"),
                                    ALU.subtract).then_inc(s_wqk, 1)
            pool.wait_ge(s_wqk, GROUP * g + h + 1)

        def split_half(pool, s_raw, s_done, g, half, hi, lo, raw, count):
            pool.wait_ge(s_raw, 16 * (g + 1))
            nc.gpsimd.tensor_tensor(hi, raw, one(GROUP * P), ALU.mult).then_inc(s_wtmp, 1)
            pool.wait_ge(s_wtmp, count + 1)
            nc.gpsimd.tensor_tensor(lo, raw, f(hi), ALU.subtract).then_inc(s_done, 1)

        W_STEPS = GROUP * 4 + 4

        def split_v(pool, g, c, count):
            split_half(pool, s_wv_raw, s_wv, g, c, wv_hi[:, c, :], wv_lo[:, c, :], wv_raw[:, c, :], count)

        def split_o(pool, g, c, count):
            hs = slice(2 * c, 2 * c + 2)
            hi, lo, raw = (w[:, hs, :].rearrange("p h d -> p (h d)") for w in (wo_hi, wo_lo, wo_raw))
            split_half(pool, s_wo_raw, s_wo, g, c, hi, lo, raw, count)

        def normalise(pool, g, u, first=False):
            gg, uu = back(g, u, 1)
            v = UNITS * gg + uu
            for i in range(QT):
                pool.wait_ge(s_inv, QT * v + i + 1)
                p = prob[:, uu % 4, tri(i):tri(i) + (i + 1) * P]
                nc.gpsimd.tensor_tensor(p, p, row_inv[:, uu % 2, i:i + 1].broadcast_to((P, (i + 1) * P)),
                                        ALU.mult).then_inc(s_prob, 1)

        def attn_pool_early(pool, g, first=False):
            base = W_STEPS * g
            if first:
                split_qk(pool, g, 0, base)
                split_qk(pool, g, 1, base + 4)
                split_v(pool, g, 0, base + 8)
                split_v(pool, g, 1, base + 9)
                split_qk(pool, g, 2, base + 10)
                normalise(pool, g, 1, first)
                split_qk(pool, g, 3, base + 14)
                pool.wait_ge(s_xnt, 4)
                nc.gpsimd.tensor_tensor(X[:], X[:], bo_row[:, :].rearrange("p (o d) -> p o d", o=1)
                                        .broadcast_to((P, NT, D)), ALU.add).then_inc(s_bo, 1)
            else:
                normalise(pool, g, 0)
                pool.wait_ge(s_proj, NJ * (g - 1) + job_number(UNITS - 1, "k") + 1)
                split_qk(pool, g, 3, base + 14)
                normalise(pool, g, 1)
            normalise(pool, g, 2, first)
            normalise(pool, g, 3, first)
            normalise(pool, g, 4, first)
            if not first:
                pool.wait_ge(s_y, 4 * g)
            split_o(pool, g, 0, base + 18)
            split_o(pool, g, 1, base + 19)

        def attn_pool_late(pool, g, ahead=True):
            base = W_STEPS * (g + 1)
            for u in range(5, UNITS):
                normalise(pool, g, u)
                if u == 6 and not ahead:
                    mix0_prepare(pool)
                if ahead:
                    h = u - 5
                    pool.wait_ge(s_proj, NJ * g + job_number(GROUP + h, "k") + 1)
                    if u < 7:
                        split_qk(pool, g + 1, h, base + 4 * h)
                    else:
                        pool.wait_ge(s_proj, NJ * g + last_value_job(1) + 1)
                        split_v(pool, g + 1, 0, base + 8)
                        split_v(pool, g + 1, 1, base + 9)
                        split_qk(pool, g + 1, 2, base + 10)

        def attn_loads(sp, g, first=False):
            for h in range(GROUP):
                if not first:
                    sp.wait_ge(s_wqk, GROUP * (g - 1) + h + 1)
                sp.dma_start(wqk_raw[:, h, :, :, :].rearrange("p a c e -> p (a c e)"),
                             a["w_qk"][bass.ds(GROUP * g + h, 1), :, :].rearrange("o p n -> p (o n)")).then_inc(s_wqk_raw[h], 16)
                if h == 1:
                    if not first:
                        sp.wait_ge(s_wv, 2 * g)
                    sp.dma_start(wv_raw.rearrange("p c e -> p (c e)"),
                                 a["w_v"][bass.ds(g, 1), :, :].rearrange("o p n -> p (o n)")).then_inc(s_wv_raw, 16)
            if not first:
                sp.wait_ge(s_wo, 2 * g)
            sp.dma_start(wo_raw.rearrange("p c e -> p (c e)"),
                         a["w_o"][bass.ds(g, 1), :, :].rearrange("o p n -> p (o n)")).then_inc(s_wo_raw, 16)

        ATTN_F = 2048 + 1024 + 1024 + 256 + 4 * TRI
        ATTN_DONE = 4 * GROUPS

        RING = 4
        B0 = layout(farena, FWORDS, skip=(ATTN_F,), router=(KC, E0), down=(KC, 2 * LAT), gate_up=(2, KC, HID),
                    shared_out=(D,), lat_up=(D,), pick=(E0, P), route_bias=(E0,),
                    expert=(RING, 2 * HID + 2 * LAT), e=(NT, E0), p=(NT, E0), b=(NT, E0), left=(NT, E0),
                    chosen=(NT, E0), w=(NT, E0), top=(NT, 8), total=(NT,))
        QK_R, V_R, O_R = 2 * GROUP * 2 * KC * P, 2 * KC * GROUP * P, 2 * GROUP * D
        M0 = layout(rarena, QK_R, expert=(RING, 2 * HID + 2 * LAT), pick=(RING, P), lat_hi=(TOKENS,), lat_lo=(TOKENS,))
        M0 |= layout(rarena, QK_R + V_R, skip=(QK_R,), w_split=(NT, 2 * E0), router_hi=(KC, E0), router_lo=(KC, E0),
                     down_hi=(KC, 2 * LAT), down_lo=(KC, 2 * LAT), gate_up_hi=(2, KC, HID), gate_up_lo=(2, KC, HID))
        M0 |= layout(rarena, RWORDS, skip=(QK_R + V_R + O_R,), wT=(TOKENS,), hid_hi=(RING, SEQ), hid_lo=(RING, SEQ))
        N0 = layout(farena, ATTN_F, shared_hid=(TOKENS,), acc=(TOKENS,), shared_gate=(2, SEQ), shared_prod=(2, SEQ))
        G0 = layout(farena, ATTN_F, skip=(2048 + 1536 + 1024 + 136 + 16 + 512,), gate=(RING, SEQ), prod=(RING, SEQ))
        zeros_bf = sb("zeros_bf", [P, LAT + SEQ], BF16)
        s_m0_raw, s_m0_w, s_m0_tmp = sem("s_m0_raw"), sem("s_m0_w"), sem("s_m0_tmp")
        s_logit0, s_e0, s_route0, s_split0, s_wT_ps, s_wT = (sem(n) for n in (
            "s_logit0", "s_e0", "s_route0", "s_split0", "s_wT_ps", "s_wT"))
        s_gate0, s_value0 = sem("s_gate0"), sem("s_value0")
        s_lat, s_lat_hi, s_lat_lo = (sem(n) for n in ("s_lat", "s_lat_hi", "s_lat_lo"))
        s_ex_raw = [sem(f"s_ex_raw{i}") for i in range(RING)]
        s_square, s_hid_hi, s_hid_lo = sem("s_square"), sem("s_hid_hi"), sem("s_hid_lo")
        s_ex_hi, s_ex_lo, s_pick = (sem(n) for n in ("s_ex_hi", "s_ex_lo", "s_pick"))
        s_front, s_relu, s_prod, s_weighted, s_hid, s_back = (sem(n) for n in (
            "s_front", "s_relu", "s_prod", "s_weighted", "s_hid", "s_back"))
        s_zeros, s_acc, s_out0, s_out0_added = (sem(n) for n in ("s_zeros", "s_acc", "s_out0", "s_out0_added"))
        N_M0 = 8

        def mix0_loads(sp):
            for dst, name in ((B0["router"], "m0_router"), (B0["gate_up"], "m0_gate_up"),
                              (B0["shared_out"], "m0_shared_out"), (B0["down"][:, :, 0:LAT], "m0_down"),
                              (B0["down"][:, :, LAT:2 * LAT], "m0_down"), (B0["lat_up"], "m0_lat_up"),
                              (B0["pick"][0:2 * E0, :, :], "m0_pick")):
                sp.dma_start(dst, a[name]).then_inc(s_m0_raw, 16)
            sp.dma_start(B0["route_bias"], a["m0_bias"].broadcast_to((P, E0))).then_inc(s_m0_raw, 16)

        def expert_loads(sp, e, par, first=False):
            if not first:
                sp.wait_ge(s_ex_lo, 2 * e - 2 * (RING - 1))
            sp.dma_start(B0["expert"][:, par, :],
                         a["m0_expert"][:, bass.ds(e, 1), :].rearrange("l o n -> l (o n)")).then_inc(s_ex_raw[par], 16)

        def mix0_prepare(pool):
            pool.wait_ge(s_m0_raw, 16 * N_M0)
            pool.wait_ge(s_proj, NJ * (GROUPS - 1) + last_value_job(1) + 1)
            k = 0
            for name in ("router", "down", "gate_up"):
                n = {"router": KC * E0, "down": KC * 2 * LAT, "gate_up": 2 * KC * HID}[name]
                flat = "p a b -> p (a b)" if name != "gate_up" else "p a b c -> p (a b c)"
                raw, hi, lo = (v.rearrange(flat) for v in (B0[name], M0[name + "_hi"], M0[name + "_lo"]))
                nc.gpsimd.tensor_tensor(hi, raw, one(n), ALU.mult).then_inc(s_m0_tmp, 1)
                k += 1
                pool.wait_ge(s_m0_tmp, k)
                nc.gpsimd.tensor_tensor(lo, raw, f(hi), ALU.subtract).then_inc(s_m0_w, 1)

        def expert_hi(pool, e, par, first=False):
            pool.wait_ge(s_ex_raw[par], 4 * (e - par) + 16)
            if not first:
                pool.wait_ge(s_front, 2 * e - 2 * (RING - 1))
                pool.wait_ge(s_back, 2 * e - 2 * (RING - 1))
            nc.gpsimd.tensor_tensor(M0["expert"][:, par, :], B0["expert"][:, par, :], one(2 * HID + 2 * LAT),
                                    ALU.mult).then_inc(s_ex_hi, 1)

        def expert_lo(dve, e, par):
            dve.wait_ge(s_ex_hi, e + 1)
            for part in ((slice(LAT, P), slice(0, 2 * HID)), (slice(0, P), slice(2 * HID + LAT, 2 * HID + 2 * LAT))):
                w = M0["expert"][part[0], par, part[1]]
                nc.vector.tensor_tensor(w, B0["expert"][part[0], par, part[1]], f(w), ALU.subtract).then_inc(s_ex_lo, 1)

        def expert_pick(e, par):
            nc.vector.tensor_scalar(M0["pick"][0:2 * E0, par, :],
                                    B0["pick"][0:2 * E0, bass.ds(e, 1), :].rearrange("p o n -> p (o n)"),
                                    1.0, None, ALU.mult).then_inc(s_pick, 1)

        BLOCK = 2 * RING
        BLOCKS = 2 * E0 // BLOCK
        BACK_LAG = 4

        def mix0_blocks(eng, block_of):
            block_of(0, first=True)
            with eng.Fori(1, BLOCKS - 1) as k:
                block_of(k)
            block_of(BLOCKS - 1, last=True)

        def front(pe, n, j, first=False):
            x, par = j % 2, j // 2
            half = slice(x * SEQ, (x + 1) * SEQ)
            for w, out, done, used in ((1, bank[x], s_gate0, s_relu), (0, bank[2 + x], s_value0, s_prod)):
                if not (first and j < 2):
                    pe.wait_ge(used, n + 1)
                lhs = M0["expert"][:, par, w * HID:(w + 1) * HID]
                nc.tensor.matmul(out[:, :], lhs, M0["lat_hi"][:, half], start=True, stop=False)
                nc.tensor.matmul(out[:, :], lhs, M0["lat_lo"][:, half], start=False, stop=True).then_inc(done, 1)
            if not (first and j < 2):
                pe.wait_ge(s_weighted, n - 1)
            nc.tensor.matmul(bank[4 + x][:, :], M0["pick"][0:2 * E0, par, :], M0["wT"][0:2 * E0, half],
                             start=True, stop=True).then_inc(s_front, 1)

        def back_product(pe, n, j, last=False):
            x, par = j % 2, j // 2
            pe.wait_ge(s_hid_lo, n + 1)
            w = M0["expert"][:, par, 2 * HID:2 * HID + 2 * LAT]
            nc.tensor.matmul(bank[6 + x][:, :], w, M0["hid_hi"][:, j % RING, :], start=False, stop=False,
                             skip_group_check=True)
            nc.tensor.matmul(bank[6 + x][0:LAT, :], w[:, 0:LAT], M0["hid_lo"][:, j % RING, :], start=False, stop=last,
                             skip_group_check=True).then_inc(s_back, 1)

        def mix0_logits():
            nc.tensor.wait_ge(s_m0_w, 1)
            nc.tensor.wait_ge(s_proj_lo, NJ * GROUPS)
            for t in range(NT):
                k = 0
                for xs, ws in ((xnT_hi, "router_hi"), (xnT_hi, "router_lo"), (xnT_lo, "router_hi")):
                    for c in range(KC):
                        mm = nc.tensor.matmul(bank[4][:, t * E0:(t + 1) * E0], xs[:, c, t * P:(t + 1) * P],
                                              M0[ws][:, c, :], start=(k == 0), stop=(k == 2 * KC + 1))
                        k += 1
            mm.then_inc(s_logit0, 1)

        def mix0_latent(x):
            if x == 0:
                nc.tensor.wait_ge(s_m0_w, 2)
            else:
                nc.tensor.wait_ge(s_e0, 1)
            half = slice(x * SEQ, (x + 1) * SEQ)
            k = 0
            for ws, xs in (("down_hi", xnT_hi), ("down_hi", xnT_lo), ("down_lo", xnT_hi)):
                for c in range(KC):
                    mm = nc.tensor.matmul(bank[5 - x][:, :], M0[ws][:, c, :], xs[:, c, half],
                                          start=(k == 0), stop=(k == 2 * KC + 1))
                    k += 1
            mm.then_inc(s_lat, 1)

        def mix0_shared(x, w):
            half = slice(x * SEQ, (x + 1) * SEQ)
            nc.tensor.wait_ge(s_m0_w, 3)
            nc.tensor.wait_ge(s_exp, QT * UNITS * GROUPS)
            nc.tensor.wait_ge(s_lat_lo, x + 1)
            out = bank[x] if w else bank[5 - x]
            k = 0
            for ws, xs in (("gate_up_hi", xnT_hi), ("gate_up_hi", xnT_lo), ("gate_up_lo", xnT_hi)):
                for c in range(KC):
                    mm = nc.tensor.matmul(out[:, :], M0[ws][:, w, c, :], xs[:, c, half],
                                          start=(k == 0), stop=(k == 2 * KC + 1))
                    k += 1
            mm.then_inc(s_gate0 if w else s_value0, 1)

        wT_bank = (bank[0], y_bank)

        def mix0_turn_weights():
            nc.tensor.wait_ge(s_split0, 2)
            nc.tensor.wait_ge(s_relu, 1)
            nc.tensor.wait_ge(s_y_added, ATTN_DONE - 2)
            for t in range(NT):
                mm = nc.tensor.transpose(wT_bank[t // 4][0:2 * E0, (t % 4) * P:(t % 4 + 1) * P],
                                         f(M0["w_split"][:, t, :]), ident[:, :])
                if t % 4 == 3:
                    mm.then_inc(s_wT_ps, 1)

        def mix0_tensor(pe):
            def block_of(k, first=False, last=False):
                for j in range(BLOCK):
                    n = BLOCK * k + j
                    if j % 2 == 0:
                        pe.wait_ge(s_pick, RING * k + j // 2 + 1)
                    front(pe, n, j, first)
                    if first and j == 1:
                        attn_tensor_slot(pe, GROUPS, 3, tail=True, steps=(1, 2, 3))
                    if first and j == 2:
                        pe.wait_ge(s_y_added, ATTN_DONE)
                        pe.wait_ge(s_zeros, 1)
                        for x in range(2):
                            nc.tensor.matmul(bank[6 + x][:, :], zeros_bf[:, 0:P], zeros_bf[:, 0:SEQ],
                                             start=True, stop=False, skip_group_check=True)
                    if j >= BACK_LAG:
                        back_product(pe, n - BACK_LAG, j - BACK_LAG)
                    elif not first:
                        back_product(pe, n - BACK_LAG, j - BACK_LAG + BLOCK)

            def shared_out(r):
                nc.tensor.matmul(bank[r][:, :], zeros_bf[:, 0:P], zeros_bf[:, 0:SEQ], start=True, stop=False,
                                 skip_group_check=True)
                for t in (2 * r, 2 * r + 1):
                    nc.tensor.matmul(bank[r][:, (t % 2) * D:(t % 2 + 1) * D], N0["shared_hid"][:, t * P:(t + 1) * P],
                                     B0["shared_out"], start=False, stop=False, skip_group_check=True)

            pe.wait_ge(s_wT, 2)
            pe.wait_ge(s_pT_lo, QT * UNITS * GROUPS)
            pe.wait_ge(s_prod, 2)
            mix0_blocks(pe, block_of)
            last = 2 * E0 - 1
            pe.wait_ge(s_weighted, last)
            back_product(pe, last - 3, BLOCK - 4)
            shared_out(0)
            back_product(pe, last - 2, BLOCK - 3)
            shared_out(2)
            back_product(pe, last - 1, BLOCK - 2, last=True)
            pe.wait_ge(s_weighted, last + 1)
            shared_out(1)
            shared_out(3)
            back_product(pe, last, BLOCK - 1, last=True)
            for t in range(NT):
                if t % 4 == 0:
                    pe.wait_ge(s_acc, t // 4 + 1)
                mm = nc.tensor.matmul(bank[t // 2][:, (t % 2) * D:(t % 2 + 1) * D], N0["acc"][:, t * P:(t + 1) * P],
                                      B0["lat_up"], start=False, stop=True, skip_group_check=True)
                if t % 2:
                    mm.then_inc(s_out0, 1)

        def mix0_sigmoid():
            nc.scalar.wait_ge(s_logit0, 1)
            nc.scalar.activation(B0["e"].rearrange("p t e -> p (t e)"), bank[4][:, 0:NT * E0], ACT.Exp,
                                 scale=-1.0).then_inc(s_e0, 1)

        def mix0_latent_hi(x):
            nc.scalar.wait_ge(s_lat, x + 1)
            nc.scalar.activation(M0["lat_hi"][:, x * SEQ:(x + 1) * SEQ], bank[5 - x][:, :],
                                 ACT.Identity).then_inc(s_lat_hi, 1)

        def mix0_shared_relu(x):
            nc.scalar.wait_ge(s_gate0, x + 1)
            nc.scalar.activation(N0["shared_gate"][:, x, :], bank[x][:, :], ACT.Relu).then_inc(s_relu, 1)

        def mix0_weights_out():
            for x in range(2):
                nc.scalar.wait_ge(s_wT_ps, x + 1)
                nc.scalar.activation(M0["wT"][0:2 * E0, x * SEQ:(x + 1) * SEQ], wT_bank[x][0:2 * E0, :],
                                     ACT.Identity).then_inc(s_wT, 1)

        def mix0_scalar(act):
            def block_of(k, first=False, last=False):
                for j in range(BLOCK):
                    n = BLOCK * k + j
                    gate = G0["gate"][:, j % RING, :]
                    act.wait_ge(s_gate0, n + 3)
                    if not (first and j < RING):
                        act.wait_ge(s_prod, n - 1)
                    nc.scalar.activation(gate, bank[j % 2][:, :], ACT.Relu).then_inc(s_relu, 1)
                    if not (first and j < 2):
                        hidden_hi(n - 2, (j - 2) % RING, first and j < 2 + RING)
                    act.wait_ge(s_relu, n + 3)
                    nc.scalar.activation(gate, gate, ACT.Square).then_inc(s_square, 1)

            def hidden_hi(n, ring, first=False):
                act.wait_ge(s_weighted, n + 1)
                if not first:
                    act.wait_ge(s_back, n - 3)
                nc.scalar.activation(M0["hid_hi"][:, ring, :], G0["prod"][:, ring, :], ACT.Identity).then_inc(s_hid_hi, 1)

            mix0_blocks(act, block_of)
            hidden_hi(2 * E0 - 2, RING - 2)
            hidden_hi(2 * E0 - 1, RING - 1)
            for x in range(2):
                act.wait_ge(s_back, 2 * E0 - 1 + x)
                nc.scalar.activation(N0["acc"][:, x * SEQ:(x + 1) * SEQ], bank[6 + x][:, :],
                                     ACT.Identity).then_inc(s_acc, 1)

        route0_steps = [0]

        def route0(dve, ins):
            route0_steps[0] += 1
            ins.then_inc(s_route0, 1)
            dve.wait_ge(s_route0, route0_steps[0])

        def mix0_choose(dve):
            e, p, b, left, top = (B0[n] for n in ("e", "p", "b", "left", "top"))
            dve.wait_ge(s_m0_raw, 16 * N_M0)
            dve.wait_ge(s_e0, 1)
            route0(dve, nc.vector.tensor_scalar(e, e, 1.0, None, ALU.add))
            route0(dve, nc.vector.reciprocal(p, e))
            route0(dve, nc.vector.tensor_tensor(b, p, B0["route_bias"].rearrange("p (o e) -> p o e", o=1)
                                                .broadcast_to((P, NT, E0)), ALU.add))
            for t in range(NT):
                nc.vector.max(top[:, t, :], b[:, t, :]).then_inc(s_route0, 1)
            route0_steps[0] += NT
            dve.wait_ge(s_route0, route0_steps[0])
            for t in range(NT):
                nc.vector.match_replace(left[:, t, :], top[:, t, :], b[:, t, :], -3.0e38).then_inc(s_route0, 1)
            route0_steps[0] += NT

        def mix0_route(dve):
            p, b, left, chosen, w, total = (B0[n] for n in ("p", "b", "left", "chosen", "w", "total"))
            dve.wait_ge(s_route0, route0_steps[0])
            route0(dve, nc.vector.tensor_tensor(chosen, left, b, ALU.not_equal))
            route0(dve, nc.vector.tensor_tensor(chosen, chosen, p, ALU.mult))
            route0(dve, nc.vector.tensor_reduce(total, chosen, X_AXIS, ALU.add))
            route0(dve, nc.vector.reciprocal(total, total))
            route0(dve, nc.vector.tensor_scalar(total, total, ROUTE_SCALE, None, ALU.mult))
            route0(dve, nc.vector.tensor_tensor(w, chosen, total.rearrange("p (t o) -> p t o", o=1)
                                                .broadcast_to((P, NT, E0)), ALU.mult))
            nc.vector.tensor_copy(M0["w_split"][:, :, 0:E0], w).then_inc(s_split0, 1)
            dve.wait_ge(s_split0, 1)
            nc.vector.tensor_tensor(M0["w_split"][:, :, E0:2 * E0], w, f(M0["w_split"][:, :, 0:E0]),
                                    ALU.subtract).then_inc(s_split0, 1)

        def mix0_latent_lo(x):
            nc.vector.wait_ge(s_lat_hi, x + 1)
            half = slice(x * SEQ, (x + 1) * SEQ)
            nc.vector.tensor_tensor(M0["lat_lo"][:, half], bank[5 - x][:, :], f(M0["lat_hi"][:, half]),
                                    ALU.subtract).then_inc(s_lat_lo, 1)

        def mix0_shared_prod(x):
            nc.vector.wait_ge(s_relu, x + 1)
            nc.vector.wait_ge(s_value0, x + 1)
            nc.vector.tensor_tensor(N0["shared_prod"][:, x, :], bank[5 - x][:, :], N0["shared_gate"][:, x, :],
                                    ALU.mult).then_inc(s_prod, 1)

        def mix0_vector(dve):
            def block_of(k, first=False, last=False):
                for j in range(BLOCK):
                    n = BLOCK * k + j
                    dve.wait_ge(s_square, n + 1)
                    dve.wait_ge(s_value0, n + 3)
                    if not (first and j < RING):
                        dve.wait_ge(s_hid_lo, n - 3)
                    nc.vector.tensor_tensor(G0["prod"][:, j % RING, :], bank[2 + j % 2][:, :], G0["gate"][:, j % RING, :],
                                            ALU.mult).then_inc(s_prod, 1)
                    dve.wait_ge(s_front, n + 1)
                    dve.wait_ge(s_prod, n + 3)
                    nc.vector.tensor_tensor(G0["prod"][:, j % RING, :], bank[4 + j % 2][:, :], G0["prod"][:, j % RING, :],
                                            ALU.mult).then_inc(s_weighted, 1)
                    if not (last and j >= BLOCK - 4):
                        ahead = RING * k + j // 2 + 2
                        par = (j // 2 + 2) % RING
                        if j % 2:
                            expert_lo(dve, ahead, par)
                            expert_pick(ahead, par)
                    if first and j == 1:
                        attn_vector_slot(dve, GROUPS, 3, tail=True, steps=(1, 2, 3))

            mix0_blocks(dve, block_of)

        def mix0_pool(pool):
            nc.gpsimd.memset(zeros_bf[:, :], 0.0).then_inc(s_zeros, 1)
            pool.wait_ge(s_proj, NJ * GROUPS)
            for e in range(2):
                expert_hi(pool, e, e, first=True)
            for x in range(2):
                pool.wait_ge(s_prod, x + 1)
                nc.gpsimd.tensor_tensor(N0["shared_hid"][:, x * SEQ:(x + 1) * SEQ], N0["shared_prod"][:, x, :],
                                        N0["shared_gate"][:, x, :], ALU.mult).then_inc(s_hid, 1)

            def block_of(k, first=False, last=False):
                for j in range(BLOCK):
                    n = BLOCK * k + j
                    if j % 2 == 0 and not (last and j >= BLOCK - 4):
                        expert_hi(pool, RING * k + j // 2 + 2, (j // 2 + 2) % RING, first=first and j < 4)
                    pool.wait_ge(s_hid_hi, n + 1)
                    nc.gpsimd.tensor_tensor(M0["hid_lo"][:, j % RING, :], G0["prod"][:, j % RING, :],
                                            f(M0["hid_hi"][:, j % RING, :]), ALU.subtract).then_inc(s_hid_lo, 1)

            mix0_blocks(pool, block_of)

        M0_END = QK_R + V_R
        STEPS = BATCH * KC
        TILES = HM * QT
        L1a = layout(farena, FWORDS, rope=(4, SEQ), w_raw=(3, KC, D), cos=(SEQ,), sin=(SEQ,), blocks=(HM, DH1 + 1),
                     gate=(HEADS1,), w_out=(KC, D), rot=(2, KC, SEQ), low=(KC, SEQ), k_feat=(KC, SEQ),
                     memory=(STEPS, HM, DH1 + 1), q_feat=(STEPS, SEQ), k_rows=(NT, D),
                     values=(STEPS, QT, HM, DH1 + 1), attended=(STEPS, QT, HM, DH1 + 1))
        L1b = layout(farena, FWORDS, prob=(4, SEQ), head_values=(HM, QT, VW), z=(SEQ,), skip=(1024 + 136 + 16 + 512,),
                     pT=(2, QT, SEQ))
        s_inv_att = sem("s_inv_att")
        L1c = layout(farena, FWORDS, skip=(2048 + 1536 + 1024 + 136 + 16 + 512,), mixed=(KC, TOKENS), out=(4, D),
                     inv=(2, HEADS1))
        pick_raw = layout(farena, FWORDS, skip=(FWORDS - 4 * 4 * P - 584,), pick=(4, 4, P))["pick"]
        R1 = layout(rarena, RWORDS, skip=(M0_END,), w_hi=(3, KC, D), w_lo=(3, KC, D), qk_hi=(2, STEPS, SEQ), qk_lo=(2, STEPS, SEQ),
                    pick=(4, 4, P), pairs=(2, 4, SEQ))
        names = ("s_l1_raw s_l1_out_raw s_l1_tmp s_l1_w s_pick1 s_ones s_proj1 s_rope s_rot s_hi1 s_neg1 s_exp1 s_lo1_even s_lo1_odd s_feat "
                 "s_kT s_k_rows s_v1 s_values s_mem_ps s_mem s_sel_q s_sel_k s_pair_q s_pair_k s_hv s_score1 s_max1 "
                 "s_prob1 s_pT1 s_pT_even s_pT_odd s_pv1 s_z1 s_zT1 s_att s_gates s_memout s_inv1 s_mix_a s_mix_b "
                 "s_mix s_mixT s_mixT_sb s_wo1 s_att_added").split()
        (s_l1_raw, s_l1_out_raw, s_l1_tmp, s_l1_w, s_pick1, s_ones, s_proj1, s_rope, s_rot, s_hi1, s_neg1, s_exp1, s_lo1_even, s_lo1_odd, s_feat,
         s_kT, s_k_rows, s_v1, s_values, s_mem_ps, s_mem, s_sel_q, s_sel_k, s_pair_q, s_pair_k, s_hv, s_score1, s_max1,
         s_prob1, s_pT1, s_pT_even, s_pT_odd, s_pv1, s_z1, s_zT1, s_att, s_gates, s_memout, s_inv1, s_mix_a, s_mix_b,
         s_mix, s_mixT, s_mixT_sb, s_wo1, s_att_added) = (sem(n) for n in names)
        neg_max1 = small[:, 112:116]
        N_L1 = 5
        C = DH1 + 1

        def l1_loads(sp):
            sp.wait_ge(s_hid, 2)
            sp.wait_ge(s_pT, QT * UNITS * GROUPS)
            for dst, name in ((L1a["w_raw"], "l1_w"), (L1a["cos"], "l1_cos"), (L1a["sin"], "l1_sin"),
                              (L1a["blocks"], "l1_blocks")):
                sp.dma_start(dst, a[name]).then_inc(s_l1_raw, 16)
            sp.dma_start(L1a["gate"], a["l1_gate"].broadcast_to((P, HEADS1))).then_inc(s_l1_raw, 16)
            sp.dma_start(L1a["w_out"], a["l1_w_out"]).then_inc(s_l1_out_raw, 16)

        def l1_pick_load(sp):
            sp.wait_ge(s_out0_added, 4)
            sp.wait_ge(s_xnt, 8)
            sp.dma_start(pick_raw, a["l1_pick"]).then_inc(s_l1_out_raw, 16)

        CHUNKS = 2 * BATCH * KC
        rope_pair = [L1a["rope"][:, 0:2, :], L1a["rope"][:, 2:4, :],
                     L1a["w_raw"].rearrange("p w c d -> p (w c d)")[:, 0:2 * SEQ].rearrange("p (k t) -> p k t", k=2)]
        rot = L1a["rot"].rearrange("p a c t -> p (a c) t")

        def l1_pool_project(pool):
            pool.wait_ge(s_l1_raw, 16 * N_L1)
            pool.wait_ge(s_y_added, ATTN_DONE)
            for w in range(3):
                flat = "p c d -> p (c d)"
                raw, hi, lo = (v[:, w, :, :].rearrange(flat) for v in (L1a["w_raw"], R1["w_hi"], R1["w_lo"]))
                nc.gpsimd.tensor_tensor(hi, raw, one(KC * D), ALU.mult).then_inc(s_l1_tmp, 1)
                pool.wait_ge(s_l1_tmp, w + 1)
                nc.gpsimd.tensor_tensor(lo, raw, f(hi), ALU.subtract).then_inc(s_l1_w, 1)
            pool.wait_ge(s_out0_added, 4)
            nc.gpsimd.memset(L1a["values"].rearrange("p s k h c -> p (s k h) c")[:, :, DH1:C], 1.0).then_inc(s_ones, 1)
            for c in range(CHUNKS + 1):
                if c < CHUNKS:
                    pool.wait_ge(s_rope, 2 * (c + 1))
                    if c >= 4:
                        pool.wait_ge(s_feat, c - 3)
                    t = rope_pair[c % 3]
                    nc.gpsimd.tensor_tensor(rot[:, c % 4, :], t[:, 0, :], t[:, 1, :],
                                            ALU.add if c % 2 else ALU.subtract).then_inc(s_rot, 1)
                if c == CHUNKS - 1:
                    pool.wait_ge(s_l1_out_raw, 32)
                    gathering(0)
                    pool.wait_ge(s_rot, CHUNKS)
                    nc.gpsimd.memset(L1b["head_values"], 0.0).then_inc(s_ones, 1)
                if c % 2:
                    rotated_lo(pool, nc.gpsimd, c - 1, s_lo1_even)
            for pr in range(1, 4):
                gathering(pr)
            pool.wait_ge(s_pick1, 4)

        def gathering(pr):
            nc.gpsimd.tensor_tensor(R1["pick"][:, pr, :, :].rearrange("p b c -> p (b c)"),
                                    pick_raw[:, pr, :, :].rearrange("p b c -> p (b c)"), one(4 * P),
                                    ALU.mult).then_inc(s_pick1, 1)

        def rotated_lo(eng, ops, c, done):
            b, w, m = c // 4, c // 2 % 2, c % 2
            eng.wait_ge(s_hi1, c + 1)
            ops.tensor_tensor(R1["qk_lo"][:, w, KC * b + m, :], rot[:, c % 4, :],
                              f(R1["qk_hi"][:, w, KC * b + m, :]), ALU.subtract).then_inc(done, 1)

        keys_bank = (bank[0:2], (bank[5], bank[7]))

        def l1_turn_keys(pe, b):
            pe.wait_ge(s_feat, 4 * b + 4)
            if b:
                pe.wait_ge(s_k_rows, 2)
            for tt in range(QT):
                for m in range(KC):
                    mm = nc.tensor.transpose(keys_bank[b][tt // 2][:, ((tt % 2) * KC + m) * P:((tt % 2) * KC + m + 1) * P],
                                             L1a["k_feat"][:, m, tt * P:(tt + 1) * P], ident[:, :])
                if tt % 2:
                    mm.then_inc(s_kT, 1)

        def l1_memory(pe, b):
            pe.wait_ge(s_values, QT * (b + 1))
            pe.wait_ge(s_k_rows, 2 * b + 2)
            if b:
                pe.wait_ge(s_values, NT)
            for m in range(KC):
                st = KC * b + m
                for kt in range(QT):
                    mm = nc.tensor.matmul(bank[4 + st][:, 0:HM * C], L1a["k_rows"][:, QT * b + kt, m * P:(m + 1) * P],
                                          L1a["values"][:, st, kt, :, :].rearrange("p h c -> p (h c)"),
                                          start=(kt == 0), stop=(kt == QT - 1))
                mm.then_inc(s_mem_ps, 1)

        def l1_tensor_project(pe):
            def three(out, left, right, k0=True):
                terms = [(l, r) for l, r in ((left[0], right[0]), (left[0], right[1]), (left[1], right[0]))]
                k = 0
                for l, r in terms:
                    for c in range(KC):
                        mm = nc.tensor.matmul(out, l(c), r(c), start=(k == 0), stop=(k == 2 * KC + 1))
                        k += 1
                return mm

            def project(j):
                b, w = j // 2, j % 2
                half = slice(b * SEQ, (b + 1) * SEQ)
                pe.wait_ge(s_xnl, 6 + 2 * b)
                if j < 2:
                    pe.wait_ge(s_l1_w, j + 1)
                else:
                    pe.wait_ge(s_rope, 4 * (j - 1))
                for m in range(KC):
                    mm = three(bank[4 + 2 * (j % 2) + m][:, :],
                               [lambda c, v=v, m=m: v[:, w, c, m * P:(m + 1) * P] for v in (R1["w_hi"], R1["w_lo"])],
                               [lambda c, v=v: v[:, c, half] for v in (xnT_hi, xnT_lo)])
                mm.then_inc(s_proj1, 1)

            def project_values(j):
                pe.wait_ge(s_xnl, min(8, 7 + j))
                if j == 0:
                    pe.wait_ge(s_l1_w, 3)
                if j >= 2:
                    pe.wait_ge(s_values, 2 * (j - 1))
                for t in (2 * j, 2 * j + 1):
                    mm = three(bank[2 + j % 2][:, (t % 2) * D:(t % 2 + 1) * D],
                               [lambda c, v=v: v[:, c, t * P:(t + 1) * P] for v in (xnT_hi, xnT_lo)],
                               [lambda c, v=v: v[:, 2, c, :] for v in (R1["w_hi"], R1["w_lo"])])
                mm.then_inc(s_v1, 1)

            project(0)
            norm_tensor(pe, 1, 1)
            project(1)
            project_values(0)
            project(2)
            project_values(1)
            project(3)
            project_values(2)
            l1_turn_keys(pe, 0)
            project_values(3)
            pe.wait_ge(s_ones, 1)
            pe.wait_ge(s_rope, 2 * CHUNKS - 4)
            l1_memory(pe, 0)
            pe.wait_ge(s_lo1_even, CHUNKS // 4)
            pe.wait_ge(s_lo1_odd, CHUNKS // 4)
            pe.wait_ge(s_pick1, 1)
            pe.wait_ge(s_rope, 2 * CHUNKS)
            pe.wait_ge(s_mem, KC)

        def l1_copy_keys(act, b):
            for r in range(2):
                act.wait_ge(s_kT, 2 * b + r + 1)
                nc.scalar.activation(L1a["k_rows"][:, QT * b + 2 * r:QT * b + 2 * r + 2, :],
                                     keys_bank[b][r][:, :].rearrange("p (t d) -> p t d", t=2),
                                     ACT.Identity).then_inc(s_k_rows, 1)

        def l1_scalar_project(act):
            def copy_values(j):
                act.wait_ge(s_v1, j + 1)
                for t in (2 * j, 2 * j + 1):
                    b, kt = t // QT, t % QT
                    nc.scalar.activation(L1a["values"][:, KC * b:KC * (b + 1), kt, :, 0:DH1],
                                         bank[2 + j % 2][:, (t % 2) * D:(t % 2 + 1) * D]
                                         .rearrange("p (m h d) -> p m h d", m=KC, h=HM), ACT.Identity).then_inc(s_values, 1)

            for c in range(CHUNKS):
                b, w, m = c // 4, c // 2 % 2, c % 2
                act.wait_ge(s_rot, c + 1)
                if c >= 2:
                    act.wait_ge(s_feat, c - 1)
                nc.scalar.activation(L1a["low"][:, m, :], rot[:, c % 4, :], ACT.Relu, scale=-1.0).then_inc(s_neg1, 1)
                nc.scalar.activation(R1["qk_hi"][:, w, KC * b + m, :], rot[:, c % 4, :], ACT.Identity).then_inc(s_hi1, 1)
                act.wait_ge(s_neg1, c + 1)
                nc.scalar.activation(L1a["low"][:, m, :], L1a["low"][:, m, :], ACT.Exp, scale=-1.0).then_inc(s_exp1, 1)
                if c == 2:
                    act.wait_ge(s_ones, 1)
                if c in (2, 4, 6, 7):
                    copy_values((c - 1) // 2)
                if c == 5:
                    l1_copy_keys(act, 0)

        def l1_vector_project(dve):
            dve.wait_ge(s_l1_raw, 16 * N_L1)
            for c in range(CHUNKS + 2):
                if c < CHUNKS:
                    j, m = c // 2, c % 2
                    dve.wait_ge(s_proj1, j + 1)
                    if c >= 3:
                        dve.wait_ge(s_rot, c - 2)
                    q0, q1 = bank[4 + 2 * (j % 2)][:, :], bank[4 + 2 * (j % 2) + 1][:, :]
                    products = ((q1, "cos"), (q0, "sin")) if m else ((q0, "cos"), (q1, "sin"))
                    if c == 2:
                        dve.wait_ge(s_l1_w, 3)
                    for k, (x, y) in enumerate(products):
                        nc.vector.tensor_tensor(rope_pair[c % 3][:, k, :], x, L1a[y], ALU.mult).then_inc(s_rope, 1)
                if c == 1:
                    norm_lo(dve, 1, 1)
                if c == CHUNKS + 1:
                    l1_mask_memory(dve, 0)
                if c >= 2:
                    d = c - 2
                    b, w, m = d // 4, d // 2 % 2, d % 2
                    if m:
                        rotated_lo(dve, nc.vector, d, s_lo1_odd)
                    dve.wait_ge(s_exp1, d + 1)
                    if d == 6:
                        dve.wait_ge(s_kT, 2)
                    out = L1a["k_feat"][:, m, :] if w else L1a["q_feat"][:, KC * b + m, :]
                    nc.vector.scalar_tensor_tensor(out=out, in0=rot[:, d % 4, :], scalar=0.0, in1=L1a["low"][:, m, :],
                                                   op0=ALU.max, op1=ALU.add).then_inc(s_feat, 1)

        def l1_mask_memory(dve, b):
            for st in range(KC * b, KC * (b + 1)):
                dve.wait_ge(s_mem_ps, st + 1)
                nc.vector.tensor_tensor(L1a["memory"][:, st, :, :].rearrange("p h c -> p (h c)"), bank[4 + st][:, 0:HM * C],
                                        L1a["blocks"].rearrange("p h c -> p (h c)"), ALU.mult).then_inc(s_mem, 1)

        LAG_S, LAG_T, LAG_V = 6, 9, 14
        TURNS_LAST = 21
        TAIL1 = 24
        score1_bank, turn1_bank, side_bank, z1_bank = bank[0:3], (bank[3], bank[5], bank[7]), bank[4], bank[6]

        def in_bank_before(t):
            return 2 if t < 2 else 5 if t == 2 else 3

        def behind(s, n, lag, first, tail):
            if (first and n < lag) or (tail and lag <= n):
                return None
            return (s, n - lag) if n >= lag else (s - 1, n - lag + TILES)

        def turned(s, n, first, tail, delay=0):
            if first or n - delay not in (5, 21):
                return None
            return s - 1, (n - delay) // 16

        def pair_rows(pe, s, pr, w):
            if w == 0:
                pe.wait_ge(s_pair_k, 4 * s + pr)
                if pr % 2 and not (isinstance(s, int) and s == 0):
                    pe.wait_ge(s_att, 2 * s - (1 if pr == 1 else 0))
            else:
                pe.wait_ge(s_pair_q, 4 * s + pr + 1)
            nc.tensor.matmul(side_bank[:, :], R1["pick"][:, pr, 2 * w, :], R1["qk_hi"][:, w, bass.ds(s, 1), :]
                             .rearrange("p o t -> p (o t)"), start=True, stop=False)
            nc.tensor.matmul(side_bank[:, :], R1["pick"][:, pr, 2 * w + 1, :], R1["qk_lo"][:, w, bass.ds(s, 1), :]
                             .rearrange("p o t -> p (o t)"), start=False, stop=True).then_inc(s_sel_k if w else s_sel_q, 1)

        def l1_tensor_slot(pe, s, n, first=False, tail=False):
            at = behind(s, n, LAG_T, first, tail)
            if at:
                ss, t = at
                pe.wait_ge(s_prob1, TILES * ss + t + 1)
                if not (first and t < 3):
                    old = t - in_bank_before(t)
                    pe.wait_ge(s_pT_odd if old % 2 else s_pT_even, TILES // 2 * ss + old // 2 + 1)
                for kt in range(QT):
                    mm = nc.tensor.transpose(turn1_bank[t % 3][:, kt * P:(kt + 1) * P],
                                             L1b["prob"][:, t % 4, kt * P:(kt + 1) * P], ident[:, :])
                mm.then_inc(s_pT1, 1)
            at = behind(s, n, LAG_S, first, tail)
            if at:
                ss, t = at
                h, i = t // QT, t % QT
                if t % 8 == 0:
                    pe.wait_ge(s_pair_k, 4 * ss + t // 8 + 1)
                if not (first and t < 3):
                    pe.wait_ge(s_prob1, TILES * ss + t - in_bank_before(t) + 1)
                rows = slice(64 * (h % 2), 64 * (h % 2) + 64)
                nc.tensor.matmul(score1_bank[t % 3][:, :], R1["pairs"][rows, 0, h // 2, i * P:(i + 1) * P],
                                 R1["pairs"][rows, 1, h // 2, :], start=True, stop=True).then_inc(s_score1, 1)
            at = behind(s, n, LAG_V, first, tail)
            if at:
                ss, t = at
                h, kt = t // QT, t % QT
                if kt == 0:
                    pe.wait_ge(s_pT_even, TILES // 2 * ss + 2 * h + 2)
                    pe.wait_ge(s_pT_odd, TILES // 2 * ss + 2 * h + 2)
                    pe.wait_ge(s_hv, HM * ss + h + 1)
                    if h % 2 == 0 and not (first and h < 4):
                        pe.wait_ge(s_z1, 4 * ss + h // 2 - 1)
                g = h % 4
                nc.tensor.matmul(z1_bank[g * VW:(g + 1) * VW, :], L1b["head_values"][:, h, kt, :],
                                 L1b["pT"][:, h % 2, kt, :], start=(kt == 0), stop=(kt == QT - 1)).then_inc(s_pv1, 1)
            if n % 8 in (0, 3) and not tail:
                pair_rows(pe, s, n // 8, n % 8 // 3)
            at = turned(s, n, first, tail)
            if at:
                ss, g = at
                pe.wait_ge(s_z1, 4 * ss + 2 * g + 2)
                pe.wait_ge(s_pair_k, 4 * ss + (4 if tail else 5 + 2 * g))
                for i in range(QT):
                    mm = nc.tensor.transpose(side_bank[:, i * P:(i + 1) * P], L1b["z"][:, i * P:(i + 1) * P], ident[:, :])
                mm.then_inc(s_zT1, 1)

        def l1_scalar_slot(act, s, n, first=False, tail=False):
            if n % 8 in (1, 4) and not tail:
                pr, w = n // 8, n % 8 // 4
                act.wait_ge(s_sel_k if w else s_sel_q, 4 * s + pr + 1)
                if not first:
                    act.wait_ge(s_score1, TILES * (s - 1) + 8 * (pr + 1))
                nc.scalar.activation(R1["pairs"][:, w, pr, :], side_bank[:, :],
                                     ACT.Identity).then_inc(s_pair_k if w else s_pair_q, 1)
            at = behind(s, n, LAG_T, first, tail)
            if at and at[1] % 2:
                ss, t = at
                turned_out(act, nc.scalar, ss, t, first)
            at = behind(s, n, LAG_S, first, tail)
            if at:
                ss, t = at
                act.wait_ge(s_max1, TILES * ss + t + 1)
                if not (first and t < 4):
                    act.wait_ge(s_pT1, TILES * ss + t - 3)
                nc.scalar.activation(L1b["prob"][:, t % 4, :], score1_bank[t % 3][:, :], ACT.Exp,
                                     bias=neg_max1[:, t % 4:t % 4 + 1]).then_inc(s_prob1, 1)
            at = behind(s, n, LAG_V, first, tail)
            if at and at[1] % 8 == 7:
                ss, t = at
                act.wait_ge(s_pv1, TILES * ss + t + 1)
                if not (first and t < 16):
                    act.wait_ge(s_zT1, 2 * ss + t // 16)
                half = slice(64 * (t // 8 % 2), 64 * (t // 8 % 2) + 64)
                nc.scalar.activation(L1b["z"][half, :], z1_bank[half, :], ACT.Identity).then_inc(s_z1, 1)

        def turned_out(eng, ops, ss, t, first):
            h, i = t // QT, t % QT
            eng.wait_ge(s_pT1, TILES * ss + t + 1)
            if not first or h >= 2:
                eng.wait_ge(s_pv1, TILES * ss + QT * (h - 1))
            out = L1b["pT"][:, h % 2, :, i * P:(i + 1) * P]
            src = turn1_bank[t % 3][:, :].rearrange("p (k q) -> p k q", k=QT)
            if ops is nc.scalar:
                ops.activation(out, src, ACT.Identity).then_inc(s_pT_odd, 1)
            else:
                ops.tensor_copy(out, src).then_inc(s_pT_even, 1)

        def l1_vector_slot(dve, s, n, first=False, tail=False):
            at = turned(s, n, first, tail, delay=1)
            if at:
                ss, g = at
                dve.wait_ge(s_zT1, 2 * ss + g + 1)
                for i in range(QT):
                    ins = nc.vector.tensor_scalar(
                        L1a["attended"][:, bass.ds(ss, 1), i, 4 * g:4 * g + 4, :].rearrange("p o h c -> p (o h) c"),
                        side_bank[:, i * P:(i + 1) * P].rearrange("p (h c) -> p h c", h=4)[:, :, 0:C],
                        1.0, None, ALU.mult)
                ins.then_inc(s_att, 1)
            at = behind(s, n, LAG_S, first, tail)
            if at:
                ss, t = at
                dve.wait_ge(s_score1, TILES * ss + t + 1)
                if not (first and t < 4):
                    dve.wait_ge(s_prob1, TILES * ss + t - 3)
                nc.vector.tensor_reduce(neg_max1[:, t % 4:t % 4 + 1], score1_bank[t % 3][:, :], X_AXIS, ALU.max,
                                        negate=True).then_inc(s_max1, 1)
            at = behind(s, n, LAG_T, first, tail)
            if at and at[1] % 2 == 0:
                ss, t = at
                turned_out(dve, nc.vector, ss, t, first)
            if n % QT == 2 and not tail:
                h = n // QT
                if not first:
                    dve.wait_ge(s_pv1, TILES * (s - 1) + QT * (h + 1))
                nc.vector.tensor_scalar(L1b["head_values"][:, h, :, 0:C],
                                        L1a["values"][:, bass.ds(s, 1), :, h, :].rearrange("p o k c -> p (o k) c"),
                                        1.0, None, ALU.mult).then_inc(s_hv, 1)

        def l1_run(eng, slot, early, between=None):
            for n in range(TILES):
                if n in early:
                    early[n]()
                slot(eng, 0, n, first=True)
            with eng.Fori(1, STEPS) as s:
                for n in range(TILES):
                    slot(eng, s, n)
            for n in range(TAIL1):
                if between and n == TURNS_LAST:
                    between()
                slot(eng, STEPS, n, tail=True)

        def early_tensor(pe):
            def pick_ready(pr):
                return lambda: pe.wait_ge(s_pick1, pr + 1)

            def before_turning():
                pe.wait_ge(s_mem, STEPS)
                pe.wait_ge(s_lo1_even, CHUNKS // 2)
                pe.wait_ge(s_lo1_odd, CHUNKS // 2)

            return {3: lambda: l1_turn_keys(pe, 1), 7: lambda: l1_memory(pe, 1), 8: pick_ready(1), 9: before_turning,
                    16: pick_ready(2), 24: pick_ready(3)}

        def early_scalar(act):
            def keys_and_gate():
                l1_copy_keys(act, 1)
                nc.scalar.activation(L1a["gate"], L1a["gate"], ACT.Exp, scale=-1.0).then_inc(s_gates, 1)

            return {4: keys_and_gate}

        def early_vector(dve):
            def memory_and_gates():
                l1_mask_memory(dve, 1)
                dve.wait_ge(s_kT, 4)
                dve.wait_ge(s_pick1, 4)
                mix_gates(dve)
                mix1_fill(dve)

            return {8: memory_and_gates}

        def mix_memory(pe, t):
            b, i = t // QT, t % QT
            if t >= 2:
                pe.wait_ge(s_mix_a, t - 1)
            for m in range(KC):
                mm = nc.tensor.matmul(bank[2 + t % 2][:, m * HM * C:(m + 1) * HM * C],
                                      L1a["q_feat"][:, KC * b + m, i * P:(i + 1) * P],
                                      L1a["memory"][:, KC * b + m, :, :].rearrange("p h c -> p (h c)"),
                                      start=True, stop=True)
            mm.then_inc(s_memout, 1)

        def mix_turn(pe, r):
            pe.wait_ge(s_mix, 2 * r + 2)
            if r:
                pe.wait_ge(s_mixT_sb, r)
            for c in range(KC):
                for t in range(2):
                    mm = nc.tensor.transpose(bank[4][:, (2 * c + t) * P:(2 * c + t + 1) * P],
                                             L1c["out"][:, (2 * r + t) % 4, c * P:(c + 1) * P], ident[:, :])
            mm.then_inc(s_mixT, 1)

        def mix_output(pe, r):
            pe.wait_ge(s_mixT_sb, r + 1)
            if r >= 2:
                pe.wait_ge(s_att_added, r - 1)
            for t in (2 * r, 2 * r + 1):
                for c in range(KC):
                    mm = nc.tensor.matmul(bank[6 + r % 2][:, (t % 2) * D:(t % 2 + 1) * D],
                                          L1c["mixed"][:, c, t * P:(t + 1) * P], L1a["w_out"][:, c, :],
                                          start=(c == 0), stop=(c == KC - 1))
            mm.then_inc(s_wo1, 1)

        def mix_turned_out(act, r):
            act.wait_ge(s_mixT, r + 1)
            nc.scalar.activation(L1c["mixed"][:, :, 2 * P * r:2 * P * (r + 1)],
                                 bank[4][:, :].rearrange("p (c t) -> p c t", c=KC), ACT.Identity).then_inc(s_mixT_sb, 1)

        mix_steps = [0]

        def mix_step(dve, ins):
            mix_steps[0] += 1
            ins.then_inc(s_inv1, 1)
            dve.wait_ge(s_inv1, mix_steps[0])

        def mix_gates(dve):
            gate, gates = L1a["gate"], L1d["gates"]
            dve.wait_ge(s_gates, 1)
            mix_step(dve, nc.vector.tensor_scalar(gate, gate, 1.0, None, ALU.add))
            mix_step(dve, nc.vector.reciprocal(gates[:, 0, :], gate))
            mix_step(dve, nc.vector.tensor_scalar(gates[:, 1, :], gates[:, 0, :], -1.0, 1.0, ALU.mult, ALU.add))

        def mix_attended_factors(dve):
            inv = L1d["inv_att"]
            dve.wait_ge(s_pv1, STEPS * TILES)
            dve.wait_ge(s_att, 2 * STEPS)
            mix_step(dve, nc.vector.reciprocal(inv, L1a["attended"][:, :, :, :, DH1]))
            for m in range(KC):
                nc.vector.tensor_tensor(inv[:, m::KC, :, :], inv[:, m::KC, :, :],
                                        L1d["gates"][:, 1, HM * m:HM * (m + 1)].rearrange("p (a b h) -> p a b h", a=1, b=1)
                                        .broadcast_to((P, BATCH, QT, HM)), ALU.mult).then_inc(s_inv_att, 1)

        def mix_pool(pool):
            pool.wait_ge(s_inv_att, KC)
            for st in range(STEPS):
                att = L1a["attended"][:, st, :, :, 0:DH1]
                nc.gpsimd.tensor_tensor(att, att, L1d["inv_att"][:, st, :, :].rearrange("p i (h o) -> p i h o", o=1)
                                        .broadcast_to((P, QT, HM, DH1)), ALU.mult).then_inc(s_mix_b, 1)

        def mix_add(dve, t):
            b, i = t // QT, t % QT
            dve.wait_ge(s_mix_a, t + 1)
            dve.wait_ge(s_mix_b, KC * (b + 1))
            out = L1c["out"][:, t % 4, :].rearrange("p (m h d) -> p m h d", m=KC, h=HM)
            nc.vector.tensor_tensor(out, out, L1a["attended"][:, KC * b:KC * (b + 1), i, :, 0:DH1],
                                    ALU.add).then_inc(s_mix, 1)

        def mix_tiles(dve, tiles):
            for t in tiles:
                mem = bank[2 + t % 2][:, 0:HEADS1 * C].rearrange("p (m h c) -> p m h c", m=KC, h=HM)
                inv = L1c["inv"][:, t % 2, :]
                dve.wait_ge(s_memout, t + 1)
                nc.vector.reciprocal(inv.rearrange("p (m h) -> p m h", m=KC), mem[:, :, :, DH1]).then_inc(s_inv1, 1)
                mix_steps[0] += 1
                if t != tiles[0]:
                    mix_add(dve, t - 1)
                dve.wait_ge(s_inv1, mix_steps[0])
                mix_step(dve, nc.vector.tensor_tensor(inv, inv, L1d["gates"][:, 0, :], ALU.mult))
                if t >= 4:
                    dve.wait_ge(s_mixT, t // 2 - 1)
                out = L1c["out"][:, t % 4, :].rearrange("p (m h d) -> p m h d", m=KC, h=HM)
                nc.vector.tensor_tensor(out, mem[:, :, :, 0:DH1], inv.rearrange("p (m h o) -> p m h o", m=KC, o=1)
                                        .broadcast_to((P, KC, HM, DH1)), ALU.mult).then_inc(s_mix_a, 1)
            mix_add(dve, tiles[-1])

        def mix_added(dve, r):
            dve.wait_ge(s_wo1, r + 1)
            rows = X[:, 2 * r:2 * r + 2, :]
            nc.vector.tensor_tensor(rows, bank[6 + r % 2][:, :].rearrange("p (t d) -> p t d", t=2), rows,
                                    ALU.add).then_inc(s_att_added, 1)

        B1 = layout(farena, FWORDS, skip=(2048 + 1536,), chunk=(3, KC * P), router=(KC, E1))
        L1d = layout(farena, FWORDS, skip=(2048 + 1536 + 1024 + 136 + 16 + 512 + 2048 + 1024 + 1024 + 544 + 2048,),
                     pick=(FC, P), logit=(NT, 16), found=(NT, 8), wanted=(NT, 8), left=(NT, 16), w=(NT, E1), total=(NT,),
                     gates=(2, HEADS1), inv_att=(STEPS, QT, HM))
        D1 = layout(farena, FWORDS, silu=(2, SEQ), prod=(2, SEQ), hid=(2, SEQ))
        M1 = layout(rarena, M0_END, chunk_hi=(3, KC * P), chunk_lo=(3, KC * P), router_hi=(KC, E1),
                    router_lo=(KC, E1), pick=(P,), w_split=(NT, 2 * E1), wT=(TOKENS,), hid_hi=(2, SEQ), hid_lo=(2, SEQ))
        (s_m1_raw, s_m1_tmp, s_m1_router, s_logit1, s_lg, s_route1, s_ex1, s_exd1, s_split1, s_wT1_ps, s_wT1, s_pick2, s_gate1,
         s_up1, s_silu1, s_prod1, s_hid1, s_hid1_hi, s_hid1_lo, s_back1) = (sem(n) for n in (
             "s_m1_raw s_m1_tmp s_m1_router s_logit1 s_lg s_route1 s_ex1 s_exd1 s_split1 s_wT1_ps s_wT1 s_pick2 s_gate1 "
             "s_up1 s_silu1 s_prod1 s_hid1 s_hid1_hi s_hid1_lo s_back1").split())
        s_chunk_raw = [sem(f"s_chunk_raw{k}") for k in range(3)]
        s_chunk = [sem(f"s_chunk{k}") for k in range(3)]
        s_y1 = [sem(f"s_y1_{r}") for r in range(4)]
        GATE, UP, DOWN = range(3)
        ABSENT, TAKEN = -3.0e38, -3.2e38

        def chunk_load(sp, k, c, first=False):
            if not first:
                sp.wait_ge(s_chunk[k], c)
            sp.dma_start(B1["chunk"][:, k, :], a["m1_chunk"][:, bass.ds(c, 1), k, :]
                         .rearrange("p o n -> p (o n)")).then_inc(s_chunk_raw[k], 16)

        def mix1_loads(sp):
            sp.wait_ge(s_rope, 2 * CHUNKS)
            sp.wait_ge(s_mem_ps, STEPS)
            sp.dma_start(B1["router"], a["m1_router"]).then_inc(s_m1_raw, 16)
            sp.dma_start(L1d["pick"][0:2 * E1, :, :], a["m1_pick"]).then_inc(s_m1_raw, 16)
            for k in range(3):
                chunk_load(sp, k, 0, first=True)
            with sp.Fori(1, FC) as c:
                for k in range(3):
                    chunk_load(sp, k, c)

        def split_chunk(pool, k, c, used, first=False):
            pool.wait_ge(s_chunk_raw[k], 16 * (c + 1))
            if not first:
                pool.wait_ge(used, 2 * c)
            nc.gpsimd.tensor_tensor(M1["chunk_hi"][:, k, :], B1["chunk"][:, k, :], one(KC * P),
                                    ALU.mult).then_inc(s_m1_tmp, 1)
            pool.wait_ge(s_m1_tmp, 3 * c + k + 1)
            nc.gpsimd.tensor_tensor(M1["chunk_lo"][:, k, :], B1["chunk"][:, k, :], f(M1["chunk_hi"][:, k, :]),
                                    ALU.subtract).then_inc(s_chunk[k], 1)

        def mix1_prepare(pool):
            pool.wait_ge(s_m1_raw, 32)
            flat = "p c e -> p (c e)"
            nc.gpsimd.tensor_tensor(M1["router_hi"].rearrange(flat), B1["router"].rearrange(flat), one(KC * E1),
                                    ALU.mult).then_inc(s_m1_router, 1)
            pool.wait_ge(s_m1_router, 1)
            nc.gpsimd.tensor_tensor(M1["router_lo"].rearrange(flat), B1["router"].rearrange(flat),
                                    f(M1["router_hi"].rearrange(flat)), ALU.subtract).then_inc(s_m1_router, 1)
            for k in range(3):
                split_chunk(pool, k, 0, None, first=True)

        def mix1_pool(pool):
            def hid_lo(n, x, first=False):
                pool.wait_ge(s_hid1_hi, n + 1)
                if not first:
                    pool.wait_ge(s_back1, n - 1)
                nc.gpsimd.tensor_tensor(M1["hid_lo"][:, x, :], D1["hid"][:, x, :], f(M1["hid_hi"][:, x, :]),
                                        ALU.subtract).then_inc(s_hid1_lo, 1)

            def chunk(c, first=False, last=False):
                hid_lo(2 * c, 0, first)
                if not last:
                    split_chunk(pool, GATE, c + 1, s_gate1)
                    split_chunk(pool, UP, c + 1, s_up1)
                hid_lo(2 * c + 1, 1, first)
                if not last:
                    split_chunk(pool, DOWN, c + 1, s_back1)

            chunk(0, first=True)
            with pool.Fori(1, FC - 1) as c:
                chunk(c)
            chunk(FC - 1, last=True)

        def mix1_logits(pe, tiles):
            pe.wait_ge(s_m1_router, 2)
            for t in tiles:
                k = 0
                for xs, ws in ((xnT_hi, "router_hi"), (xnT_hi, "router_lo"), (xnT_lo, "router_hi")):
                    for c in range(KC):
                        mm = nc.tensor.matmul(bank[5][:, t * E1:(t + 1) * E1], xs[:, c, t * P:(t + 1) * P],
                                              M1[ws][:, c, :], start=(k == 0), stop=(k == 2 * KC + 1))
                        k += 1
            mm.then_inc(s_logit1, 1)

        def terms(left, right):
            return ((left[0], right[0]), (left[0], right[1]), (left[1], right[0]))

        def projection(out, k, x):
            half = slice(x * SEQ, (x + 1) * SEQ)
            m = 0
            for w, v in terms((M1["chunk_hi"], M1["chunk_lo"]), (xnT_hi, xnT_lo)):
                for c in range(KC):
                    mm = nc.tensor.matmul(out, w[:, k, c * P:(c + 1) * P], v[:, c, half], start=(m == 0),
                                          stop=(m == 2 * KC + 1))
                    m += 1
            return mm

        def gate_step(n, x, c, first=False):
            if x == 0:
                nc.tensor.wait_ge(s_chunk[GATE], c + 1)
            if not first:
                nc.tensor.wait_ge(s_silu1, n - 1)
            projection(bank[3 if x else 0][:, :], GATE, x).then_inc(s_gate1, 1)

        def up_step(n, x, c, first=False):
            if x == 0:
                nc.tensor.wait_ge(s_chunk[UP], c + 1)
            if not (first and x == 0):
                nc.tensor.wait_ge(s_prod1, n)
            projection(bank[1][:, :], UP, x).then_inc(s_up1, 1)

        def gate_up(n, x, c, first=False):
            gate_step(n, x, c, first)
            up_step(n, x, c, first)

        def weights(n, x, c, first=False):
            nc.tensor.wait_ge(s_pick2, c + 1)
            if not (first and x == 0):
                nc.tensor.wait_ge(s_hid1, n)
            nc.tensor.matmul(bank[2][:, :], M1["pick"][0:2 * E1, :], M1["wT"][0:2 * E1, x * SEQ:(x + 1) * SEQ],
                             start=True, stop=True).then_inc(s_ex1, 1)

        def mix1_turn_weights(pe):
            pe.wait_ge(s_split1, 2)
            pe.wait_ge(s_mix_a, NT)
            for t in range(NT):
                mm = nc.tensor.transpose(bank[2 if t < 4 else 3][0:2 * E1, (t % 4) * P:(t % 4 + 1) * P],
                                         f(M1["w_split"][:, t, :]), ident[:, :])
                if t % 4 == 3:
                    mm.then_inc(s_wT1_ps, 1)

        def mix1_tensor(pe):
            def back(n, x, c, last=False):
                pe.wait_ge(s_hid1_lo, n + 1)
                if x == 0:
                    pe.wait_ge(s_chunk[DOWN], c + 1)
                for i in range(QT):
                    r = 2 * x + i // 2
                    out = bank[4 + r][:, (i % 2) * D:(i % 2 + 1) * D]
                    for m, (h, w) in enumerate(terms((M1["hid_hi"], M1["hid_lo"]), (M1["chunk_hi"], M1["chunk_lo"]))):
                        mm = nc.tensor.matmul(out, h[:, x, i * P:(i + 1) * P], w[:, DOWN, :], start=False,
                                              stop=last and m == 2, skip_group_check=True)
                mm.then_inc(s_back1, 1)

            pe.wait_ge(s_att_added, 4)
            for r in range(4):
                nc.tensor.matmul(bank[4 + r][:, :], zeros_bf[:, 0:P], zeros_bf[:, 0:SEQ], start=True, stop=False,
                                 skip_group_check=True)
            pe.wait_ge(s_wT1, 2)
            weights(0, 0, 0, first=True)
            gate_up(1, 1, 0, first=True)
            weights(1, 1, 0, first=True)
            back(0, 0, 0)
            with pe.Fori(1, FC) as c:
                gate_up(2 * c, 0, c)
                weights(2 * c, 0, c)
                back(2 * c - 1, 1, c - 1)
                gate_up(2 * c + 1, 1, c)
                weights(2 * c + 1, 1, c)
                back(2 * c, 0, c)
            back(2 * FC - 1, 1, FC - 1)

        def silu(act, n, x, first=False):
            act.wait_ge(s_gate1, n + 1)
            if not first:
                act.wait_ge(s_prod1, n - 1)
            nc.scalar.activation(D1["silu"][:, x, :], bank[3 if x else 0][:, :], ACT.Silu).then_inc(s_silu1, 1)

        def mix1_exp(act):
            act.wait_ge(s_exd1, 1)
            nc.scalar.activation(L1d["w"], L1d["w"], ACT.Exp).then_inc(s_exd1, 1)

        def mix1_weights_out(act):
            for x in range(2):
                act.wait_ge(s_wT1_ps, x + 1)
                nc.scalar.activation(M1["wT"][0:2 * E1, x * SEQ:(x + 1) * SEQ], bank[2 + x][0:2 * E1, :],
                                     ACT.Identity).then_inc(s_wT1, 1)

        def mix1_scalar(act):
            def hid_hi(n, x, first=False):
                act.wait_ge(s_hid1, n + 1)
                if not first:
                    act.wait_ge(s_back1, n - 1)
                nc.scalar.activation(M1["hid_hi"][:, x, :], D1["hid"][:, x, :], ACT.Identity).then_inc(s_hid1_hi, 1)

            silu(act, 1, 1, first=True)
            hid_hi(0, 0, first=True)
            hid_hi(1, 1, first=True)
            with act.Fori(1, FC) as c:
                for x in range(2):
                    silu(act, 2 * c + x, x)
                    hid_hi(2 * c + x, x)

        route1_steps = [0]

        def route1(dve, *instructions):
            for ins in instructions:
                ins.then_inc(s_route1, 1)
            route1_steps[0] += len(instructions)
            dve.wait_ge(s_route1, route1_steps[0])

        def mix1_fill(dve):
            route1(dve, nc.vector.memset(L1d["logit"][:, :, E1:16], ABSENT), nc.vector.memset(L1d["wanted"], ABSENT))

        def mix1_choose(dve):
            logit, found, wanted, left, w = (L1d[n] for n in ("logit", "found", "wanted", "left", "w"))
            dve.wait_ge(s_logit1, 2)
            nc.vector.tensor_copy(logit[:, :, 0:E1], bank[5][:, 0:NT * E1].rearrange("p (t e) -> p t e", t=NT)).then_inc(s_lg, 1)
            dve.wait_ge(s_lg, 1)
            route1(dve, *[nc.vector.max(found[:, t, :], logit[:, t, 0:E1]) for t in range(NT)])
            nc.vector.tensor_tensor(w, logit[:, :, 0:E1], found[:, :, 0:1].broadcast_to((P, NT, E1)),
                                    ALU.subtract).then_inc(s_exd1, 1)
            route1(dve, nc.vector.tensor_copy(wanted[:, :, 0:2], found[:, :, 0:2]))
            route1(dve, *[nc.vector.match_replace(left[:, t, 0:14], wanted[:, t, :], logit[:, t, 0:14], TAKEN)
                          for t in range(NT)])

        def mix1_route(dve):
            logit, left, w, total = (L1d[n] for n in ("logit", "left", "w", "total"))
            route1(dve, nc.vector.tensor_tensor(left[:, :, 0:E1], left[:, :, 0:E1], logit[:, :, 0:E1], ALU.not_equal))
            dve.wait_ge(s_exd1, 2)
            route1(dve, nc.vector.tensor_tensor(w, w, left[:, :, 0:E1], ALU.mult))
            route1(dve, nc.vector.tensor_reduce(total, w, X_AXIS, ALU.add))
            route1(dve, nc.vector.reciprocal(total, total))
            route1(dve, nc.vector.tensor_tensor(w, w, total.rearrange("p (t o) -> p t o", o=1)
                                                .broadcast_to((P, NT, E1)), ALU.mult))
            nc.vector.tensor_copy(M1["w_split"][:, :, 0:E1], w).then_inc(s_split1, 1)
            dve.wait_ge(s_split1, 1)
            nc.vector.tensor_tensor(M1["w_split"][:, :, E1:2 * E1], w, f(M1["w_split"][:, :, 0:E1]),
                                    ALU.subtract).then_inc(s_split1, 1)

        def mix1_vector(dve):
            def pick(c):
                nc.vector.tensor_scalar(M1["pick"][0:2 * E1, :],
                                        L1d["pick"][0:2 * E1, bass.ds(c, 1), :].rearrange("p o n -> p (o n)"),
                                        1.0, None, ALU.mult).then_inc(s_pick2, 1)

            def hidden(n, x, first=False):
                dve.wait_ge(s_silu1, n + 1)
                dve.wait_ge(s_up1, n + 1)
                if not first:
                    dve.wait_ge(s_hid1, n - 1)
                nc.vector.tensor_tensor(D1["prod"][:, x, :], bank[1][:, :], D1["silu"][:, x, :], ALU.mult).then_inc(s_prod1, 1)
                dve.wait_ge(s_ex1, n + 1)
                dve.wait_ge(s_prod1, n + 1)
                if not first:
                    dve.wait_ge(s_hid1_lo, n - 1)
                nc.vector.tensor_tensor(D1["hid"][:, x, :], bank[2][:, :], D1["prod"][:, x, :], ALU.mult).then_inc(s_hid1, 1)

            dve.wait_ge(s_m1_raw, 32)
            pick(0)
            hidden(0, 0, first=True)
            hidden(1, 1, first=True)
            with dve.Fori(1, FC) as c:
                pick(c)
                hidden(2 * c, 0)
                hidden(2 * c + 1, 1)
            for r in range(4):
                dve.wait_ge(s_back1, 2 * FC - 1 + r // 2)
                rows = X[:, 2 * r:2 * r + 2, :]
                nc.vector.tensor_tensor(rows, bank[4 + r][:, :].rearrange("p (t d) -> p t d", t=2), rows,
                                        ALU.add).then_inc(s_y1[r], 1)

        consts = [(ident, "ident"), (mask_neg, "mask_neg"), (ident_bf, "ident_bf"), (bias_qkv, "bias_qkv"),
                  (scale0, "scale0")]
        N_CONST = len(consts) + 1
        s_out = sem("s_out")

        block = ctx.enter_context(nc.Block())

        @block.sync
        def _(sp):
            for b in range(BATCH):
                sp.dma_start(X[:, QT * b:QT * (b + 1), :], a["x"][:, QT * b:QT * (b + 1), :]).then_inc(s_x[b], 16)
            for dst, name in consts:
                sp.dma_start(dst[:], a[name]).then_inc(s_const, 16)
            sp.dma_start(bo_row[:], a["b_o"].broadcast_to((P, D))).then_inc(s_const, 16)
            attn_loads(sp, 0, first=True)
            with sp.Fori(1, GROUPS) as g:
                attn_loads(sp, g)
            mix0_loads(sp)
            for e in range(RING):
                expert_loads(sp, e, e, first=True)
            l1_loads(sp)
            with sp.Fori(1, E0 // RING) as k:
                for par in range(RING):
                    expert_loads(sp, RING * k + par, par)
            l1_pick_load(sp)
            mix1_loads(sp)
            for r in range(4):
                sp.wait_ge(s_y1[r], 1)
                sp.dma_start(a["out"][:, 2 * r:2 * r + 2, :], X[:, 2 * r:2 * r + 2, :]).then_inc(s_out, 16)
            sp.wait_ge(s_out, 64)

        @block.tensor
        def _(pe):
            norm_tensor(pe, 0, 0)
            norm_tensor(pe, 0, 1)
            pe.wait_ge(s_xnl, 4)
            for u in range(UNITS):
                attn_tensor_slot(pe, 0, u, first=True)
            with pe.Fori(1, GROUPS) as g:
                for u in range(UNITS):
                    attn_tensor_slot(pe, g, u)
            mix0_logits()
            mix0_latent(0)
            attn_tensor_slot(pe, GROUPS, 0, tail=True)
            mix0_latent(1)
            for x in range(2):
                attn_tensor_slot(pe, GROUPS, 1 + x, tail=True, steps=(0,))
                mix0_shared(x, 1)
                attn_tensor_slot(pe, GROUPS, 1 + x, tail=True, steps=(1,))
                mix0_shared(x, 0)
                attn_tensor_slot(pe, GROUPS, 1 + x, tail=True, steps=(2,))
                if x == 1:
                    mix0_turn_weights()
                attn_tensor_slot(pe, GROUPS, 1 + x, tail=True, steps=(3,))
            attn_tensor_slot(pe, GROUPS, 3, tail=True, steps=(0,))
            mix0_tensor(pe)
            norm_tensor(pe, 1, 0)
            l1_tensor_project(pe)
            l1_run(pe, l1_tensor_slot, early_tensor(pe), between=lambda: mix1_logits(pe, range(0, QT)))
            mix_memory(pe, 0)
            mix_memory(pe, 1)
            mix1_logits(pe, range(QT, NT))
            mix_memory(pe, 2)
            mix_memory(pe, 3)
            gate_step(0, 0, 0, first=True)
            mix_turn(pe, 0)
            mix_memory(pe, 4)
            mix_memory(pe, 5)
            up_step(0, 0, 0, first=True)
            mix_turn(pe, 1)
            mix_output(pe, 0)
            mix_memory(pe, 6)
            mix_memory(pe, 7)
            mix_turn(pe, 2)
            mix_output(pe, 1)
            mix_turn(pe, 3)
            mix1_turn_weights(pe)
            mix_output(pe, 2)
            mix_output(pe, 3)
            mix1_tensor(pe)

        @block.scalar
        def _(act):
            norm_scalar(act, 0)
            norm_hi(act, 0, 0)
            norm_hi(act, 0, 1)
            act.wait_ge(s_bk, 1)
            for u in range(UNITS):
                attn_scalar_slot(act, 0, u, first=True)
            with act.Fori(1, GROUPS) as g:
                for u in range(UNITS):
                    attn_scalar_slot(act, g, u)
            mix0_sigmoid()
            mix0_latent_hi(0)
            attn_scalar_slot(act, GROUPS, 0, tail=True)
            mix0_latent_hi(1)
            for x in range(2):
                attn_scalar_slot(act, GROUPS, 1 + x, tail=True, steps=(0, 1))
                mix0_shared_relu(x)
                attn_scalar_slot(act, GROUPS, 1 + x, tail=True, steps=(2,))
                if x == 1:
                    mix0_weights_out()
                attn_scalar_slot(act, GROUPS, 1 + x, tail=True, steps=(3,))
            attn_scalar_slot(act, GROUPS, 3, tail=True)
            mix0_scalar(act)
            norm_scalar(act, 1)
            norm_hi(act, 1, 0)
            norm_hi(act, 1, 1)
            l1_scalar_project(act)
            act.wait_ge(s_ones, 2)
            act.wait_ge(s_lo1_even, CHUNKS // 2)
            l1_run(act, l1_scalar_slot, early_scalar(act))
            silu(act, 0, 0, first=True)
            mix_turned_out(act, 0)
            mix_turned_out(act, 1)
            mix1_exp(act)
            mix_turned_out(act, 2)
            mix_turned_out(act, 3)
            mix1_weights_out(act)
            mix1_scalar(act)

        @block.vector
        def _(dve):
            norm_vector(dve, 0)
            norm_lo(dve, 0, 1)
            dve.wait_ge(s_const, 16 * N_CONST)
            nc.vector.tensor_scalar(bias_qkv[:, 1, :], bias_qkv[:, 1, :], scale0[:, 0:1], None, ALU.mult).then_inc(s_bk, 1)
            dve.wait_ge(s_bk, 1)
            nc.vector.tensor_copy(bias_now[:, 0, :], bias_qkv[:, :, 0]).then_inc(s_bias, 1)
            for u in range(UNITS):
                attn_vector_slot(dve, 0, u, first=True)
            with dve.Fori(1, GROUPS) as g:
                for u in range(UNITS):
                    attn_vector_slot(dve, g, u)
            mix0_choose(dve)
            mix0_latent_lo(0)
            attn_vector_slot(dve, GROUPS, 0, tail=True)
            mix0_latent_lo(1)
            attn_vector_slot(dve, GROUPS, 1, tail=True, steps=(0, 1))
            mix0_route(dve)
            attn_vector_slot(dve, GROUPS, 1, tail=True, steps=(2, 3))
            attn_vector_slot(dve, GROUPS, 2, tail=True, steps=(0,))
            mix0_shared_prod(0)
            attn_vector_slot(dve, GROUPS, 2, tail=True, steps=(1,))
            for e in range(2):
                expert_lo(dve, e, e)
                expert_pick(e, e)
            attn_vector_slot(dve, GROUPS, 2, tail=True, steps=(2, 3))
            mix0_shared_prod(1)
            attn_vector_slot(dve, GROUPS, 3, tail=True, steps=(0,))
            mix0_vector(dve)
            norm_vector(dve, 1)
            l1_vector_project(dve)
            dve.wait_ge(s_ones, 2)
            dve.wait_ge(s_lo1_even, CHUNKS // 2)
            l1_run(dve, l1_vector_slot, early_vector(dve))
            mix_attended_factors(dve)
            mix_tiles(dve, range(0, QT))
            mix1_choose(dve)
            mix_tiles(dve, range(QT, NT))
            mix1_route(dve)
            for r in range(NT // 2):
                mix_added(dve, r)
            mix1_vector(dve)

        @block.gpsimd
        def _(pool):
            pool.wait_ge(s_const, 16 * N_CONST)
            attn_pool_early(pool, 0, first=True)
            with pool.Fori(0, GROUPS - 1) as g:
                attn_pool_late(pool, g)
                attn_pool_early(pool, g + 1)
            attn_pool_late(pool, GROUPS - 1, ahead=False)
            normalise(pool, GROUPS, 0)
            mix0_pool(pool)
            l1_pool_project(pool)
            mix1_prepare(pool)
            mix_pool(pool)
            mix1_pool(pool)


def kernel(**inputs):
    import numpy as np
    import concourse.bacc as bacc
    from concourse.bass_utils import run_bass_kernel_spmd

    def get(name):
        return np.asarray(inputs[name])

    bf16 = mybir.dt.np(BF16)
    wq, wk = get("L0_attn_W_Q"), get("L0_attn_W_K")
    wqk = np.stack([wq, wk], 1).reshape(HEADS0, 2, KC, P, DH0).transpose(0, 3, 1, 2, 4)
    wv = get("L0_attn_W_V").reshape(GROUPS, GROUP, KC, P, DH0).transpose(0, 3, 2, 1, 4)
    wo = get("L0_attn_W_O").reshape(GROUPS, GROUP, DH0, D).transpose(0, 2, 1, 3)
    bias = np.stack([get("L0_attn_b_Q"), get("L0_attn_b_K"), get("L0_attn_b_V")]).transpose(2, 0, 1)
    arrays = {
        "x": get("L0_attn_x").reshape(NT, P, D).transpose(1, 0, 2),
        "w_qk": wqk.reshape(HEADS0, P, 2 * KC * DH0),
        "w_v": wv.reshape(GROUPS, P, KC * GROUP * DH0),
        "w_o": wo.reshape(GROUPS, P, GROUP * D),
        "bias_qkv": bias,
        "b_o": get("L0_attn_b_O").reshape(1, D),
        "ident": np.eye(P, dtype=np.float32),
        "ident_bf": np.eye(P, dtype=np.float32).astype(bf16),
        "mask_neg": np.triu(np.full((P, P), MASKED, np.float32), 1).astype(bf16),
        "scale0": np.tile(np.array([[DH0 ** -0.5, 1.0]], np.float32), (P, 1)),
    }
    arrays |= {
        "m0_router": get("L0_ffn_Wg").T.reshape(KC, P, E0).transpose(1, 0, 2),
        "m0_down": get("L0_ffn_Wdown").T.reshape(KC, P, LAT).transpose(1, 0, 2),
        "m0_gate_up": np.stack([get("L0_ffn_sw1"), get("L0_ffn_swg")]).transpose(0, 2, 1)
        .reshape(2, KC, P, HID).transpose(2, 0, 1, 3),
        "m0_shared_out": get("L0_ffn_sw2").T,
        "m0_lat_up": np.tile(get("L0_ffn_Wup").T, (2, 1)),
        "m0_pick": np.tile(np.repeat(np.eye(E0, dtype=np.float32)[:, :, None], P, 2), (2, 1, 1)),
        "m0_bias": get("L0_ffn_biases").reshape(1, E0),
        "m0_expert": np.concatenate([
            np.tile(np.stack([get("L0_ffn_rw1"), get("L0_ffn_rwg")], 1).transpose(3, 0, 1, 2).reshape(LAT, E0, 2 * HID), (2, 1, 1)),
            np.tile(get("L0_ffn_rw2").transpose(2, 0, 1), (1, 1, 2))], -1),
    }
    def rows(w):
        return w.reshape(KC, P, -1).transpose(1, 0, 2)

    freq = (np.float32(1.0) / np.float32(10000.0) ** (np.arange(0, D, 2, dtype=np.float32) / np.float32(D))).astype(np.float32)
    angle = (np.arange(SEQ, dtype=np.float32)[:, None] * freq[None, :]).astype(np.float32).T
    pick = np.zeros((P, 4, 4, P), np.float32)
    for pr in range(4):
        for kind, parts in enumerate(((0, 1), (2, 3), (0, 2), (1, 3))):
            for j in range(2):
                for part in parts:
                    for d in range(DH1):
                        pick[DH1 * (2 * pr + j) + d, pr, kind, 64 * j + DH1 * part + d] = DH1 ** -0.5 if kind < 2 else 1.0
    arrays |= {
        "l1_w": np.stack([rows(get(n).T) for n in ("L1_attn_Wq", "L1_attn_Wk", "L1_attn_Wv")], 1),
        "l1_cos": np.cos(angle),
        "l1_sin": np.sin(angle),
        "l1_blocks": np.repeat(np.repeat(np.eye(HM, dtype=np.float32), DH1, 0)[:, :, None], DH1 + 1, 2),
        "l1_gate": get("L1_attn_gate").reshape(1, HEADS1),
        "l1_w_out": rows(get("L1_attn_Wo").T),
        "l1_pick": pick,
    }
    expert_of = np.repeat(np.eye(E1, dtype=np.float32), F1, 1).reshape(E1, FC, P)
    gate = get("L1_ffn_gate_proj").reshape(FC, P, KC, P).transpose(3, 0, 2, 1)
    up = get("L1_ffn_up_proj").reshape(FC, P, KC, P).transpose(3, 0, 2, 1)
    down = get("L1_ffn_down_proj").transpose(0, 2, 1).reshape(FC, P, D).transpose(1, 0, 2)
    arrays |= {
        "m1_router": rows(get("L1_ffn_gate_w").T),
        "m1_pick": np.tile(expert_of, (2, 1, 1)),
        "m1_chunk": np.stack([gate.reshape(P, FC, KC * P), up.reshape(P, FC, KC * P), down], 2),
    }
    nc = bacc.Bacc("TRN2", target_bir_lowering=False, num_devices=1)
    aps, feed = {}, {}
    for name, v in arrays.items():
        v = np.ascontiguousarray(v)
        feed[f"in_{name}"] = v
        aps[name] = nc.dram_tensor(f"in_{name}", v.shape, mybir.dt.from_np(v.dtype), kind="ExternalInput").ap()
    aps["out"] = nc.dram_tensor("out_x", (P, NT, D), F32, kind="ExternalOutput").ap()
    program(nc, aps)
    r = run_bass_kernel_spmd(nc, [feed], core_ids=[0])
    got = np.asarray(r.results[0]["out_x"])
    return np.ascontiguousarray(got.transpose(1, 0, 2).reshape(BATCH, SEQ, D))
```
